# Optimizing a Trainium2 kernel written in Bass

```python
import numpy as np
import jax
import jax.numpy as jnp

def _softmax(x, axis=-1):
    return jax.nn.softmax(x, axis=axis)

def _gelu(x):
    return jax.nn.gelu(x, approximate=True)

def _silu(x):
    return jax.nn.silu(x)

def _sigmoid(x):
    return jax.nn.sigmoid(x)

def _layernorm(x, axis=-1, eps=1e-05):
    m = jnp.mean(x, axis=axis, keepdims=True)
    v = jnp.var(x, axis=axis, keepdims=True)
    return (x - m) / jnp.sqrt(v + eps)

def _scatter_add(tgt, idx, src, axis=0):
    return tgt.at[idx].add(src)

def _segment_sum(src, seg, n):
    return jax.ops.segment_sum(src, seg, n)
kernel_name = 'mk_adj_ffn_d2_adj_r2_b71f40'

def setup_inputs(seed: int=0):
    np.random.seed(seed)
    _w = jnp.asarray

    def _rec_inputs():
        import jax
        import jax.numpy as jnp
        _gk = jax.random.key(seed)
        x = 7.22e-05 + 1 * jax.random.normal(jax.random.fold_in(_gk, 1), (32, 256, 128), jnp.float32)
        _a = jax.random.bernoulli(jax.random.fold_in(_gk, 2), 0.0078125, (32, 256, 256))
        _a = jnp.logical_or(_a, jnp.swapaxes(_a, -1, -2))
        _a = jnp.logical_or(_a, jnp.eye(256, dtype=bool))
        _af = _a.astype(jnp.float32)
        adj = _af
        return (x, adj)
    x, adj = _rec_inputs()

    def _L0_gnn_setup():
        import jax, jax.numpy as jnp
        import numpy as np
        from jax import lax
        DIM = 128
        EPS = 1e-05

        def _bn(h, g, b, m, v):
            scale = g / jnp.sqrt(v + EPS)
            return h * scale[None, :, None] + (b - m * scale)[None, :, None]

        def _conv1d(h, w, pad):
            return lax.conv_general_dilated(h, w, window_strides=(1,), padding=[(pad, pad)], dimension_numbers=('NCH', 'OIH', 'NCH'))
        key = jax.random.key(seed)
        ks = jax.random.split(key, 16)
        bs, n, d = (16, 1024, DIM)
        s = 0.05
        return {'x': jax.random.normal(ks[0], (bs, n, d), jnp.float32), 'mask': jnp.ones((bs, n, n), jnp.float32), 'w_se': jax.random.normal(ks[1], (3, d), jnp.float32) * s, 'b_se': jnp.zeros((3,), jnp.float32), 'conv1_w': jax.random.normal(ks[2], (d, d, 1), jnp.float32) * s, 'bn1_g': jnp.ones((d,), jnp.float32), 'bn1_b': jnp.zeros((d,), jnp.float32), 'bn1_m': jnp.zeros((d,), jnp.float32), 'bn1_v': jnp.ones((d,), jnp.float32), 'conv2_w': jax.random.normal(ks[3], (d, d, 17), jnp.float32) * s, 'bn2_g': jnp.ones((d,), jnp.float32), 'bn2_b': jnp.zeros((d,), jnp.float32), 'bn2_m': jnp.zeros((d,), jnp.float32), 'bn2_v': jnp.ones((d,), jnp.float32), 'w_msg': jax.random.normal(ks[4], (d, d), jnp.float32) * s, 'b_msg': jnp.zeros((d,), jnp.float32), 'w_ih': jax.random.normal(ks[5], (3 * d, 2 * d), jnp.float32) * s, 'b_ih': jnp.zeros((3 * d,), jnp.float32), 'w_hh': jax.random.normal(ks[6], (3 * d, d), jnp.float32) * s, 'b_hh': jnp.zeros((3 * d,), jnp.float32)}
    _L0_gnn_all = _L0_gnn_setup()
    _L0_gnn_in = {k: v for k, v in _L0_gnn_all.items() if k in ('w_se', 'b_se', 'conv1_w', 'bn1_g', 'bn1_b', 'bn1_m', 'bn1_v', 'conv2_w', 'bn2_g', 'bn2_b', 'bn2_m', 'bn2_v', 'w_msg', 'b_msg', 'w_ih', 'b_ih', 'w_hh', 'b_hh')}
    del _L0_gnn_all

    def _L0_ffn_setup():
        import jax, jax.numpy as jnp
        import numpy as np
        D_MODEL = 128
        D_STATE = 64
        D_CONV = 4
        EXPAND = 2
        HEADDIM = 64
        D_INNER = EXPAND * D_MODEL
        NHEADS = D_INNER // HEADDIM
        CONV_DIM = D_INNER + 2 * D_STATE
        D_IN_PROJ = 2 * D_INNER + 2 * D_STATE + NHEADS
        CHUNK = 128
        EPS = 1e-05

        def segsum(a):
            T = a.shape[-1]
            cs = jnp.cumsum(a, axis=-1)
            ss = cs[..., :, None] - cs[..., None, :]
            mask = jnp.tril(jnp.ones((T, T), dtype=bool))
            return jnp.where(mask, ss, -jnp.inf)

        def mamba2_block(x, W_in, conv_w, conv_b, dt_bias, A_log, D, norm_w, W_out, W_lin, b_lin):
            Bsz, L, _ = x.shape
            zxbcdt = x @ W_in
            z, xBC, dt = jnp.split(zxbcdt, [D_INNER, D_INNER + CONV_DIM], axis=-1)
            xp = jnp.pad(xBC, ((0, 0), (D_CONV - 1, 0), (0, 0)))
            conv = conv_b + sum((xp[:, k:k + L, :] * conv_w[:, k] for k in range(D_CONV)))
            xBC = jax.nn.silu(conv)
            xh, Bmat, Cmat = jnp.split(xBC, [D_INNER, D_INNER + D_STATE], axis=-1)
            dt = jax.nn.softplus(dt + dt_bias)
            A = -jnp.exp(A_log)
            nc = L // CHUNK
            xh = xh.reshape(Bsz, nc, CHUNK, NHEADS, HEADDIM)
            Bc = Bmat.reshape(Bsz, nc, CHUNK, D_STATE)
            Cc = Cmat.reshape(Bsz, nc, CHUNK, D_STATE)
            dtc = dt.reshape(Bsz, nc, CHUNK, NHEADS)
            dA = jnp.einsum('bclh,h->bhcl', dtc, A)
            A_cum = jnp.cumsum(dA, axis=-1)
            Lmat = jnp.exp(segsum(dA))
            xdt = xh * dtc[..., None]
            Y_diag = jnp.einsum('bcln,bcsn,bhcls,bcshp->bclhp', Cc, Bc, Lmat, xdt)
            decay_states = jnp.exp(A_cum[..., -1:] - A_cum)
            states = jnp.einsum('bcln,bhcl,bclhp->bchpn', Bc, decay_states, xdt)
            chunk_decay = jnp.exp(A_cum[..., -1])

            def step(h, inp):
                s, d = inp
                return (h * d[..., None, None] + s, h)
            _, prevs = jax.lax.scan(step, jnp.zeros_like(states[:, 0]), (jnp.moveaxis(states, 1, 0), jnp.moveaxis(chunk_decay, 2, 0)))
            prevs = jnp.moveaxis(prevs, 0, 1)
            Y_off = jnp.einsum('bcln,bchpn,bhcl->bclhp', Cc, prevs, jnp.exp(A_cum))
            Y = (Y_diag + Y_off + xh * D[:, None]).reshape(Bsz, L, D_INNER)
            Y = Y * jax.nn.silu(z)
            Y = Y * jax.lax.rsqrt(jnp.mean(Y * Y, axis=-1, keepdims=True) + EPS) * norm_w
            out = Y @ W_out
            return out @ W_lin + b_lin
        key = jax.random.key(seed)
        ks = jax.random.split(key, 12)
        B, L = (8, 2048)

        def gauss(k, shape, scale):
            return jax.random.normal(k, shape, dtype=jnp.float32) * scale
        return {'x': gauss(ks[0], (B, L, D_MODEL), 1.0), 'W_in': gauss(ks[1], (D_MODEL, D_IN_PROJ), D_MODEL ** (-0.5)), 'conv_w': gauss(ks[2], (CONV_DIM, D_CONV), 0.3), 'conv_b': gauss(ks[3], (CONV_DIM,), 0.1), 'dt_bias': jax.random.uniform(ks[4], (NHEADS,), minval=-4.0, maxval=-1.0), 'A_log': jnp.log(jax.random.uniform(ks[5], (NHEADS,), minval=1.0, maxval=16.0)), 'D': jnp.ones((NHEADS,), jnp.float32), 'norm_w': jnp.ones((D_INNER,), jnp.float32), 'W_out': gauss(ks[6], (D_INNER, D_MODEL), D_INNER ** (-0.5)), 'W_lin': gauss(ks[7], (D_MODEL, D_MODEL), D_MODEL ** (-0.5)), 'b_lin': jnp.zeros((D_MODEL,), jnp.float32)}
    _L0_ffn_all = _L0_ffn_setup()
    _L0_ffn_in = {k: v for k, v in _L0_ffn_all.items() if k in ('W_in', 'conv_w', 'conv_b', 'dt_bias', 'A_log', 'D', 'norm_w', 'W_out', 'W_lin', 'b_lin')}
    del _L0_ffn_all

    def _L1_gnn_setup():
        import jax, jax.numpy as jnp
        import numpy as np
        B, N, C_IN, C_OUT = (8, 1024, 128, 128)
        key = jax.random.key(seed)
        k1, k2, k3 = jax.random.split(key, 3)
        x = jax.random.normal(k1, (B, N, C_IN), dtype=jnp.float32)
        adj = jax.random.uniform(k2, (B, N, N), dtype=jnp.float32)
        limit = float(np.sqrt(6.0 / (C_IN + C_OUT)))
        weight = jax.random.uniform(k3, (C_IN, C_OUT), minval=-limit, maxval=limit, dtype=jnp.float32)
        bias = jnp.zeros((C_OUT,), dtype=jnp.float32)
        return {'x': x, 'adj': adj, 'weight': weight, 'bias': bias}
    _L1_gnn_all = _L1_gnn_setup()
    _L1_gnn_in = {k: v for k, v in _L1_gnn_all.items() if k in ('weight', 'bias')}
    del _L1_gnn_all

    def _L1_ffn_setup():
        import jax, jax.numpy as jnp
        import numpy as np
        N_EXPERTS = 8
        TOP_K = 2
        key = jax.random.key(seed)
        ks = jax.random.split(key, 5)
        B, T, C, E, H = (8, 1024, 128, 8, 341)
        scale = 1.0 / np.sqrt(C)
        return {'x': jax.random.normal(ks[0], (B, T, C), dtype=jnp.float32), 'router_w': jax.random.normal(ks[1], (E, C), dtype=jnp.float32) * scale, 'w1': jax.random.normal(ks[2], (E, H, C), dtype=jnp.float32) * scale, 'w2': jax.random.normal(ks[3], (E, C, H), dtype=jnp.float32) * (1.0 / np.sqrt(H)), 'w3': jax.random.normal(ks[4], (E, H, C), dtype=jnp.float32) * scale}
    _L1_ffn_all = _L1_ffn_setup()
    _L1_ffn_in = {k: v for k, v in _L1_ffn_all.items() if k in ('router_w', 'w1', 'w2', 'w3')}
    del _L1_ffn_all
    return {'x': x, 'adj': adj, 'L0_gnn_w_se': _L0_gnn_in['w_se'], 'L0_gnn_b_se': _L0_gnn_in['b_se'], 'L0_gnn_conv1_w': _L0_gnn_in['conv1_w'], 'L0_gnn_bn1_g': _L0_gnn_in['bn1_g'], 'L0_gnn_bn1_b': _L0_gnn_in['bn1_b'], 'L0_gnn_bn1_m': _L0_gnn_in['bn1_m'], 'L0_gnn_bn1_v': _L0_gnn_in['bn1_v'], 'L0_gnn_conv2_w': _L0_gnn_in['conv2_w'], 'L0_gnn_bn2_g': _L0_gnn_in['bn2_g'], 'L0_gnn_bn2_b': _L0_gnn_in['bn2_b'], 'L0_gnn_bn2_m': _L0_gnn_in['bn2_m'], 'L0_gnn_bn2_v': _L0_gnn_in['bn2_v'], 'L0_gnn_w_msg': _L0_gnn_in['w_msg'], 'L0_gnn_b_msg': _L0_gnn_in['b_msg'], 'L0_gnn_w_ih': _L0_gnn_in['w_ih'], 'L0_gnn_b_ih': _L0_gnn_in['b_ih'], 'L0_gnn_w_hh': _L0_gnn_in['w_hh'], 'L0_gnn_b_hh': _L0_gnn_in['b_hh'], 'L0_ffn_W_in': _L0_ffn_in['W_in'], 'L0_ffn_conv_w': _L0_ffn_in['conv_w'], 'L0_ffn_conv_b': _L0_ffn_in['conv_b'], 'L0_ffn_dt_bias': _L0_ffn_in['dt_bias'], 'L0_ffn_A_log': _L0_ffn_in['A_log'], 'L0_ffn_D': _L0_ffn_in['D'], 'L0_ffn_norm_w': _L0_ffn_in['norm_w'], 'L0_ffn_W_out': _L0_ffn_in['W_out'], 'L0_ffn_W_lin': _L0_ffn_in['W_lin'], 'L0_ffn_b_lin': _L0_ffn_in['b_lin'], 'L1_gnn_weight': _L1_gnn_in['weight'], 'L1_gnn_bias': _L1_gnn_in['bias'], 'L1_ffn_router_w': _L1_ffn_in['router_w'], 'L1_ffn_w1': _L1_ffn_in['w1'], 'L1_ffn_w2': _L1_ffn_in['w2'], 'L1_ffn_w3': _L1_ffn_in['w3']}

def reference(x, adj, L0_gnn_w_se, L0_gnn_b_se, L0_gnn_conv1_w, L0_gnn_bn1_g, L0_gnn_bn1_b, L0_gnn_bn1_m, L0_gnn_bn1_v, L0_gnn_conv2_w, L0_gnn_bn2_g, L0_gnn_bn2_b, L0_gnn_bn2_m, L0_gnn_bn2_v, L0_gnn_w_msg, L0_gnn_b_msg, L0_gnn_w_ih, L0_gnn_b_ih, L0_gnn_w_hh, L0_gnn_b_hh, L0_ffn_W_in, L0_ffn_conv_w, L0_ffn_conv_b, L0_ffn_dt_bias, L0_ffn_A_log, L0_ffn_D, L0_ffn_norm_w, L0_ffn_W_out, L0_ffn_W_lin, L0_ffn_b_lin, L1_gnn_weight, L1_gnn_bias, L1_ffn_router_w, L1_ffn_w1, L1_ffn_w2, L1_ffn_w3):
    import jax
    import jax.numpy as jnp

    def _L0_gnn_ref(x, mask, w_se, b_se, conv1_w, bn1_g, bn1_b, bn1_m, bn1_v, conv2_w, bn2_g, bn2_b, bn2_m, bn2_v, w_msg, b_msg, w_ih, b_ih, w_hh, b_hh):
        import jax, jax.numpy as jnp
        import numpy as np
        from jax import lax
        DIM = 128
        EPS = 1e-05

        def _bn(h, g, b, m, v):
            scale = g / jnp.sqrt(v + EPS)
            return h * scale[None, :, None] + (b - m * scale)[None, :, None]

        def _conv1d(h, w, pad):
            return lax.conv_general_dilated(h, w, window_strides=(1,), padding=[(pad, pad)], dimension_numbers=('NCH', 'OIH', 'NCH'))
        d = x.shape[-1]
        xc = jnp.transpose(x, (0, 2, 1))
        h = _bn(_conv1d(xc, conv1_w, 0), bn1_g, bn1_b, bn1_m, bn1_v)
        h = jax.nn.relu(h)
        h = _bn(_conv1d(h, conv2_w, 8), bn2_g, bn2_b, bn2_m, bn2_v)
        x_conv = jnp.transpose(jax.nn.relu(h + xc), (0, 2, 1))
        s = x @ w_se.T + b_se
        sq = jnp.sum(s * s, axis=-1)
        dist = sq[:, :, None] + sq[:, None, :] - 2.0 * jnp.einsum('bnd,bmd->bnm', s, s)
        A = jnp.exp(-dist) * mask
        msg = jax.nn.relu(x @ w_msg.T + b_msg)
        x_nmp = jnp.einsum('bnm,bmd->bnd', A, msg)
        x_in = jnp.concatenate([x_conv, x_nmp], axis=-1)
        gi = x_in @ w_ih.T + b_ih
        gh = x @ w_hh.T + b_hh
        gi_r, gi_z, gi_n = (gi[..., :d], gi[..., d:2 * d], gi[..., 2 * d:])
        gh_r, gh_z, gh_n = (gh[..., :d], gh[..., d:2 * d], gh[..., 2 * d:])
        r = jax.nn.sigmoid(gi_r + gh_r)
        z = jax.nn.sigmoid(gi_z + gh_z)
        nn_ = jnp.tanh(gi_n + r * gh_n)
        return (1.0 - z) * nn_ + z * x

    def _L0_ffn_ref(x, W_in, conv_w, conv_b, dt_bias, A_log, D, norm_w, W_out, W_lin, b_lin):
        import jax, jax.numpy as jnp
        import numpy as np
        D_MODEL = 128
        D_STATE = 64
        D_CONV = 4
        EXPAND = 2
        HEADDIM = 64
        D_INNER = EXPAND * D_MODEL
        NHEADS = D_INNER // HEADDIM
        CONV_DIM = D_INNER + 2 * D_STATE
        D_IN_PROJ = 2 * D_INNER + 2 * D_STATE + NHEADS
        CHUNK = 128
        EPS = 1e-05

        def segsum(a):
            T = a.shape[-1]
            cs = jnp.cumsum(a, axis=-1)
            ss = cs[..., :, None] - cs[..., None, :]
            mask = jnp.tril(jnp.ones((T, T), dtype=bool))
            return jnp.where(mask, ss, -jnp.inf)

        def mamba2_block(x, W_in, conv_w, conv_b, dt_bias, A_log, D, norm_w, W_out, W_lin, b_lin):
            Bsz, L, _ = x.shape
            zxbcdt = x @ W_in
            z, xBC, dt = jnp.split(zxbcdt, [D_INNER, D_INNER + CONV_DIM], axis=-1)
            xp = jnp.pad(xBC, ((0, 0), (D_CONV - 1, 0), (0, 0)))
            conv = conv_b + sum((xp[:, k:k + L, :] * conv_w[:, k] for k in range(D_CONV)))
            xBC = jax.nn.silu(conv)
            xh, Bmat, Cmat = jnp.split(xBC, [D_INNER, D_INNER + D_STATE], axis=-1)
            dt = jax.nn.softplus(dt + dt_bias)
            A = -jnp.exp(A_log)
            nc = L // CHUNK
            xh = xh.reshape(Bsz, nc, CHUNK, NHEADS, HEADDIM)
            Bc = Bmat.reshape(Bsz, nc, CHUNK, D_STATE)
            Cc = Cmat.reshape(Bsz, nc, CHUNK, D_STATE)
            dtc = dt.reshape(Bsz, nc, CHUNK, NHEADS)
            dA = jnp.einsum('bclh,h->bhcl', dtc, A)
            A_cum = jnp.cumsum(dA, axis=-1)
            Lmat = jnp.exp(segsum(dA))
            xdt = xh * dtc[..., None]
            Y_diag = jnp.einsum('bcln,bcsn,bhcls,bcshp->bclhp', Cc, Bc, Lmat, xdt)
            decay_states = jnp.exp(A_cum[..., -1:] - A_cum)
            states = jnp.einsum('bcln,bhcl,bclhp->bchpn', Bc, decay_states, xdt)
            chunk_decay = jnp.exp(A_cum[..., -1])

            def step(h, inp):
                s, d = inp
                return (h * d[..., None, None] + s, h)
            _, prevs = jax.lax.scan(step, jnp.zeros_like(states[:, 0]), (jnp.moveaxis(states, 1, 0), jnp.moveaxis(chunk_decay, 2, 0)))
            prevs = jnp.moveaxis(prevs, 0, 1)
            Y_off = jnp.einsum('bcln,bchpn,bhcl->bclhp', Cc, prevs, jnp.exp(A_cum))
            Y = (Y_diag + Y_off + xh * D[:, None]).reshape(Bsz, L, D_INNER)
            Y = Y * jax.nn.silu(z)
            Y = Y * jax.lax.rsqrt(jnp.mean(Y * Y, axis=-1, keepdims=True) + EPS) * norm_w
            out = Y @ W_out
            return out @ W_lin + b_lin
        return mamba2_block(x, W_in, conv_w, conv_b, dt_bias, A_log, D, norm_w, W_out, W_lin, b_lin)

    def _L1_gnn_ref(x, adj, weight, bias):
        import jax, jax.numpy as jnp
        import numpy as np
        B, N, C_IN, C_OUT = (8, 1024, 128, 128)
        d_inv_sqrt = (jnp.sum(adj, axis=-1) + 1e-05) ** (-0.5)
        adj_norm = d_inv_sqrt[..., :, None] * adj * d_inv_sqrt[..., None, :]
        support = jnp.einsum('bni,io->bno', x, weight)
        return jnp.einsum('bnm,bmo->bno', adj_norm, support) + bias

    def _L1_ffn_ref(x, router_w, w1, w2, w3):
        import jax, jax.numpy as jnp
        import numpy as np
        N_EXPERTS = 8
        TOP_K = 2
        B, T, C = x.shape
        flat = x.reshape(-1, C)
        logits = flat @ router_w.T
        probs = jax.nn.softmax(logits, axis=-1)
        topk_probs, topk_idx = jax.lax.top_k(probs, TOP_K)
        topk_probs = topk_probs / (jnp.sum(topk_probs, axis=-1, keepdims=True) + 1e-09)
        onehot = jax.nn.one_hot(topk_idx, N_EXPERTS, dtype=flat.dtype)
        gates = jnp.einsum('nk,nke->ne', topk_probs, onehot)
        h1 = jnp.einsum('nc,ehc->neh', flat, w1)
        h3 = jnp.einsum('nc,ehc->neh', flat, w3)
        h = jax.nn.silu(h1) * h3
        y = jnp.einsum('neh,ech->nec', h, w2)
        out = jnp.einsum('ne,nec->nc', gates, y)
        return out.reshape(B, T, C)
    x = x + _L0_gnn_ref(_layernorm(x, axis=-1), adj, L0_gnn_w_se, L0_gnn_b_se, L0_gnn_conv1_w, L0_gnn_bn1_g, L0_gnn_bn1_b, L0_gnn_bn1_m, L0_gnn_bn1_v, L0_gnn_conv2_w, L0_gnn_bn2_g, L0_gnn_bn2_b, L0_gnn_bn2_m, L0_gnn_bn2_v, L0_gnn_w_msg, L0_gnn_b_msg, L0_gnn_w_ih, L0_gnn_b_ih, L0_gnn_w_hh, L0_gnn_b_hh)
    x = x + _L0_ffn_ref(_layernorm(x, axis=-1), L0_ffn_W_in, L0_ffn_conv_w, L0_ffn_conv_b, L0_ffn_dt_bias, L0_ffn_A_log, L0_ffn_D, L0_ffn_norm_w, L0_ffn_W_out, L0_ffn_W_lin, L0_ffn_b_lin)
    x = x + _L1_gnn_ref(_layernorm(x, axis=-1), adj, L1_gnn_weight, L1_gnn_bias)
    x = x + _L1_ffn_ref(_layernorm(x, axis=-1), L1_ffn_router_w, L1_ffn_w1, L1_ffn_w2, L1_ffn_w3)
    return x

_drawn_inputs = setup_inputs


def setup_inputs(seed=0):
    import zlib

    import numpy as np

    out = dict(_drawn_inputs(seed))
    spreads = {'L0_gnn_b_se': (0.0, 0.8),
     'L0_gnn_bn1_g': (1.0, 0.2),
     'L0_gnn_bn1_b': (0.0, 0.1),
     'L0_gnn_bn1_m': (0.0, 0.1),
     'L0_gnn_bn1_v': (1.0, 0.6),
     'L0_gnn_bn2_g': (1.0, 0.2),
     'L0_gnn_bn2_b': (0.0, 0.322),
     'L0_gnn_bn2_m': (0.0, 0.293),
     'L0_gnn_bn2_v': (1.0, 0.6),
     'L0_gnn_b_msg': (0.0, 0.1),
     'L0_gnn_b_ih': (0.0, 0.1),
     'L0_gnn_b_hh': (0.0, 0.1),
     'L0_ffn_D': (1.0, 0.2),
     'L0_ffn_norm_w': (1.0, 0.2),
     'L0_ffn_b_lin': (0.0, 0.1),
     'L1_gnn_bias': (0.0, 0.1)}
    factors = {'L0_ffn_A_log': 4.269}
    for name, (base, spread) in spreads.items():
        noise = np.random.default_rng([zlib.crc32(name.encode()), seed]).standard_normal(out[name].shape)
        drawn = base * np.exp(spread * noise) if base else spread * noise
        out[name] = jnp.asarray(drawn.astype(out[name].dtype))
    for name, factor in factors.items():
        out[name] = (out[name] * factor).astype(out[name].dtype)
    return out
```

```python
from contextlib import ExitStack

import concourse.bass as bass
from concourse import mybir

F32 = mybir.dt.float32
F32R = mybir.dt.float32r
ACT = mybir.ActivationFunctionType
ALU = mybir.AluOpType
AX = mybir.AxisListType

P = 128
BS = 32
N = 256
T = 4
G = 2
S = T * P
STEPS = BS * N // S
NT = STEPS * T
EPS = 1e-5


class Step:

    def __init__(self, u, p, steps=STEPS):
        self.u, self.p, self.t, self.steps = u, p, 2 * u + p, steps

    def back(self, lag):
        q = self.p - lag
        return Step(self.u + q // 2, q % 2, self.steps)

    def live(self):
        return not isinstance(self.t, int) or 0 <= self.t < self.steps


def run_steps(eng, body, lags, steps=STEPS):
    head = max(1, (lags + 1) // 2)
    for t in range(2 * head):
        body(Step(t // 2, t % 2, steps))
    with eng.Fori(head, steps // 2) as u:
        body(Step(u, 0, steps))
        body(Step(u, 1, steps))
    for t in range(steps, steps + lags):
        body(Step(t // 2, t % 2, steps))


def need(eng, sem, count):
    if isinstance(count, int) and count <= 0:
        return
    eng.wait_ge(sem, count)


def hold(eng, sem, count):
    need(eng, sem, count)
    if not isinstance(count, int):
        eng.nop(nofuse=True)


class Pair:

    def __init__(self, hi, lo):
        self.hi, self.lo = hi, lo

    def __getitem__(self, k):
        return Pair(self.hi[k], self.lo[k])


def product(pe, out, lhsT, rhs, start, stop):
    pe.matmul(out, lhsT.hi, rhs.hi, start=start, stop=False)
    pe.matmul(out, lhsT.hi, rhs.lo, start=False, stop=False)
    return pe.matmul(out, lhsT.lo, rhs.hi, start=False, stop=stop)


class Phase:

    def __init__(self, nc, ctx, name):
        self.nc, self.ctx, self.name, self.sems = nc, ctx, name, []
        ctx.callback(self.clear)

    def clear(self):
        self.nc.clear_and_free_semaphores(self.sems)
        self.nc.all_engine_barrier()

    def sb(self, name, shape, dt=F32):
        return self.ctx.enter_context(self.nc.sbuf_tensor(self.name + name, shape, dt))

    def pair(self, name, shape):
        return Pair(self.sb(name + "_hi", shape, F32R), self.sb(name + "_lo", shape, F32R))

    def psum(self, name, shape):
        return self.ctx.enter_context(self.nc.psum_tensor(self.name + name, shape, F32))

    def sem(self, name):
        self.sems.append(self.nc.alloc_semaphore(name=self.name + name))
        return self.sems[-1]


def column(v):
    return v.rearrange("(p a) -> p a", a=1)


def spread(v, parts=P):
    return bass.AP(v.tensor, v.offset, [[0, parts]] + list(v.ap))


def layer_norm_stats(dve, X, s, stats, mv, stats_done, mv_done):
    for j in range(T):
        dve.bn_stats(stats[:, j, :], X[:, s.t * T + j, :]).then_inc(stats_done, 1)
    for j in range(T):
        hold(dve, stats_done, T * s.t + j + 1)
        dve.bn_aggr(mv[:, j, :], stats[:, j, :]).then_inc(mv_done, 1)


def layer_norm_apply(dve, X, s, xn, mv, rstd, xn_ready):
    for j in range(T):
        dve.tensor_scalar(xn[:, j, :], X[:, s.t * T + j, :], mv[:, j, 0:1], rstd[:, j:j + 1], ALU.subtract, ALU.mult).then_inc(xn_ready, 1)


def gnn_phase(nc, x_dram, adjT_dram, w, X, eye):
    TAPS = 17
    PAD = TAPS // 2
    NP = N + 2 * PAD
    L0, R0, KD = 0, 32, 9
    with ExitStack() as ctx:
        ph = Phase(nc, ctx, "g_")
        sb, pair, sem = ph.sb, ph.pair, ph.sem
        stage = sb("stage", [P, TAPS * P])
        conv1 = pair("conv1", [P, P])
        conv2 = pair("conv2", [P, TAPS * P])
        w_lr = pair("w_lr", [P, 64])
        w_msg = pair("w_msg", [P, P])
        w_ih = pair("w_ih", [P, 2 * 3 * P])
        w_hh = pair("w_hh", [P, 3 * P])
        b_msg = sb("b_msg", [P, P])
        lr_cols = sb("lr_cols", [64, 3])
        vecs = sb("vecs", [P, 14])
        BN = {"g1": 0, "b1": 1, "m1": 2, "v1": 3, "g2": 4, "b2": 5, "m2": 6, "v2": 7}
        B_IH, B_HH = 8, 11
        scales = sb("scales", [P, 8])
        tmp2 = sb("tmp2", [P, 4])
        minus_half = sb("minus_half", [P, 4])
        adjT = sb("adjT", [P, 2, G, 2, N])
        stats = sb("stats", [P, T, 6])
        mv = sb("mv", [P, T, 2])
        veps = sb("veps", [P, T])
        rstd = sb("rstd", [P, T])
        xn = sb("xn", [P, T, P])
        xf = sb("xf", [P, 2, S])
        xs = pair("xs", [P, 2, S])
        h1f = sb("h1f", [P, G, N])
        h1 = pair("h1", [P, G, NP])
        t1 = sb("t1", [64, S])
        t2 = sb("t2", [64, S])
        q = sb("q", [64, S])
        right = sb("right", [KD, S])
        mb = sb("mb", [P, T, P])
        mf = sb("mf", [P, T, P])
        msg = pair("msg", [P, T, P])
        E = sb("E", [P, G, 2, N])
        Am = sb("Am", [P, G, 2, N])
        A = pair("A", [P, G, 2, N])
        v = sb("v", [P, S])
        xcf = sb("xcf", [P, S])
        xc = pair("xc", [P, S])
        nm = pair("nm", [P, S])
        gh = sb("gh", [P, S])
        tr = sb("tr", [P, S])
        tz = sb("tz", [P, S])
        u_ = sb("u", [P, S])
        tn = sb("tn", [P, S])
        d_ = sb("d", [P, S])
        g_ = sb("gg", [P, S])
        hT = sb("hT", [P, S])
        p_conv2 = ph.psum("p_conv2", [P, S])
        p_msg = p_conv2
        p_nmp = ph.psum("p_nmp", [P, S])
        p_lr = p_nmp
        p_xT = ph.psum("p_xT", [P, S])
        p_conv1 = p_xT
        p_dist = ph.psum("p_dist", [P, G, 2, N])
        p_back = p_dist[:, 0, :, :].rearrange("p a b -> p (a b)")
        p_r = ph.psum("p_r", [P, S])
        p_z = ph.psum("p_z", [P, S])
        p_n = ph.psum("p_n", [P, S])

        loaded = sem("loaded")
        w_loaded = sem("w_loaded")
        w_split = sem("w_split")
        stage_clear, w_hi = sem("stage_clear"), sem("w_hi")
        consts = sem("consts")
        bn_ready = sem("bn_ready")
        x_in = [sem(f"x_in{p}") for p in range(2)]
        stats_done, mv_done, veps_done, rstd_done = sem("stats_done"), sem("mv_done"), sem("veps_done"), sem("rstd_done")
        xn_ready = sem("xn_ready")
        xT_done, x_hi_f, x_split = sem("xT_done"), sem("x_hi_f"), sem("x_split")
        conv1_done, h1_hi_f, h1_split = sem("conv1_done"), sem("h1_hi_f"), sem("h1_split")
        lr_done, t1_ready, t2_ready, q_ready, right_ready = (sem(s) for s in ("lr_done", "t1_ready", "t2_ready", "q_ready", "right_ready"))
        msg_done, msg_biased, msg_hi_f, msg_split = (sem(s) for s in ("msg_done", "msg_biased", "msg_hi_f", "msg_split"))
        dist_done, exp_done, masked, A_split = (sem(s) for s in ("dist_done", "exp_done", "masked", "A_split"))
        conv2_done, v_ready, xc_hi_f, xc_split = (sem(s) for s in ("conv2_done", "v_ready", "xc_hi_f", "xc_split"))
        nmp_done, nmp_hi, nmp_split = sem("nmp_done"), sem("nmp_hi"), sem("nmp_split")
        ghn_done, gh_ready, r_done, z_done, n_done = (sem(s) for s in ("ghn_done", "gh_ready", "r_done", "z_done", "n_done"))
        tr_ready, tz_ready, rg_ready, u_ready, tn_ready, d_ready, g_ready, hT_ready = (
            sem(s) for s in ("tr_ready", "tz_ready", "rg_ready", "u_ready", "tn_ready", "d_ready", "g_ready", "hT_ready"))
        back_done, x_updated = sem("back_done"), sem("x_updated")

        weights = [(w["conv1T"], conv1), (w["conv2T"], conv2), (w["w_msgT"], w_msg), (w["w_ihT"], w_ih), (w["w_hhT"], w_hh)]
        block = ctx.enter_context(nc.Block())

        @block.sync
        def _(sp):
            sp.dma_start(vecs[:], w["gnn_vecs"]).then_inc(loaded, 16)
            sp.dma_start(b_msg[:], spread(w["b_msg"])).then_inc(loaded, 16)
            sp.dma_start(lr_cols[:], w["lr_const"]).then_inc(consts, 16)
            sp.wait_ge(consts, 16)
            for row in (L0, L0 + 3, R0, R0 + 6):
                sp.dma_start(lr_cols[row:row + 3, 0:1], column(w["b_se"])).then_inc(loaded, 16)
            sp.wait_ge(stage_clear, 1)
            for k, at in enumerate((L0, L0 + 3, R0, R0 + 6)):
                sp.dma_start(stage[:, at:at + 3], w["w_seT"]).then_inc(w_loaded, 16)
            for k, (src, dst) in enumerate(weights):
                sp.wait_ge(w_split, k + 1)
                width = src.shape[1]
                sp.dma_start(stage[:, 0:width], src).then_inc(w_loaded, 16)

            def body(s):
                if s.live():
                    hold(sp, masked, s.t - 1)
                    sp.dma_start(adjT[:, s.p], adjT_dram[bass.ts(s.t, G)].rearrange("g (a m) n -> m g a n", m=P)).then_inc(x_in[s.p], 16)
                    sp.dma_start(X[:, bass.ts(s.t, T), :], x_dram[bass.ts(s.t, T)].rearrange("t p d -> p t d")).then_inc(x_in[s.p], 16)
            run_steps(sp, body, 0)

        @block.gpsimd
        def _(pool):
            pool.memset(stage[:, 0:64], 0.0).then_inc(stage_clear, 1)
            pool.memset(minus_half[:], -0.5).then_inc(bn_ready, 1)
            for part in (h1.hi, h1.lo):
                pool.memset(part[:].bitcast(F32), 0.0).then_inc(bn_ready, 1)
            pool.wait_ge(loaded, 16 * 6)
            v_cols = vecs[:, BN["v1"]:BN["v2"] + 1:4]
            g_cols = vecs[:, BN["g1"]:BN["g2"] + 1:4]
            b_cols = vecs[:, BN["b1"]:BN["b2"] + 1:4]
            m_cols = vecs[:, BN["m1"]:BN["m2"] + 1:4]
            pool.tensor_scalar(tmp2[:, 0:2], v_cols, EPS, None, ALU.add).then_inc(bn_ready, 1)
            pool.wait_ge(bn_ready, 4)
            pool.tensor_tensor(tmp2[:, 2:4], tmp2[:, 0:2], minus_half[:, 0:2], ALU.pow).then_inc(bn_ready, 1)
            pool.wait_ge(bn_ready, 5)
            pool.tensor_tensor(scales[:, 0:2], tmp2[:, 2:4], g_cols, ALU.mult).then_inc(bn_ready, 1)
            pool.wait_ge(bn_ready, 6)
            pool.tensor_tensor(tmp2[:, 0:2], scales[:, 0:2], m_cols, ALU.mult).then_inc(bn_ready, 1)
            pool.wait_ge(bn_ready, 7)
            pool.tensor_tensor(scales[:, 2:4], b_cols, tmp2[:, 0:2], ALU.subtract).then_inc(bn_ready, 1)
            pool.tensor_tensor(scales[:, 4:6], vecs[:, B_IH:B_IH + 2], vecs[:, B_HH:B_HH + 2], ALU.add).then_inc(bn_ready, 1)
            pool.tensor_scalar(scales[:, 6:7], vecs[:, B_HH + 2:B_HH + 3], 0.5, None, ALU.mult).then_inc(bn_ready, 1)
            pool.wait_ge(bn_ready, 10)
            pool.tensor_scalar(scales[:, 4:6], scales[:, 4:6], 0.5, None, ALU.mult).then_inc(bn_ready, 1)

            def body(s):
                if s.live():
                    pool.wait_ge(mv_done, 4 * (s.t + 1))
                    hold(pool, xn_ready, 4 * s.t)
                    pool.tensor_scalar(veps[:], mv[:, :, 1], EPS, None, ALU.add).then_inc(veps_done, 1)
                    pool.wait_ge(veps_done, s.t + 1)
                    pool.tensor_tensor(rstd[:], veps[:], minus_half[:], ALU.pow).then_inc(rstd_done, 1)
                b = s.back(1)
                if s.live():
                    pool.wait_ge(x_hi_f, 2 * (s.t + 1))
                    need(pool, n_done, s.t - 1)
                    pool.tensor_tensor(xs.lo[:, s.p], xf[:, s.p], xs.hi[:, s.p].bitcast(F32), ALU.subtract).then_inc(x_split, 1)
                    pool.wait_ge(t1_ready, s.t + 1)
                    hold(pool, dist_done, s.t)
                    pool.tensor_scalar(t2[:], t1[:], lr_cols[:, 1:2], lr_cols[:, 2:3], ALU.mult, ALU.add).then_inc(t2_ready, 1)
                    pool.wait_ge(t2_ready, s.t + 1)
                    pool.tensor_tensor(q[:], t1[:], t2[:], ALU.mult).then_inc(q_ready, 1)
                if b.live():
                    pool.wait_ge(tn_ready, b.t + 1)
                    need(pool, g_ready, b.t)
                    pool.tensor_tensor(d_[:], xf[:, b.p], tn[:], ALU.subtract).then_inc(d_ready, 1)
            run_steps(pool, body, 1)

        @block.scalar
        def _(act):
            act.preload_act_table(ACT.Exp)
            act.wait_ge(bn_ready, 11)
            act.wait_ge(loaded, 16 * 6)

            def body(s):
                b = s.back(1)
                if b.live():
                    act.wait_ge(nmp_done, b.t + 1)
                    act.activation(nm.hi[:], p_nmp[:], ACT.Copy).then_inc(nmp_hi, 1)
                    act.wait_ge(v_ready, b.t + 1)
                    need(act, n_done, b.t)
                    act.activation(xcf[:], v[:], ACT.Relu, bias=scales[:, 3:4]).then_inc(xc_hi_f, 1)
                    act.activation(xc.hi[:], v[:], ACT.Relu, bias=scales[:, 3:4]).then_inc(xc_hi_f, 1)
                if s.live():
                    act.wait_ge(xT_done, s.t + 1)
                    need(act, n_done, s.t - 1)
                    need(act, d_ready, s.t - 1)
                    act.activation(xs.hi[:, s.p], p_xT[:], ACT.Copy).then_inc(x_hi_f, 1)
                    act.activation(xf[:, s.p], p_xT[:], ACT.Copy).then_inc(x_hi_f, 1)
                if b.live():
                    act.wait_ge(ghn_done, b.t + 1)
                    need(act, rg_ready, b.t)
                    act.activation(gh[:], p_n[:], ACT.Identity, bias=scales[:, 6:7], scale=0.5).then_inc(gh_ready, 1)
                if s.live():
                    act.wait_ge(conv1_done, s.t + 1)
                    need(act, conv2_done, s.t)
                    p1 = p_conv1[:].rearrange("p (g n) -> p g n", g=G)
                    act.activation(h1f[:], p1, ACT.Relu, bias=scales[:, 2:3], scale=scales[:, 0:1]).then_inc(h1_hi_f, 1)
                    act.activation(h1.hi[:, :, PAD:PAD + N], p1, ACT.Relu, bias=scales[:, 2:3], scale=scales[:, 0:1]).then_inc(h1_hi_f, 1)
                    act.wait_ge(lr_done, s.t + 1)
                    need(act, q_ready, s.t)
                    act.activation(t1[:], p_lr[0:64, :], ACT.Identity, bias=lr_cols[:, 0:1]).then_inc(t1_ready, 1)
                    act.wait_ge(msg_biased, s.t + 1)
                    need(act, nmp_done, s.t)
                    act.activation(mf[:], mb[:], ACT.Relu).then_inc(msg_hi_f, 1)
                    act.activation(msg.hi[:], mb[:], ACT.Relu).then_inc(msg_hi_f, 1)
                    act.wait_ge(q_ready, s.t + 1)
                    need(act, dist_done, s.t)
                    act.activation(right[:], q[R0:R0 + KD, :], ACT.Copy).then_inc(right_ready, 1)
                if b.live():
                    act.wait_ge(r_done, b.t + 1)
                    need(act, rg_ready, b.t)
                    act.activation(tr[:], p_r[:], ACT.Tanh, bias=scales[:, 4:5], scale=0.5).then_inc(tr_ready, 1)
                    act.wait_ge(z_done, b.t + 1)
                    need(act, g_ready, b.t)
                    act.activation(tz[:], p_z[:], ACT.Tanh, bias=scales[:, 5:6], scale=0.5).then_inc(tz_ready, 1)
                    act.wait_ge(u_ready, b.t + 1)
                    need(act, hT_ready, b.t)
                    act.activation(tn[:], u_[:], ACT.Tanh, bias=vecs[:, B_IH + 2:B_IH + 3]).then_inc(tn_ready, 1)
                if s.live():
                    act.wait_ge(dist_done, s.t + 1)
                    need(act, masked, s.t)
                    act.activation(E[:], p_dist[:], ACT.Exp).then_inc(exp_done, 1)
            run_steps(act, body, 1)

        @block.vector
        def _(dve):
            dsts = [(w_lr, 64)] + [(dst, src.shape[1]) for src, dst in weights]
            for k, (dst, width) in enumerate(dsts):
                dve.wait_ge(w_loaded, 16 * (4 + k))
                dve.tensor_copy(dst.hi[:, 0:width], stage[:, 0:width]).then_inc(w_hi, 1)
                dve.wait_ge(w_hi, 1 + k)
                dve.tensor_tensor(dst.lo[:, 0:width], stage[:, 0:width], dst.hi[:, 0:width].bitcast(F32), ALU.subtract).then_inc(w_split, 1)
            dve.wait_ge(bn_ready, 11)
            dve.wait_ge(loaded, 16 * 6)

            def body(s):
                b, c = s.back(1), s.back(2)
                if c.live():
                    dve.wait_ge(d_ready, c.t + 1)
                    dve.wait_ge(tz_ready, c.t + 1)
                    dve.scalar_tensor_tensor(out=g_[:], in0=tz[:], scalar=1.0, in1=d_[:], op0=ALU.add, op1=ALU.mult).then_inc(g_ready, 1)
                    dve.wait_ge(g_ready, c.t + 1)
                    need(dve, back_done, c.t)
                    dve.scalar_tensor_tensor(out=hT[:], in0=g_[:], scalar=0.5, in1=tn[:], op0=ALU.mult, op1=ALU.add).then_inc(hT_ready, 1)
                if b.live():
                    dve.wait_ge(exp_done, b.t + 1)
                    dve.wait_ge(x_in[b.p], 32 * (b.u + 1))
                    dve.tensor_tensor(Am[:], E[:], adjT[:, b.p], ALU.mult).then_inc(masked, 1)
                    dve.wait_ge(masked, b.t + 1)
                    need(dve, nmp_done, b.t)
                    dve.tensor_copy(A.hi[:], Am[:]).then_inc(A_split, 1)
                    dve.wait_ge(A_split, 2 * b.t + 1)
                    dve.tensor_tensor(A.lo[:], Am[:], A.hi[:].bitcast(F32), ALU.subtract).then_inc(A_split, 1)
                if s.live():
                    dve.wait_ge(x_in[s.p], 32 * (s.u + 1))
                    layer_norm_stats(dve, X, s, stats, mv, stats_done, mv_done)
                    dve.wait_ge(rstd_done, s.t + 1)
                    need(dve, xT_done, s.t)
                    layer_norm_apply(dve, X, s, xn, mv, rstd, xn_ready)
                if b.live():
                    dve.wait_ge(conv2_done, b.t + 1)
                    dve.wait_ge(x_hi_f, 2 * (b.t + 1))
                    dve.scalar_tensor_tensor(out=v[:], in0=p_conv2[:], scalar=scales[:, 1:2], in1=xf[:, b.p], op0=ALU.mult, op1=ALU.add).then_inc(v_ready, 1)
                    dve.wait_ge(nmp_hi, b.t + 1)
                    need(dve, n_done, b.t)
                    dve.tensor_tensor(nm.lo[:], p_nmp[:], nm.hi[:].bitcast(F32), ALU.subtract).then_inc(nmp_split, 1)
                    dve.wait_ge(xc_hi_f, 2 * (b.t + 1))
                    dve.tensor_tensor(xc.lo[:], xcf[:], xc.hi[:].bitcast(F32), ALU.subtract).then_inc(xc_split, 1)
                if c.live():
                    dve.wait_ge(back_done, c.t + 1)
                    xt = X[:, bass.ts(c.t, T), :].rearrange("p t d -> p (t d)")
                    dve.tensor_tensor(xt, xt, p_back, ALU.add).then_inc(x_updated, 1)
                if s.live():
                    dve.wait_ge(msg_done, s.t + 1)
                    need(dve, msg_hi_f, 2 * s.t)
                    bb = b_msg[:].rearrange("p (a d) -> p a d", a=1).broadcast_to([P, T, P])
                    dve.tensor_tensor(mb[:], p_msg[:].rearrange("p (t d) -> p t d", t=T), bb, ALU.add).then_inc(msg_biased, 1)
                    dve.wait_ge(h1_hi_f, 2 * (s.t + 1))
                    dve.tensor_tensor(h1.lo[:, :, PAD:PAD + N], h1f[:], h1.hi[:, :, PAD:PAD + N].bitcast(F32), ALU.subtract).then_inc(h1_split, 1)
                    dve.wait_ge(msg_hi_f, 2 * (s.t + 1))
                    dve.tensor_tensor(msg.lo[:], mf[:], msg.hi[:].bitcast(F32), ALU.subtract).then_inc(msg_split, 1)
                if b.live():
                    dve.wait_ge(tr_ready, b.t + 1)
                    dve.wait_ge(gh_ready, b.t + 1)
                    need(dve, u_ready, b.t)
                    dve.scalar_tensor_tensor(out=v[:], in0=tr[:], scalar=1.0, in1=gh[:], op0=ALU.add, op1=ALU.mult).then_inc(rg_ready, 1)
                    dve.wait_ge(rg_ready, b.t + 1)
                    dve.wait_ge(n_done, b.t + 1)
                    need(dve, tn_ready, b.t)
                    dve.tensor_tensor(u_[:], v[:], p_n[:], ALU.add).then_inc(u_ready, 1)
            run_steps(dve, body, 2)

        @block.tensor
        def _(pe):
            pe.wait_ge(w_split, 1 + len(weights))
            pe.wait_ge(bn_ready, 11)

            def body(s):
                b, c = s.back(1), s.back(2)
                if b.live():
                    pe.wait_ge(h1_split, b.t + 1)
                    pe.wait_ge(msg_biased, b.t + 1)
                    out = p_conv2[:].rearrange("p (g n) -> p g n", g=G)
                    for k in range(TAPS):
                        last = product(pe, out, conv2[:, k * P:(k + 1) * P], h1[:, :, k:k + N], k == 0, k == TAPS - 1)
                    last.then_inc(conv2_done, 1)
                if c.live():
                    pe.wait_ge(hT_ready, c.t + 1)
                    need(pe, exp_done, c.t + 2) if b.live() else None
                    for j in range(T):
                        last = pe.transpose(p_back[:, j * P:(j + 1) * P], hT[:, j * P:(j + 1) * P], eye[:])
                    last.then_inc(back_done, 1)
                if b.live():
                    pe.wait_ge(A_split, 2 * (b.t + 1))
                    pe.wait_ge(msg_split, b.t + 1)
                    pe.wait_ge(t1_ready, b.t + 1)
                    for g in range(G):
                        for a in range(2):
                            last = product(pe, p_nmp[:, g * N:(g + 1) * N], msg[:, 2 * g + a, :], A[:, g, a, :], a == 0, a == 1)
                    last.then_inc(nmp_done, 1)
                if s.live():
                    pe.wait_ge(xn_ready, 4 * (s.t + 1))
                    need(pe, h1_hi_f, 2 * s.t)
                    for j in range(T):
                        last = pe.transpose(p_xT[:, j * P:(j + 1) * P], xn[:, j, :], eye[:])
                    last.then_inc(xT_done, 1)
                if b.live():
                    need(pe, u_ready, b.t)
                    need(pe, tz_ready, b.t)
                    xb = xs[:, b.p]
                    product(pe, p_n[:], w_hh[:, 2 * P:3 * P], xb, True, True).then_inc(ghn_done, 1)
                    product(pe, p_r[:], w_hh[:, 0:P], xb, True, False)
                    product(pe, p_z[:], w_hh[:, P:2 * P], xb, True, False)
                if s.live():
                    pe.wait_ge(x_split, s.t + 1)
                    xb = xs[:, s.p]
                    product(pe, p_conv1[:], conv1[:, :], xb, True, True).then_inc(conv1_done, 1)
                    need(pe, nmp_split, s.t)
                    product(pe, p_lr[0:64, :], w_lr[:, :], xb, True, True).then_inc(lr_done, 1)
                    need(pe, v_ready, s.t)
                    for j in range(T):
                        last = product(pe, p_msg[:, j * P:(j + 1) * P], xb[:, j * P:(j + 1) * P], w_msg[:, :], True, True)
                    last.then_inc(msg_done, 1)
                if b.live():
                    pe.wait_ge(xc_split, b.t + 1)
                    pe.wait_ge(nmp_split, b.t + 1)
                    for k, (bank, done) in enumerate(((p_r, r_done), (p_z, z_done), (p_n, n_done))):
                        if bank is p_n:
                            pe.wait_ge(gh_ready, b.t + 1)
                        product(pe, bank[:], w_ih[:, k * P:(k + 1) * P], xc[:, :], bank is p_n, False)
                        product(pe, bank[:], w_ih[:, (3 + k) * P:(4 + k) * P], nm[:, :], False, True).then_inc(done, 1)
                if s.live():
                    pe.wait_ge(right_ready, s.t + 1)
                    need(pe, x_updated, s.t - 1)
                    for g in range(G):
                        for a in range(2):
                            m0 = g * N + a * P
                            last = pe.matmul(p_dist[:, g, a, :], q[0:KD, m0:m0 + P], right[:, g * N:(g + 1) * N], start=True, stop=True)
                    last.then_inc(dist_done, 1)
            run_steps(pe, body, 2)


HEADS = 4
HD = 64
DI = HEADS * HD
DS = 64
XBC = DI + 2 * DS
TAPS = 4
HALF_DT, CUM, OFF = 0, 1, 2


def dt_phase(nc, w, X, XT, table, cum_dram, eye):
    with ExitStack() as ctx:
        ph = Phase(nc, ctx, "t_")
        sb, sem = ph.sb, ph.sem
        w_dt = sb("w_dt", [P, HEADS])
        cols = sb("cols", [HEADS, 4])
        b_lin = sb("b_lin", [P, P])
        minus_half = sb("minus_half", [P, T])
        ones = sb("ones", [HEADS, P])
        stats, mv = sb("stats", [P, T, 6]), sb("mv", [P, T, 2])
        veps, rstd = sb("veps", [P, T]), sb("rstd", [P, T])
        xn = sb("xn", [P, T, P])
        u, absu, e, l, dt, dA = (sb(s, [HEADS, S]) for s in ("u", "absu", "e", "l", "dt", "dA"))
        rows = sb("rows", [P, 2, S])
        p_xT = ph.psum("p_xT", [P, S])
        p_dt = ph.psum("p_dt", [P, S])
        p_tab = ph.psum("p_tab", [P, T, P])
        loaded, consts = sem("loaded"), sem("consts")
        stats_done, mv_done, veps_done, rstd_done = sem("stats_done"), sem("mv_done"), sem("veps_done"), sem("rstd_done")
        xn_ready, xT_done, XT_ready, biased = sem("xn_ready"), sem("xT_done"), sem("XT_ready"), sem("biased")
        dt_done, u_ready, e_ready, l_ready, dt_ready, dA_ready = (
            sem(s) for s in ("dt_done", "u_ready", "e_ready", "l_ready", "dt_ready", "dA_ready"))
        scanned, rows_ready, rows_turned, table_ready = (sem(s) for s in ("scanned", "rows_ready", "rows_turned", "table_ready"))
        written = [sem(f"written{p}") for p in range(2)]
        block = ctx.enter_context(nc.Block())

        @block.sync
        def _(sp):
            sp.dma_start(w_dt[:], w["W_dt"]).then_inc(loaded, 16)
            sp.dma_start(cols[:, 0:1], column(w["dt_bias"])).then_inc(loaded, 16)
            sp.dma_start(cols[:, 1:2], column(w["A_log"])).then_inc(loaded, 16)
            sp.dma_start(b_lin[:], spread(w["b_lin"])).then_inc(loaded, 16)

            def body(s):
                b = s.back(1)
                if b.live():
                    hold(sp, rows_ready, 2 * (b.t + 1))
                    sp.dma_start(cum_dram[:, bass.ts(b.t, S)], rows[32:32 + HEADS, b.p]).then_inc(written[b.p], 16)
            run_steps(sp, body, 1)
            for p in range(2):
                sp.wait_ge(written[p], 16 * STEPS // 2)

        @block.gpsimd
        def _(pool):
            pool.memset(minus_half[:], -0.5).then_inc(consts, 1)
            pool.memset(ones[:], 1.0).then_inc(consts, 1)
            pool.memset(rows[:], 0.0).then_inc(consts, 1)
            pool.wait_ge(consts, 3)
            pool.wait_ge(loaded, 16 * 4)

            def body(s):
                if s.live():
                    pool.wait_ge(mv_done, T * (s.t + 1))
                    hold(pool, xn_ready, T * s.t)
                    pool.tensor_scalar(veps[:], mv[:, :, 1], EPS, None, ALU.add).then_inc(veps_done, 1)
                    pool.wait_ge(veps_done, s.t + 1)
                    pool.tensor_tensor(rstd[:], veps[:], minus_half[:], ALU.pow).then_inc(rstd_done, 1)
                    hold(pool, xn_ready, T * (s.t + 1))
                    xt = X[:, bass.ts(s.t, T), :]
                    bb = b_lin[:].rearrange("p (a d) -> p a d", a=1).broadcast_to([P, T, P])
                    pool.tensor_tensor(xt, xt, bb, ALU.add).then_inc(biased, 1)
            run_steps(pool, body, 0)

        @block.scalar
        def _(act):
            act.preload_act_table_set("natural_log_exp_and_others")
            act.wait_ge(loaded, 16 * 4)
            act.activation(cols[:, 2:3], cols[:, 1:2], ACT.Exp).then_inc(consts, 1)
            act.wait_ge(consts, 4)

            def body(s):
                b, c = s.back(1), s.back(2)
                if s.live():
                    hold(act, xT_done, s.t + 1)
                    act.activation(XT[:, bass.ts(s.t, S)], p_xT[:], ACT.Copy).then_inc(XT_ready, 1)
                if b.live():
                    act.wait_ge(u_ready, b.t + 1)
                    act.activation(absu[:], u[:], ACT.Abs).then_inc(e_ready, 1)
                    act.wait_ge(e_ready, 2 * b.t + 1)
                    act.activation(e[:], absu[:], ACT.Exp, scale=-1.0).then_inc(e_ready, 1)
                    act.wait_ge(e_ready, 2 * (b.t + 1))
                    need(act, dt_ready, 2 * b.t)
                    act.activation(l[:], e[:], ACT.Ln, bias=1.0).then_inc(l_ready, 1)
                if c.live():
                    hold(act, rows_turned, c.t + 1)
                    groups = p_tab[:, :, 0:96].rearrange("p t (g r) -> p t g r", g=3)[:, :, :, 0:HEADS]
                    act.activation(table[:, bass.ts(c.t, T)], groups, ACT.Copy).then_inc(table_ready, 1)
            run_steps(act, body, 2)

        @block.vector
        def _(dve):
            dve.wait_ge(consts, 4)
            dve.tensor_scalar(cols[:, 3:4], cols[:, 2:3], -1.0, None, ALU.mult).then_inc(consts, 1)
            dve.wait_ge(consts, 5)

            def body(s):
                b = s.back(1)
                if s.live():
                    layer_norm_stats(dve, X, s, stats, mv, stats_done, mv_done)
                    dve.wait_ge(rstd_done, s.t + 1)
                    need(dve, xT_done, s.t)
                    layer_norm_apply(dve, X, s, xn, mv, rstd, xn_ready)
                if b.live():
                    dve.wait_ge(dt_done, b.t + 1)
                    need(dve, dt_ready, 2 * b.t)
                    dve.tensor_scalar(u[:], p_dt[0:HEADS, :], cols[:, 0:1], None, ALU.add).then_inc(u_ready, 1)
                    dve.wait_ge(u_ready, b.t + 1)
                    dve.wait_ge(l_ready, b.t + 1)
                    dve.scalar_tensor_tensor(out=dt[:], in0=u[:], scalar=0.0, in1=l[:], op0=ALU.max, op1=ALU.add).then_inc(dt_ready, 1)
                    need(dve, rows_turned, b.t - 1)
                    need(dve, written[b.p], 16 * b.u)
                    hold(dve, dt_ready, 2 * b.t + 1)
                    dve.tensor_scalar(rows[0:HEADS, b.p], dt[:], 0.5, None, ALU.mult).then_inc(dt_ready, 1)
                    dve.tensor_scalar(dA[:], dt[:], cols[:, 3:4], None, ALU.mult).then_inc(dA_ready, 1)
                    hold(dve, dA_ready, b.t + 1)
                    for j in range(T):
                        dve.tensor_tensor_scan(out=rows[32:32 + HEADS, b.p, j * P:(j + 1) * P], data0=ones[:],
                                               data1=dA[:, j * P:(j + 1) * P], initial=0.0, op0=ALU.mult, op1=ALU.add).then_inc(scanned, 1)
                    hold(dve, scanned, T * (b.t + 1))
                    for g in range(G):
                        cum = rows[32:32 + HEADS, b.p, g * N:g * N + P]
                        dve.tensor_scalar(rows[64:64 + HEADS, b.p, g * N:g * N + P], cum, cum[:, P - 1:P], -1.0,
                                          ALU.subtract, ALU.mult).then_inc(rows_ready, 1)
            run_steps(dve, body, 1)

        @block.tensor
        def _(pe):
            pe.wait_ge(loaded, 16 * 4)

            def body(s):
                b, c = s.back(1), s.back(2)
                if s.live():
                    pe.wait_ge(xn_ready, T * (s.t + 1))
                    need(pe, XT_ready, s.t)
                    for j in range(T):
                        last = pe.transpose(p_xT[:, j * P:(j + 1) * P], xn[:, j, :], eye[:])
                    last.then_inc(xT_done, 1)
                if c.live():
                    pe.wait_ge(rows_ready, 2 * (c.t + 1))
                    need(pe, table_ready, c.t)
                    for j in range(T):
                        last = pe.transpose(p_tab[:, j, 0:96], rows[0:96, c.p, j * P:(j + 1) * P], eye[0:96, 0:96])
                    last.then_inc(rows_turned, 1)
                if s.live():
                    need(pe, u_ready, s.t)
                    hold(pe, XT_ready, s.t + 1)
                    pe.matmul(p_dt[0:HEADS, :], w_dt[:], XT[:, bass.ts(s.t, S)], start=True, stop=True).then_inc(dt_done, 1)
            run_steps(pe, body, 2)


def mamba_phase(nc, w, X, XT, table, cum_dram, eye):
    NB = 3 * P
    with ExitStack() as ctx:
        ph = Phase(nc, ctx, "m_")
        sb, sem = ph.sb, ph.sem
        w_in = sb("w_in", [P, DI + XBC])
        w_out = sb("w_out", [P, 2, P])
        w_outT = sb("w_outT", [P, DI])
        w_lin = sb("w_lin", [P, P])
        vecs = sb("vecs", [P, 3 * TAPS + 3 + 2])
        half_D = sb("half_D", [P, HEADS])
        mask = sb("mask", [P, NB])
        minus_half = sb("minus_half", [P, T])
        xT = sb("xT", [P, 2, S])
        cum = sb("cum", [P, 2, HEADS, S])
        tab = sb("tab", [P, 2, T, 3, HEADS])
        xp = sb("xp", [P, 3, G, TAPS - 1 + N])
        c_ = sb("c", [P, 3, G, N])
        xs = sb("xs", [P, 3, S])
        Bt, Ct = sb("Bt", [DS, S]), sb("Ct", [DS, S])
        xh = sb("xh", [P, T, DI])
        xdt = sb("xdt", [P, 2, T, DI])
        xD = sb("xD", [P, 2, T, DI])
        Gm = sb("Gm", [P, G, NB])
        dec = sb("dec", [P, G, HEADS, NB])
        W = sb("W", [P, 2, G, HEADS, NB])
        zz = sb("zz", [P, 2, T, DI])
        y1 = sb("y1", [P, T, DI])
        y2 = sb("y2", [P, 2, T, DI])
        sq = sb("sq", [P, T, DI])
        ss, ms, rs = sb("ss", [P, T]), sb("ms", [P, T]), sb("rs", [P, T])
        half_rs = sb("half_rs", [P, 2, T])
        yT = sb("yT", [P, 2, S])
        banks = [ph.psum(f"bank{k}", [P, S]) for k in range(1)]
        p_x0 = banks[0]
        p_x12 = ph.psum("p_x12", [P, 2, S])
        p_z = ph.psum("p_z", [P, T, DI])
        p_xh = ph.psum("p_xh", [P, T, DI])
        p_o = ph.psum("p_o", [P, S])
        p_yT = p_xh[:].rearrange("p t d -> p (t d)").rearrange("p (c n) -> p c n", c=2)
        p_Y = p_x12[:].rearrange("p a b -> p (a b)").rearrange("p (t d) -> p t d", t=T)
        p_G = (p_o[:, 0:NB], p_x0[:, 0:NB])
        p_x = (p_x0[:], p_x12[:, 0, :], p_x12[:, 1, :])

        names = ("loaded consts w2_done w2_ready tab_ready x_done x_taken taps silu_in tanh_ready silu_ready z_done tz_ready "
                 "zz_ready xh_done xh_ready xdt_ready xD_ready G_done Gm_ready diag_ready off_ready dec_ready W_ready Y_done "
                 "y1_ready y2_ready ss_ready ms_ready rs_ready hrs_ready yT_done yT_ready out_done x_updated")
        q = {s: sem(s) for s in names.split()}
        arrived = [sem(f"arrived{p}") for p in range(2)]
        block = ctx.enter_context(nc.Block())

        @block.sync
        def _(sp):
            for dst, src in ((w_in[:], w["W_in_zx"]), (w_outT[:], w["W_outT"]), (w_lin[:], w["W_lin"]), (vecs[:], w["mamba_vecs"]),
                             (half_D[:], spread(w["D"])), (mask[:], w["mask"])):
                sp.dma_start(dst, src).then_inc(q["loaded"], 16)

            def body(s):
                if s.live():
                    hold(sp, q["z_done"], s.t - 1)
                    hold(sp, q["diag_ready"], 16 * (s.t - 1))
                    hold(sp, q["off_ready"], 8 * (s.t - 1))
                    sp.dma_start(xT[:, s.p], XT[:, bass.ts(s.t, S)]).then_inc(arrived[s.p], 16)
                    src = cum_dram[:, bass.ts(s.t, S)]
                    sp.dma_start(cum[:, s.p], src.partition_broadcast(P)).then_inc(arrived[s.p], 16)
            run_steps(sp, body, 1)

        @block.gpsimd
        def _(pool):
            pool.memset(minus_half[:], -0.5).then_inc(q["consts"], 1)
            pool.memset(xp[:], 0.0).then_inc(q["consts"], 1)
            pool.wait_ge(q["loaded"], 16 * 6)
            pool.tensor_scalar(half_D[:], half_D[:], 0.5, None, ALU.mult).then_inc(q["consts"], 1)
            pool.wait_ge(q["consts"], 3)

            def body(s):
                m, y = s.back(1), s.back(3)
                if s.live():
                    hold(pool, q["dec_ready"], s.t - 1)
                    hold(pool, q["xdt_ready"], s.t - 1)
                    pool.tensor_copy(tab[:, s.p], table[:, bass.ts(s.t, T)]).then_inc(q["tab_ready"], 1)
                if y.live():
                    need(pool, q["zz_ready"], y.t + 1)
                    need(pool, q["yT_done"], y.t - 1)
                    need(pool, q["y1_ready"], y.t + 1)
                    pool.tensor_tensor(y2[:, y.p], y1[:], zz[:, y.p], ALU.mult).then_inc(q["y2_ready"], 1)
                if m.live():
                    need(pool, q["Y_done"], m.t - 1)
                    need(pool, q["tab_ready"], m.t + 1)
                    need(pool, q["xh_ready"], m.t + 1)
                    xh4 = xh[:].rearrange("p t (h d) -> p t h d", h=HEADS)
                    half_dt = tab[:, m.p, :, HALF_DT, :].rearrange("p t (h a) -> p t h a", a=1).broadcast_to([P, T, HEADS, HD])
                    pool.tensor_tensor(xdt[:, m.p].rearrange("p t (h d) -> p t h d", h=HEADS), xh4, half_dt, ALU.mult).then_inc(q["xdt_ready"], 1)
                    need(pool, q["y1_ready"], m.t - 1)
                    for j in range(T):
                        hD = half_D[:].rearrange("p (h a) -> p h a", a=1).broadcast_to([P, HEADS, HD])
                        pool.tensor_tensor(xD[:, m.p, j].rearrange("p (h d) -> p h d", h=HEADS), xh4[:, j], hD, ALU.mult).then_inc(q["xD_ready"], 1)
                    need(pool, q["dec_ready"], m.t + 1)
                    need(pool, q["Gm_ready"], 2 * (m.t + 1))
                    g1 = Gm[:, 1].rearrange("p (a n) -> p a n", a=1).broadcast_to([P, HEADS, NB])
                    pool.tensor_tensor(W[:, m.p, 1], dec[:, 1], g1, ALU.mult).then_inc(q["W_ready"], 1)
                if y.live():
                    need(pool, q["rs_ready"], y.t)
                    hold(pool, q["ss_ready"], T * (y.t + 1))
                    pool.tensor_scalar(ms[:], ss[:], 1.0 / (4 * DI), EPS, ALU.mult, ALU.add).then_inc(q["ms_ready"], 1)
                    need(pool, q["hrs_ready"], y.t)
                    need(pool, q["ms_ready"], y.t + 1)
                    pool.tensor_tensor(rs[:], ms[:], minus_half[:], ALU.pow).then_inc(q["rs_ready"], 1)
                    need(pool, q["x_updated"], T * (y.t - 1))
                    hold(pool, q["rs_ready"], y.t + 1)
                    pool.tensor_scalar(half_rs[:, y.p], rs[:], 0.5, None, ALU.mult).then_inc(q["hrs_ready"], 1)
            run_steps(pool, body, 3)

        @block.scalar
        def _(act):
            act.preload_act_table(ACT.Exp)
            act.wait_ge(q["loaded"], 16 * 6)
            act.wait_ge(q["consts"], 3)
            act.wait_ge(q["w2_done"], 1)
            for k in range(2):
                act.activation(w_out[:, k, :], p_z[:, k, 0:P], ACT.Copy, scale=vecs[:, 15 + k:16 + k]).then_inc(q["w2_ready"], 1)

            def body(s):
                m, y, o = s.back(1), s.back(3), s.back(4)
                if o.live():
                    need(act, q["out_done"], o.t)
                    need(act, q["yT_done"], o.t + 1)
                    act.activation(yT[:], p_yT, ACT.Copy).then_inc(q["yT_ready"], 1)
                if s.live():
                    need(act, q["silu_ready"], 3 * s.t)
                    for k in range(3):
                        act.wait_ge(q["x_done"], 3 * s.t + k + 1)
                        px = p_x[k].rearrange("p (g n) -> p g n", g=G)
                        act.activation(xp[:, k, :, TAPS - 1:], px, ACT.Copy).then_inc(q["x_taken"], 1)
                        last_tap = k * TAPS + TAPS - 1
                        act.activation(c_[:, k], px, ACT.Identity, scale=vecs[:, last_tap:last_tap + 1],
                                       bias=vecs[:, 3 * TAPS + k:3 * TAPS + k + 1]).then_inc(q["x_taken"], 1)
                if m.live():
                    act.wait_ge(arrived[m.p], 32 * (m.u + 1))
                    need(act, q["W_ready"], 2 * m.t)
                    act.wait_ge(q["tab_ready"], m.t + 1)
                    for g in range(G):
                        for h in range(HEADS):
                            act.activation(dec[:, g, h, P:2 * P], cum[:, m.p, h, g * N + P:(g + 1) * N], ACT.Exp,
                                           bias=tab[:, m.p, 2 * g, OFF, h:h + 1]).then_inc(q["off_ready"], 1)
                    act.wait_ge(q["diag_ready"], 16 * (m.t + 1))
                    diag = dec[:].rearrange("p g h (b n) -> p (g h) b n", b=3)[:, :, 0:3:2, :]
                    act.activation(diag, diag, ACT.Exp).then_inc(q["dec_ready"], 1)
                    need(act, q["z_done"], m.t + 1)
                    need(act, q["y2_ready"], m.t - 1)
                    act.activation(zz[:, m.p], p_z[:], ACT.Tanh, scale=0.5).then_inc(q["tz_ready"], 1)
                    need(act, q["xdt_ready"], m.t)
                    need(act, q["xD_ready"], T * m.t)
                    need(act, q["xh_done"], m.t + 1)
                    act.activation(xh[:], p_xh[:], ACT.Copy).then_inc(q["xh_ready"], 1)
                if y.live():
                    need(act, q["ms_ready"], y.t)
                    need(act, q["y2_ready"], y.t + 1)
                    for j in range(T):
                        act.activation(sq[:, j], y2[:, y.p, j], ACT.Square, accum_out=ss[:, j:j + 1]).then_inc(q["ss_ready"], 1)
                if s.live():
                    act.wait_ge(q["taps"], 9 * (s.t + 1))
                    act.activation(xs[:], c_[:].rearrange("p k g n -> p k (g n)"), ACT.Tanh, scale=0.5).then_inc(q["tanh_ready"], 1)
            run_steps(act, body, 4)

        @block.vector
        def _(dve):
            dve.wait_ge(q["loaded"], 16 * 6)
            dve.wait_ge(q["consts"], 3)

            def body(s):
                m, y, o = s.back(1), s.back(3), s.back(4)
                if y.live():
                    need(dve, q["xD_ready"], T * (y.t + 1))
                    need(dve, q["y2_ready"], y.t)
                    need(dve, q["Y_done"], y.t + 1)
                    dve.tensor_tensor(y1[:], p_Y, xD[:, y.p], ALU.add).then_inc(q["y1_ready"], 1)
                if m.live():
                    dve.wait_ge(arrived[m.p], 32 * (m.u + 1))
                    need(dve, q["W_ready"], 2 * m.t)
                    dve.wait_ge(q["tab_ready"], m.t + 1)
                    for g in range(G):
                        for b in range(2):
                            for h in range(HEADS):
                                l0 = g * N + b * P
                                dve.tensor_scalar(dec[:, g, h, 2 * b * P:(2 * b + 1) * P], cum[:, m.p, h, l0:l0 + P],
                                                  tab[:, m.p, 2 * g + b, CUM, h:h + 1], 0.0, ALU.subtract, ALU.min).then_inc(q["diag_ready"], 1)
                if o.live():
                    need(dve, q["hrs_ready"], o.t + 1)
                    dve.wait_ge(q["out_done"], o.t + 1)
                    for j in range(T):
                        xt = X[:, o.t * T + j, :]
                        dve.scalar_tensor_tensor(out=xt, in0=p_o[:, j * P:(j + 1) * P], scalar=half_rs[:, o.p, j:j + 1], in1=xt,
                                                 op0=ALU.mult, op1=ALU.add).then_inc(q["x_updated"], 1)
                if s.live():
                    for n, tap in enumerate(range(TAPS - 1)):
                        for k in range(3):
                            if n == 0:
                                dve.wait_ge(q["x_taken"], 6 * s.t + 2 * (k + 1))
                            else:
                                dve.wait_ge(q["taps"], 9 * s.t + 3 * (n - 1) + k + 1)
                            dve.scalar_tensor_tensor(out=c_[:, k], in0=xp[:, k, :, tap:tap + N], scalar=vecs[:, k * TAPS + tap:k * TAPS + tap + 1],
                                                     in1=c_[:, k], op0=ALU.mult, op1=ALU.add).then_inc(q["taps"], 1)
                if m.live():
                    dve.wait_ge(q["tz_ready"], m.t + 1)
                    dve.scalar_tensor_tensor(out=zz[:, m.p].rearrange("p t d -> p (t d)"), in0=zz[:, m.p].rearrange("p t d -> p (t d)"), scalar=1.0,
                                             in1=p_z[:].rearrange("p t d -> p (t d)"), op0=ALU.add, op1=ALU.mult).then_inc(q["zz_ready"], 1)
                    need(dve, q["W_ready"], 2 * m.t)
                    dve.wait_ge(q["G_done"], m.t + 1)
                    for g in range(G):
                        dve.scalar_tensor_tensor(out=Gm[:, g], in0=p_G[g], scalar=0.25, in1=mask[:], op0=ALU.mult, op1=ALU.mult).then_inc(q["Gm_ready"], 1)
                    dve.wait_ge(q["dec_ready"], m.t + 1)
                    need(dve, q["Y_done"], m.t - 1)
                    dve.wait_ge(q["Gm_ready"], 2 * m.t + 1)
                    g0 = Gm[:, 0].rearrange("p (a n) -> p a n", a=1).broadcast_to([P, HEADS, NB])
                    dve.tensor_tensor(W[:, m.p, 0], dec[:, 0], g0, ALU.mult).then_inc(q["W_ready"], 1)
                if s.live():
                    need(dve, q["xh_done"], s.t)
                    need(dve, q["G_done"], s.t)
                    dve.wait_ge(q["tanh_ready"], s.t + 1)
                    cc = c_[:].rearrange("p k g n -> p k (g n)")
                    dve.scalar_tensor_tensor(out=Bt[:], in0=xs[0:DS, 2, :], scalar=1.0, in1=cc[0:DS, 2, :], op0=ALU.add, op1=ALU.mult).then_inc(q["silu_ready"], 1)
                    dve.scalar_tensor_tensor(out=Ct[:], in0=xs[DS:P, 2, :], scalar=1.0, in1=cc[DS:P, 2, :], op0=ALU.add, op1=ALU.mult).then_inc(q["silu_ready"], 1)
                    dve.scalar_tensor_tensor(out=xs[:, 0:2, :], in0=xs[:, 0:2, :], scalar=1.0, in1=cc[:, 0:2, :], op0=ALU.add, op1=ALU.mult).then_inc(q["silu_ready"], 1)
            run_steps(dve, body, 4)

        @block.tensor
        def _(pe):
            pe.wait_ge(q["loaded"], 16 * 6)
            for k in range(2):
                last = pe.matmul(p_z[:, k, 0:P], w_outT[:, k * P:(k + 1) * P], w_lin[:], start=True, stop=True)
            last.then_inc(q["w2_done"], 1)
            pe.wait_ge(q["w2_ready"], 2)

            def body(s):
                m, v, y, o = s.back(1), s.back(2), s.back(3), s.back(4)
                if o.live():
                    need(pe, q["xh_ready"], o.t + 3) if v.live() else None
                    need(pe, q["yT_ready"], o.t)
                    need(pe, q["y2_ready"], o.t + 1)
                    for k in range(2):
                        for j in range(T):
                            last = pe.transpose(p_yT[:, k, j * P:(j + 1) * P], y2[:, o.p, j, k * P:(k + 1) * P], eye[:])
                    last.then_inc(q["yT_done"], 1)
                if s.live():
                    need(pe, q["Gm_ready"], 2 * (s.t - 1))
                    need(pe, q["y1_ready"], s.t - 2)
                    need(pe, q["x_taken"], 6 * s.t)
                    pe.wait_ge(arrived[s.p], 32 * (s.u + 1))
                    for k in range(3):
                        pe.matmul(p_x[k], w_in[:, DI + k * P:DI + (k + 1) * P], xT[:, s.p], start=True, stop=True).then_inc(q["x_done"], 1)
                if o.live():
                    need(pe, q["Gm_ready"], 2 * (o.t + 3)) if v.live() else None
                    if not m.live():
                        need(pe, q["x_updated"], T * o.t)
                    pe.wait_ge(q["yT_ready"], o.t + 1)
                    for j in range(T):
                        for k in range(2):
                            last = pe.matmul(p_o[:, j * P:(j + 1) * P], yT[:, k, j * P:(j + 1) * P], w_out[:, k, :], start=k == 0, stop=k == 1)
                    last.then_inc(q["out_done"], 1)
                if m.live():
                    need(pe, q["zz_ready"], m.t)
                    for j in range(T):
                        last = pe.matmul(p_z[:, j, :], xT[:, m.p, j * P:(j + 1) * P], w_in[:, 0:DI], start=True, stop=True)
                    last.then_inc(q["z_done"], 1)
                    need(pe, q["yT_ready"], m.t - 2)
                    pe.wait_ge(q["silu_ready"], 3 * (m.t + 1))
                    for j in range(T):
                        for k in range(2):
                            last = pe.transpose(p_xh[:, j, k * P:(k + 1) * P], xs[:, k, j * P:(j + 1) * P], eye[:])
                    last.then_inc(q["xh_done"], 1)
                    need(pe, q["x_updated"], T * (m.t - 2))
                    if s.live():
                        pe.wait_ge(q["x_taken"], 6 * s.t + 2)
                    for g in range(G):
                        l0 = g * N
                        pe.matmul(p_G[g][:, 0:N], Bt[:, l0:l0 + P], Ct[:, l0:l0 + N], start=True, stop=True)
                        last = pe.matmul(p_G[g][:, N:NB], Bt[:, l0 + P:l0 + N], Ct[:, l0 + P:l0 + N], start=True, stop=True)
                    last.then_inc(q["G_done"], 1)
                if v.live():
                    if s.live():
                        pe.wait_ge(q["x_taken"], 6 * (s.t + 1))
                    need(pe, q["y1_ready"], v.t)
                    pe.wait_ge(q["W_ready"], 2 * (v.t + 1))
                    pe.wait_ge(q["xdt_ready"], v.t + 1)
                    for g in range(G):
                        for h in range(HEADS):
                            hs = slice(h * HD, (h + 1) * HD)
                            Wh = W[:, v.p, g, h]
                            pe.matmul(p_Y[:, 2 * g, hs], Wh[:, 0:P], xdt[:, v.p, 2 * g, hs], start=True, stop=True)
                            pe.matmul(p_Y[:, 2 * g + 1, hs], Wh[:, P:2 * P], xdt[:, v.p, 2 * g, hs], start=True, stop=False)
                            last = pe.matmul(p_Y[:, 2 * g + 1, hs], Wh[:, 2 * P:NB], xdt[:, v.p, 2 * g + 1, hs], start=False, stop=True)
                    last.then_inc(q["Y_done"], 1)
            run_steps(pe, body, 4)


def graph_phase(nc, w, X, adj_dram, adjT_dram, eye):
    with ExitStack() as ctx:
        ph = Phase(nc, ctx, "c_")
        sb, sem = ph.sb, ph.sem
        weight = sb("weight", [P, P])
        bias = sb("bias", [P, P])
        minus_half = sb("minus_half", [P, T])
        adj = sb("adj", [P, 2, T, N])
        adjT = sb("adjT", [P, 2, G, 2, N])
        stats, mv = sb("stats", [P, T, 6]), sb("mv", [P, T, 2])
        veps, rstd = sb("veps", [P, T]), sb("rstd", [P, T])
        xn = sb("xn", [P, T, P])
        xT = sb("xT", [P, S])
        deg, deps = sb("deg", [P, T]), sb("deps", [P, T])
        dinv = sb("dinv", [P, 2, T])
        sup = sb("sup", [P, 2, T, P])
        p_xT = ph.psum("p_xT", [P, S])
        p_sup = ph.psum("p_sup", [P, S])
        p_agg = ph.psum("p_agg", [P, S])
        loaded, consts = sem("loaded"), sem("consts")
        stats_done, mv_done, veps_done, rstd_done = sem("stats_done"), sem("mv_done"), sem("veps_done"), sem("rstd_done")
        xn_ready, xT_done, xT_ready, biased = sem("xn_ready"), sem("xT_done"), sem("xT_ready"), sem("biased")
        deg_ready, deps_ready, dinv_ready = sem("deg_ready"), sem("deps_ready"), sem("dinv_ready")
        sup_done, sup_ready, agg_done, x_updated = (sem(s) for s in ("sup_done", "sup_ready", "agg_done", "x_updated"))
        adj_in = [sem(f"adj_in{p}") for p in range(2)]
        adjT_in = [sem(f"adjT_in{p}") for p in range(2)]
        block = ctx.enter_context(nc.Block())

        @block.sync
        def _(sp):
            sp.dma_start(weight[:], w["gcn_w"]).then_inc(loaded, 16)
            sp.dma_start(bias[:], spread(w["gcn_b"])).then_inc(loaded, 16)

            def body(s):
                if s.live():
                    hold(sp, deg_ready, s.t - 1)
                    sp.dma_start(adj[:, s.p], adj_dram[bass.ts(s.t, G)].rearrange("g (a n) m -> n (g a) m", n=P)).then_inc(adj_in[s.p], 16)
                    hold(sp, agg_done, s.t - 1)
                    sp.dma_start(adjT[:, s.p], adjT_dram[bass.ts(s.t, G)].rearrange("g (a m) n -> m g a n", m=P)).then_inc(adjT_in[s.p], 16)
            run_steps(sp, body, 1)

        @block.gpsimd
        def _(pool):
            pool.memset(minus_half[:], -0.5).then_inc(consts, 1)
            pool.wait_ge(consts, 1)
            pool.wait_ge(loaded, 32)

            def body(s):
                b = s.back(1)
                if s.live():
                    pool.wait_ge(mv_done, T * (s.t + 1))
                    hold(pool, xn_ready, T * s.t)
                    pool.tensor_scalar(veps[:], mv[:, :, 1], EPS, None, ALU.add).then_inc(veps_done, 1)
                    pool.wait_ge(veps_done, s.t + 1)
                    pool.tensor_tensor(rstd[:], veps[:], minus_half[:], ALU.pow).then_inc(rstd_done, 1)
                if b.live():
                    need(pool, dinv_ready, b.t)
                    hold(pool, deg_ready, b.t + 1)
                    pool.tensor_scalar(deps[:], deg[:], EPS, None, ALU.add).then_inc(deps_ready, 1)
                    need(pool, x_updated, T * (b.t - 1))
                    need(pool, deps_ready, b.t + 1)
                    pool.tensor_tensor(dinv[:, b.p], deps[:], minus_half[:], ALU.pow).then_inc(dinv_ready, 1)
                if s.live():
                    hold(pool, xn_ready, T * (s.t + 1))
                    xt = X[:, bass.ts(s.t, T), :]
                    bb = bias[:].rearrange("p (a d) -> p a d", a=1).broadcast_to([P, T, P])
                    pool.tensor_tensor(xt, xt, bb, ALU.add).then_inc(biased, 1)
            run_steps(pool, body, 1)

        @block.scalar
        def _(act):
            act.preload_act_table(ACT.Exp)

            def body(s):
                b = s.back(1)
                if b.live():
                    act.wait_ge(dinv_ready, b.t + 1)
                    need(act, agg_done, b.t - 1)
                    act.wait_ge(sup_done, b.t + 1)
                    for j in range(T):
                        act.activation(sup[:, b.p, j], p_sup[:, j * P:(j + 1) * P], ACT.Copy, scale=dinv[:, b.p, j:j + 1]).then_inc(sup_ready, 1)
                if s.live():
                    need(act, sup_done, s.t)
                    need(act, xT_done, s.t + 1)
                    act.activation(xT[:], p_xT[:], ACT.Copy).then_inc(xT_ready, 1)
            run_steps(act, body, 1)

        @block.vector
        def _(dve):
            def body(s):
                b, c = s.back(1), s.back(2)
                if b.live():
                    need(dve, deps_ready, b.t)
                    dve.wait_ge(adj_in[b.p], 16 * (b.u + 1))
                    dve.tensor_reduce(deg[:], adj[:, b.p], AX.X, ALU.add).then_inc(deg_ready, 1)
                if s.live():
                    layer_norm_stats(dve, X, s, stats, mv, stats_done, mv_done)
                    dve.wait_ge(rstd_done, s.t + 1)
                    need(dve, xT_done, s.t)
                    layer_norm_apply(dve, X, s, xn, mv, rstd, xn_ready)
                if c.live():
                    need(dve, biased, c.t + 1)
                    need(dve, agg_done, c.t + 1)
                    for j in range(T):
                        xt = X[:, c.t * T + j, :]
                        dve.scalar_tensor_tensor(out=xt, in0=p_agg[:, j * P:(j + 1) * P], scalar=dinv[:, c.p, j:j + 1], in1=xt,
                                                 op0=ALU.mult, op1=ALU.add).then_inc(x_updated, 1)
            run_steps(dve, body, 2)

        @block.tensor
        def _(pe):
            pe.wait_ge(loaded, 32)

            def body(s):
                b, c = s.back(1), s.back(2)
                if c.live():
                    need(pe, x_updated, T * c.t)
                    need(pe, adjT_in[c.p], 16 * (c.u + 1))
                    need(pe, sup_ready, T * (c.t + 1))
                    for j in range(T):
                        for a in range(2):
                            n0 = (j % 2) * P
                            last = pe.matmul(p_agg[:, j * P:(j + 1) * P], adjT[:, c.p, j // 2, a, n0:n0 + P], sup[:, c.p, 2 * (j // 2) + a], start=a == 0, stop=a == 1)
                    last.then_inc(agg_done, 1)
                if b.live():
                    need(pe, sup_ready, T * b.t)
                    need(pe, xT_ready, b.t + 1)
                    for j in range(T):
                        last = pe.matmul(p_sup[:, j * P:(j + 1) * P], xT[:, j * P:(j + 1) * P], weight[:], start=True, stop=True)
                    last.then_inc(sup_done, 1)
                if s.live():
                    need(pe, xT_ready, s.t)
                    need(pe, xn_ready, T * (s.t + 1))
                    for j in range(T):
                        last = pe.transpose(p_xT[:, j * P:(j + 1) * P], xn[:, j, :], eye[:])
                    last.then_inc(xT_done, 1)
            run_steps(pe, body, 2)


BF16 = mybir.dt.bfloat16
I32 = mybir.dt.int32
EX = 8
TOPK = 2
H = 341
HP = H + 1
CH = [(0, P), (P, P), (2 * P, H - 2 * P)]
SLOTS = TOPK * NT + EX
NO_ROW = 1 << 20


def route_phase(nc, w, X, gate, gather_rows, scatter_rows, tile_expert, xn_dram, eye):
    with ExitStack() as ctx:
        ph = Phase(nc, ctx, "r_")
        sb, sem = ph.sb, ph.sem
        router = sb("router", [P, EX])
        rev = sb("rev", [P, EX])
        before = sb("before", [P, P])
        ones = sb("ones", [P, P])
        tile_no = sb("tile_no", [P, NT])
        part_no = sb("part_no", [P, 1])
        slot_iota = sb("slot_iota", [P, SLOTS])
        slot_bf = sb("slot_bf", [P, SLOTS], BF16)
        row_bf = sb("row_bf", [P, P], BF16)
        minus_half = sb("minus_half", [P, T])
        stats, mv = sb("stats", [P, T, 6]), sb("mv", [P, T, 2])
        veps, rstd = sb("veps", [P, T]), sb("rstd", [P, T])
        xn = sb("xn", [P, 2, T, P])
        xT = sb("xT", [P, S])
        full = [P, NT, EX]
        logits, hot1, hot2, work, work2, both = (sb(s, full) for s in ("logits", "hot1", "hot2", "work", "work2", "both"))
        m1, m2, f1, z, rz, e2, p2, den, gsum = (sb(s, [P, NT]) for s in ("m1", "m2", "f1", "z", "rz", "e2", "p2", "den", "gsum"))
        total = sb("total", [P, EX, NT])
        upto = sb("upto", [P, EX, NT])
        pos = sb("pos", [P, NT, EX])
        padded = sb("padded", [P, EX])
        padded_i = sb("padded_i", [P, EX], I32)
        ends = sb("ends", [P, EX])
        dest = sb("dest", [P, TOPK, NT])
        dest_i, tile_i = sb("dest_i", [P, TOPK, NT], I32), sb("tile_i", [P, TOPK, NT], I32)
        dest_tile, dest_row = sb("dest_tile", [P, TOPK, NT]), sb("dest_row", [P, TOPK, NT])
        tile_k = sb("tile_k", [P, TOPK, NT])
        B = sb("B", [P, 2, 8, P], BF16)
        A = sb("A", [P, 2, 8, 2, SLOTS], BF16)
        hi_no, lo_no = sb("hi_no", [P, SLOTS]), sb("lo_no", [P, SLOTS])
        row_f, off_f, exp_f = sb("row_f", [P, SLOTS]), sb("off_f", [P, SLOTS]), sb("exp_f", [P, SLOTS])
        p_xT = ph.psum("p_xT", [P, S])
        p_log = ph.psum("p_log", [P, T, EX])
        p_rank = ph.psum("p_rank", full)
        p_total = ph.psum("p_total", full)
        p_inv = ph.psum("p_inv", [P, 2, SLOTS])
        names = ("consts stats_done mv_done veps_done rstd_done xn_ready xT_done xT_ready log_done log_ready chain ex_ready "
                 "ranked B_ready A_ready inv_done")
        q = {s: sem(s) for s in names.split()}
        written = [sem(f"written{p}") for p in range(2)]
        NCONST = 9
        INV_STEPS = STEPS
        block = ctx.enter_context(nc.Block())

        @block.sync
        def _(sp):
            for dst, src in ((router[:], w["routerT"]), (rev[:], spread(w["rev8"])), (before[:], w["before"]), (tile_no[:], spread(w["tile_no"])),
                             (part_no[:], column(w["part_no"])), (slot_iota[:], spread(w["slot_iota"]))):
                sp.dma_start(dst, src).then_inc(q["consts"], 16)
            sp.dma_start(tile_k[:, 0, :], spread(w["tile_no"])).then_inc(q["consts"], 16)

            def body(s):
                if s.live():
                    hold(sp, q["xn_ready"], T * (s.t + 1))
                    sp.dma_start(xn_dram[bass.ts(s.t, T)].rearrange("t p d -> p t d"), xn[:, s.p]).then_inc(written[s.p], 16)
            run_steps(sp, body, 1)
            for p in range(2):
                sp.wait_ge(written[p], 16 * STEPS // 2)

        @block.gpsimd
        def _(pool):
            pool.memset(minus_half[:], -0.5).then_inc(q["consts"], 1)
            pool.memset(ones[:], 1.0).then_inc(q["consts"], 1)
            pool.iota(row_i := sb("row_i", [P, P], I32)[:], [[1, P]], base=0, channel_multiplier=0).then_inc(q["consts"], 1)
            pool.wait_ge(q["consts"], 16 * 7 + 3)
            pool.tensor_copy(row_bf[:], row_i).then_inc(q["consts"], 1)

            def body(s):
                if s.live():
                    pool.wait_ge(q["mv_done"], T * (s.t + 1))
                    hold(pool, q["xn_ready"], T * s.t)
                    pool.tensor_scalar(veps[:], mv[:, :, 1], EPS, None, ALU.add).then_inc(q["veps_done"], 1)
                    pool.wait_ge(q["veps_done"], s.t + 1)
                    pool.tensor_tensor(rstd[:], veps[:], minus_half[:], ALU.pow).then_inc(q["rstd_done"], 1)
            run_steps(pool, body, 0)

        @block.scalar
        def _(act):
            act.preload_act_table(ACT.Exp)

            def body(s):
                b = s.back(1)
                if s.live():
                    need(act, q["log_done"], s.t)
                    need(act, q["xT_done"], s.t + 1)
                    act.activation(xT[:], p_xT[:], ACT.Copy).then_inc(q["xT_ready"], 1)
                if b.live():
                    hold(act, q["log_done"], b.t + 1)
                    act.activation(logits[:, bass.ts(b.t, T), :], p_log[:], ACT.Copy).then_inc(q["log_ready"], 1)
            run_steps(act, body, 1)
            act.wait_ge(q["chain"], 2)
            act.activation(work2[:], work[:], ACT.Exp).then_inc(q["ex_ready"], 1)
            act.wait_ge(q["chain"], 10)
            act.activation(e2[:], f1[:], ACT.Exp).then_inc(q["ex_ready"], 1)

        @block.vector
        def _(dve):
            def body(s):
                if s.live():
                    layer_norm_stats(dve, X, s, stats, mv, q["stats_done"], q["mv_done"])
                    need(dve, q["xT_done"], s.t - 1)
                    need(dve, written[s.p], 16 * s.u)
                    dve.wait_ge(q["rstd_done"], s.t + 1)
                    layer_norm_apply(dve, X, s, xn[:, s.p], mv, rstd, q["xn_ready"])
            run_steps(dve, body, 0)

            n = [0]

            def then(ins):
                n[0] += 1
                ins.then_inc(q["chain"], 1)
                dve.wait_ge(q["chain"], n[0])

            def wide(v):
                return v.rearrange("p (t a) -> p t a", a=1).broadcast_to(full)
            revw = rev[:].rearrange("p (a e) -> p a e", a=1).broadcast_to(full)

            def first_best(value, best, hot):
                then(dve.tensor_tensor(hot[:], value, wide(best), ALU.is_equal))
                then(dve.tensor_tensor(hot[:], hot[:], revw, ALU.mult))
                then(dve.tensor_reduce(gsum[:], hot[:], AX.X, ALU.max))
                then(dve.tensor_tensor(hot[:], hot[:], wide(gsum[:]), ALU.is_equal))

            dve.wait_ge(q["consts"], 16 * 7 + 4)
            dve.wait_ge(q["log_ready"], STEPS)
            then(dve.tensor_reduce(m1[:], logits[:], AX.X, ALU.max))
            then(dve.tensor_tensor(work[:], logits[:], wide(m1[:]), ALU.subtract))
            first_best(logits[:], m1[:], hot1)
            then(dve.scalar_tensor_tensor(out=both[:], in0=hot1[:], scalar=-3.0e38, in1=logits[:], op0=ALU.mult, op1=ALU.add))
            then(dve.tensor_reduce(m2[:], both[:], AX.X, ALU.max))
            then(dve.tensor_copy(den[:], m2[:]))
            then(dve.tensor_tensor(f1[:], m2[:], m1[:], ALU.subtract))
            first_best(both[:], m2[:], hot2)
            then(dve.tensor_tensor(both[:], hot1[:], hot2[:], ALU.add))
            dve.wait_ge(q["ex_ready"], 2)
            then(dve.tensor_reduce(z[:], work2[:], AX.X, ALU.add))
            then(dve.reciprocal(rz[:], z[:]))
            then(dve.tensor_tensor(p2[:], e2[:], rz[:], ALU.mult))
            then(dve.scalar_tensor_tensor(out=den[:], in0=p2[:], scalar=1e-9, in1=rz[:], op0=ALU.add, op1=ALU.add))
            then(dve.reciprocal(gsum[:], den[:]))
            then(dve.tensor_tensor(gate[:, 0, :], rz[:], gsum[:], ALU.mult))
            then(dve.tensor_tensor(gate[:, 1, :], p2[:], gsum[:], ALU.mult))
            dve.wait_ge(q["ranked"], 2)
            then(dve.tensor_copy(total[:], p_total[:].rearrange("p t e -> p e t")))
            for e in range(EX):
                then(dve.tensor_tensor_scan(out=upto[:, e, :], data0=ones[:, 0:NT], data1=total[:, e, :], initial=0.0, op0=ALU.mult, op1=ALU.add))
            then(dve.tensor_scalar(padded[:], upto[:, :, NT - 1], float(P - 1), None, ALU.add))
            then(dve.tensor_copy(padded_i[:], padded[:]))
            then(dve.tensor_scalar(padded_i[:], padded_i[:], 7, 7, ALU.arith_shift_right, ALU.logical_shift_left))
            then(dve.tensor_copy(padded[:], padded_i[:]))
            then(dve.tensor_tensor_scan(out=ends[:], data0=ones[:, 0:EX], data1=padded[:], initial=0.0, op0=ALU.mult, op1=ALU.add))
            then(dve.tensor_tensor(padded[:], ends[:], padded[:], ALU.subtract))
            then(dve.tensor_tensor(upto[:], upto[:], total[:], ALU.subtract))
            first = padded[:].rearrange("p (e a) -> p e a", a=1).broadcast_to([P, EX, NT])
            then(dve.tensor_tensor(upto[:], upto[:], first, ALU.add))
            then(dve.tensor_tensor(pos[:], p_rank[:], upto[:].rearrange("p e t -> p t e"), ALU.add))
            for k, hot in enumerate((hot1, hot2)):
                then(dve.tensor_tensor(work[:], hot[:], pos[:], ALU.mult))
                then(dve.tensor_reduce(dest[:, k, :], work[:], AX.X, ALU.add))
            then(dve.tensor_copy(dest_i[:], dest[:]))
            then(dve.tensor_scalar(tile_i[:], dest_i[:], 7, None, ALU.arith_shift_right))
            then(dve.tensor_copy(dest_tile[:], tile_i[:]))
            then(dve.scalar_tensor_tensor(out=dest_row[:], in0=dest_tile[:], scalar=-float(P), in1=dest[:], op0=ALU.mult, op1=ALU.add))
            then(dve.tensor_scalar(row_f[:], slot_iota[:], float(P), None, ALU.mult))
            then(dve.tensor_scalar(exp_f[:], row_f[:], ends[:, 0:1], None, ALU.is_ge))
            for e in range(1, EX - 1):
                then(dve.scalar_tensor_tensor(out=exp_f[:], in0=row_f[:], scalar=ends[:, e:e + 1], in1=exp_f[:], op0=ALU.is_ge, op1=ALU.add))
            then(dve.tensor_copy(tile_expert[:], exp_f[:]))
            then(dve.tensor_copy(slot_bf[:], slot_iota[:]))
            then(dve.tensor_scalar(tile_k[:, 1, :], tile_k[:, 0, :], float(NT), None, ALU.add))

            def invert(s):
                if s.live():
                    need(dve, q["inv_done"], s.t - 1)
                    for n_, (j, k) in enumerate((j, k) for j in range(T) for k in range(TOPK)):
                        t = s.t * T + j
                        dve.tensor_scalar(A[:, s.p, n_, 0], slot_bf[:], dest_tile[:, k, bass.ds(t, 1)], tile_k[:, k, bass.ds(t, 1)], ALU.is_equal, ALU.mult).then_inc(q["A_ready"], 1)
                        dve.tensor_scalar(A[:, s.p, n_, 1], slot_bf[:], dest_tile[:, k, bass.ds(t, 1)], part_no[:, 0:1], ALU.is_equal, ALU.mult).then_inc(q["A_ready"], 1)
                        dve.tensor_scalar(B[:, s.p, n_], row_bf[:], dest_row[:, k, bass.ds(t, 1)], None, ALU.is_equal).then_inc(q["A_ready"], 1)
            run_steps(dve, invert, 0)
            dve.wait_ge(q["inv_done"], INV_STEPS)
            then(dve.tensor_copy(hi_no[:], p_inv[:, 0, :]))
            then(dve.tensor_copy(lo_no[:], p_inv[:, 1, :]))
            then(dve.tensor_scalar(row_f[:], hi_no[:], float(P), -float(P), ALU.mult, ALU.add))
            then(dve.tensor_tensor(row_f[:], row_f[:], lo_no[:], ALU.add))
            then(dve.tensor_scalar(off_f[:], hi_no[:], 0.0, float(NO_ROW), ALU.is_equal, ALU.mult))
            then(dve.tensor_tensor(off_f[:], off_f[:], row_f[:], ALU.add))
            then(dve.tensor_copy(scatter_rows[:], off_f[:]))
            then(dve.tensor_scalar(off_f[:], row_f[:], float(NT * P), -float(NT * P), ALU.is_ge, ALU.mult))
            then(dve.tensor_tensor(off_f[:], off_f[:], row_f[:], ALU.add))
            then(dve.tensor_scalar(off_f[:], off_f[:], 0.0, None, ALU.max))
            then(dve.tensor_copy(gather_rows[:], off_f[:]))

        @block.tensor
        def _(pe):
            pe.wait_ge(q["consts"], 16 * 7 + 4)

            def body(s):
                if s.live():
                    need(pe, q["xT_ready"], s.t)
                    need(pe, q["xn_ready"], T * (s.t + 1))
                    for j in range(T):
                        last = pe.transpose(p_xT[:, j * P:(j + 1) * P], xn[:, s.p, j, :], eye[:])
                    last.then_inc(q["xT_done"], 1)
                    need(pe, q["log_ready"], s.t)
                    need(pe, q["xT_ready"], s.t + 1)
                    for j in range(T):
                        last = pe.matmul(p_log[:, j, :], xT[:, j * P:(j + 1) * P], router[:], start=True, stop=True)
                    last.then_inc(q["log_done"], 1)
            run_steps(pe, body, 0)
            pe.wait_ge(q["chain"], 15)
            chosen = both[:].rearrange("p t e -> p (t e)")
            pe.matmul(p_rank[:].rearrange("p t e -> p (t e)"), before[:], chosen, start=True, stop=True).then_inc(q["ranked"], 1)
            pe.matmul(p_total[:].rearrange("p t e -> p (t e)"), ones[:], chosen, start=True, stop=True).then_inc(q["ranked"], 1)

            def invert(s):
                if s.live():
                    need(pe, q["A_ready"], 24 * (s.t + 1))
                    for n_ in range(8):
                        first = isinstance(s.t, int) and s.t == 0 and n_ == 0
                        last = pe.matmul(p_inv[:].rearrange("p a b -> p (a b)"), B[:, s.p, n_], A[:, s.p, n_].rearrange("p a b -> p (a b)"), start=first, stop=False, skip_group_check=True)
                    last.then_inc(q["inv_done"], 1)
            run_steps(pe, invert, 0)


def expert_phase(nc, w, gather_rows, scatter_rows, tile_expert, xn_dram, y_dram, eye):
    with ExitStack() as ctx:
        ph = Phase(nc, ctx, "e_")
        sb, pair, sem = ph.sb, ph.pair, ph.sem
        w1, w3 = pair("w1", [P, EX, HP]), pair("w3", [P, EX, HP])
        w2 = pair("w2", [P, len(CH), EX * P])
        stage = sb("stage", [P, EX * H])
        rows_in = sb("rows_in", [P, 2, 1], I32)
        rows_out = sb("rows_out", [P, 2, 1], I32)
        xg = sb("xg", [P, 2, P])
        xT = pair("xT", [P, 2, P])
        sl = sb("sl", [P, 2, HP])
        g = sb("g", [P, 2, HP])
        gT = pair("gT", [P, 2, len(CH), P])
        y = sb("y", [P, 2, P])
        p_x = ph.psum("p_x", [P, S])
        p_h1, p_h3 = ([ph.psum(f"p_{n}{k}", [P, S]) for k in range(2)] for n in ("h1", "h3"))
        p_g = ph.psum("p_g", [P, len(CH), P])
        p_y = ph.psum("p_y", [P, S])
        names = ("w_loaded w_hi w_split in_ready out_ready x_done x_hi x_split h1_done h3_done sl_ready g_ready gT_done gT_hi "
                 "gT_split y_done y_ready")
        q = {s: sem(s) for s in names.split()}
        gathered = [sem(f"gathered{p}") for p in range(2)]
        scattered = [sem(f"scattered{p}") for p in range(2)]
        loads = [(w["w1T"], w1[:, :, 0:H], True), (w["w3T"], w3[:, :, 0:H], True)] + [(w["w2T"][r0:r0 + n], w2[:, k], False) for k, (r0, n) in enumerate(CH)]
        block = ctx.enter_context(nc.Block())
        LAGS = 5

        @block.sync
        def _(sp):
            for k, (src, dst, _) in enumerate(loads):
                if k:
                    sp.wait_ge(q["w_split"], k)
                sp.dma_start(stage[0:src.shape[0], 0:src.shape[1]], src).then_inc(q["w_loaded"], 16)

        @block.gpsimd
        def _(pool):
            for part in (w1.hi, w1.lo, w3.hi, w3.lo):
                pool.memset(part[:, :, H:HP].bitcast(F32), 0.0).then_inc(q["w_hi"], 1)

            def body(s):
                o = s.back(4)
                if s.live():
                    need(pool, q["in_ready"], s.t + 1)
                    hold(pool, q["x_done"], s.t - 1)
                    pool.indirect_dma_start(xg[:, s.p], None, xn_dram, bass.IndirectOffsetOnAxis(ap=rows_in[:, s.p], axis=0)).then_inc(gathered[s.p], 16)
                if o.live():
                    need(pool, q["out_ready"], o.t + 1)
                    hold(pool, q["y_ready"], o.t + 1)
                    pool.indirect_dma_start(y_dram, bass.IndirectOffsetOnAxis(ap=rows_out[:, o.p], axis=0), y[:, o.p], None,
                                            bounds_check=TOPK * NT * P - 1, oob_is_err=False).then_inc(scattered[o.p], 16)
            run_steps(pool, body, 4, SLOTS)
            for p in range(2):
                pool.wait_ge(scattered[p], 16 * SLOTS // 2)

        @block.scalar
        def _(act):
            act.preload_act_table(ACT.Silu)

            def body(s):
                a, b, c, d = s.back(1), s.back(2), s.back(3), s.back(4)
                if a.live():
                    need(act, q["h3_done"], a.t - 1)
                    need(act, q["x_done"], a.t + 1)
                    act.activation(xT.hi[:, a.p], p_x[:, 0:P], ACT.Copy).then_inc(q["x_hi"], 1)
                if c.live():
                    need(act, q["y_done"], c.t - 1)
                    need(act, q["gT_done"], c.t + 1)
                    act.activation(gT.hi[:, c.p, 0:2], p_g[:, 0:2], ACT.Copy).then_inc(q["gT_hi"], 1)
                    act.activation(gT.hi[0:CH[2][1], c.p, 2], p_g[0:CH[2][1], 2], ACT.Copy).then_inc(q["gT_hi"], 1)
                if b.live():
                    need(act, q["g_ready"], b.t - 1)
                    need(act, q["h1_done"], b.t + 1)
                    act.activation(sl[:, b.p], p_h1[b.p][:, 0:HP], ACT.Silu).then_inc(q["sl_ready"], 1)
                if d.live():
                    need(act, scattered[d.p], 16 * d.u)
                    need(act, q["y_done"], d.t + 1)
                    act.activation(y[:, d.p], p_y[:, 0:P], ACT.Copy).then_inc(q["y_ready"], 1)
            run_steps(act, body, 4, SLOTS)

        @block.vector
        def _(dve):
            for k, (src, dst, wide) in enumerate(loads):
                n, width = src.shape
                from_ = stage[0:n, 0:width]
                if wide:
                    from_ = from_.rearrange("p (e h) -> p e h", e=EX)
                dve.wait_ge(q["w_loaded"], 16 * (k + 1))
                dve.tensor_copy(dst.hi[0:n], from_).then_inc(q["w_hi"], 1)
                dve.wait_ge(q["w_hi"], 4 + k + 1)
                dve.tensor_tensor(dst.lo[0:n], from_, dst.hi[0:n].bitcast(F32), ALU.subtract).then_inc(q["w_split"], 1)

            def body(s):
                a, b, c, o = s.back(1), s.back(2), s.back(3), s.back(4)
                if s.live():
                    need(dve, gathered[s.p], 16 * s.u)
                    dve.tensor_copy(rows_in[:, s.p], gather_rows[:, bass.ds(s.t, 1)]).then_inc(q["in_ready"], 1)
                if a.live():
                    need(dve, q["h3_done"], a.t - 1)
                    need(dve, q["x_hi"], a.t + 1)
                    dve.tensor_tensor(xT.lo[:, a.p], p_x[:, 0:P], xT.hi[:, a.p].bitcast(F32), ALU.subtract).then_inc(q["x_split"], 1)
                if c.live():
                    need(dve, q["y_done"], c.t - 1)
                    need(dve, q["gT_hi"], 2 * (c.t + 1))
                    dve.tensor_tensor(gT.lo[:, c.p, 0:2], p_g[:, 0:2], gT.hi[:, c.p, 0:2].bitcast(F32), ALU.subtract).then_inc(q["gT_split"], 1)
                    r = CH[2][1]
                    dve.tensor_tensor(gT.lo[0:r, c.p, 2], p_g[0:r, 2], gT.hi[0:r, c.p, 2].bitcast(F32), ALU.subtract).then_inc(q["gT_split"], 1)
                if b.live():
                    need(dve, q["gT_done"], b.t - 1)
                    need(dve, q["h3_done"], b.t + 1)
                    need(dve, q["sl_ready"], b.t + 1)
                    dve.tensor_tensor(g[:, b.p], sl[:, b.p], p_h3[b.p][:, 0:HP], ALU.mult).then_inc(q["g_ready"], 1)
                if c.live():
                    need(dve, scattered[c.p], 16 * c.u)
                    dve.tensor_copy(rows_out[:, c.p], scatter_rows[:, bass.ds(c.t, 1)]).then_inc(q["out_ready"], 1)
            run_steps(dve, body, 4, SLOTS)

        @block.tensor
        def _(pe):
            pe.wait_ge(q["w_split"], len(loads))
            pe.wait_ge(q["w_hi"], 4 + len(loads))

            def body(s):
                a, b, c, d = s.back(1), s.back(2), s.back(3), s.back(4)
                if d.live():
                    need(pe, q["y_ready"], d.t)
                    need(pe, q["gT_split"], 2 * (d.t + 1))
                    e = pe.value_load(tile_expert[0:1, bass.ds(d.t, 1)], min_val=0, max_val=EX - 1)
                    for k, (_, r) in enumerate(CH):
                        last = product(pe, p_y[:, 0:P], gT[0:r, d.p, k], w2[0:r, k, bass.ts(e, P)], k == 0, k == len(CH) - 1)
                    last.then_inc(q["y_done"], 1)
                if a.live():
                    need(pe, q["x_split"], a.t)
                    need(pe, gathered[a.p], 16 * (a.u + 1))
                    pe.transpose(p_x[:, 0:P], xg[:, a.p], eye[:]).then_inc(q["x_done"], 1)
                if c.live():
                    need(pe, q["gT_split"], 2 * c.t)
                    need(pe, q["g_ready"], c.t + 1)
                    for k, (h0, r) in enumerate(CH):
                        last = pe.transpose(p_g[0:r, k, :], g[:, c.p, h0:h0 + r], eye[:])
                    last.then_inc(q["gT_done"], 1)
                if b.live():
                    need(pe, q["g_ready"], b.t - 1)
                    need(pe, q["x_split"], b.t + 1)
                    e = pe.value_load(tile_expert[0:1, bass.ds(b.t, 1)], min_val=0, max_val=EX - 1)
                    for bank, wk, done in ((p_h1, w1, "h1_done"), (p_h3, w3, "h3_done")):
                        rhs = Pair(wk.hi[:].rearrange("p e h -> p (e h)"), wk.lo[:].rearrange("p e h -> p (e h)"))[:, bass.ts(e, HP)]
                        product(pe, bank[b.p][:, 0:HP], xT[:, b.p], rhs, True, True).then_inc(q[done], 1)
            run_steps(pe, body, 4, SLOTS)


def combine_phase(nc, X, gate, y_dram, out_dram):
    with ExitStack() as ctx:
        ph = Phase(nc, ctx, "o_")
        sb, sem = ph.sb, ph.sem
        y = sb("y", [P, 2, TOPK, T, P])
        y_in = [sem(f"y_in{p}") for p in range(2)]
        written = [sem(f"written{p}") for p in range(2)]
        summed = sem("summed")
        block = ctx.enter_context(nc.Block())

        @block.sync
        def _(sp):
            def body(s):
                if s.live():
                    hold(sp, summed, TOPK * T * (s.t - 1))
                    for k in range(TOPK):
                        sp.dma_start(y[:, s.p, k], y_dram[bass.ds(k * NT * P + s.t * S, S)].rearrange("(t p) d -> p t d", p=P)).then_inc(y_in[s.p], 16)
            run_steps(sp, body, 1)

        @block.scalar
        def _(act):
            def body(s):
                if s.live():
                    hold(act, summed, TOPK * T * (s.t + 1))
                    act.dma_start(out_dram[bass.ts(s.t, T)].rearrange("t p d -> p t d"), X[:, bass.ts(s.t, T), :]).then_inc(written[s.p], 16)
            run_steps(act, body, 0)
            for p in range(2):
                act.wait_ge(written[p], 16 * STEPS // 2)

        @block.vector
        def _(dve):
            def body(s):
                if s.live():
                    dve.wait_ge(y_in[s.p], 32 * (s.u + 1))
                    for k in range(TOPK):
                        for j in range(T):
                            if k:
                                need(dve, summed, TOPK * T * s.t + j + 1)
                            xt = X[:, s.t * T + j, :]
                            dve.scalar_tensor_tensor(out=xt, in0=y[:, s.p, k, j], scalar=gate[:, k, bass.ds(s.t * T + j, 1)], in1=xt,
                                                     op0=ALU.mult, op1=ALU.add).then_inc(summed, 1)
            run_steps(dve, body, 0)


def build(nc, ins, out_dram, scratch):
    with ExitStack() as ctx:
        X = ctx.enter_context(nc.sbuf_tensor("x_tokens", [P, NT, P], F32))
        eye = ctx.enter_context(nc.sbuf_tensor("eye", [P, P], F32))
        eye_in = ctx.enter_context(nc.semaphore("eye_in"))
        x_dram = ins["x"].rearrange("b (t p) d -> (b t) p d", p=P)
        with nc.Block() as block:
            @block.sync
            def _(sp):
                sp.dma_start(eye[:], ins["eye"]).then_inc(eye_in, 16)
                sp.wait_ge(eye_in, 16)
        gnn_phase(nc, x_dram, ins["adjT"], ins, X, eye)
        table_ctx = ExitStack()
        with table_ctx:
            XT = table_ctx.enter_context(nc.sbuf_tensor("xT_all", [P, NT * P], F32))
            table = table_ctx.enter_context(nc.sbuf_tensor("table", [P, NT, 3, HEADS], F32))
            dt_phase(nc, ins, X, XT, table, scratch["cum"], eye)
            mamba_phase(nc, ins, X, XT, table, scratch["cum"], eye)
        graph_phase(nc, ins, X, ins["adj"], ins["adjT"], eye)
        gate = ctx.enter_context(nc.sbuf_tensor("gate", [P, TOPK, NT], F32))
        gather_rows = ctx.enter_context(nc.sbuf_tensor("gather_rows", [P, SLOTS], I32))
        scatter_rows = ctx.enter_context(nc.sbuf_tensor("scatter_rows", [P, SLOTS], I32))
        tile_expert = ctx.enter_context(nc.sbuf_tensor("tile_expert", [P, SLOTS], I32))
        xn_tiles = scratch["xn"].rearrange("(t p) d -> t p d", p=P)
        route_phase(nc, ins, X, gate, gather_rows, scatter_rows, tile_expert, xn_tiles, eye)
        expert_phase(nc, ins, gather_rows, scatter_rows, tile_expert, scratch["xn"], scratch["y"], eye)
        combine_phase(nc, X, gate, scratch["y"], out_dram.rearrange("b (t p) d -> (b t) p d", p=P))


def kernel(x, adj, L0_gnn_w_se, L0_gnn_b_se, L0_gnn_conv1_w, L0_gnn_bn1_g, L0_gnn_bn1_b, L0_gnn_bn1_m, L0_gnn_bn1_v,
           L0_gnn_conv2_w, L0_gnn_bn2_g, L0_gnn_bn2_b, L0_gnn_bn2_m, L0_gnn_bn2_v, L0_gnn_w_msg, L0_gnn_b_msg,
           L0_gnn_w_ih, L0_gnn_b_ih, L0_gnn_w_hh, L0_gnn_b_hh, L0_ffn_W_in, L0_ffn_conv_w, L0_ffn_conv_b,
           L0_ffn_dt_bias, L0_ffn_A_log, L0_ffn_D, L0_ffn_norm_w, L0_ffn_W_out, L0_ffn_W_lin, L0_ffn_b_lin,
           L1_gnn_weight, L1_gnn_bias, L1_ffn_router_w, L1_ffn_w1, L1_ffn_w2, L1_ffn_w3):
    import numpy as np
    import concourse.bacc as bacc
    from concourse.bass_utils import run_bass_kernel_spmd

    def lay(a, *order):
        a = np.asarray(a)
        return np.ascontiguousarray(a.transpose(*order) if order else a)

    lr_const = np.zeros((64, 3), np.float32)
    for rows, col in ((slice(0, 3), (0, 0, 2)), (slice(3, 6), (0, -1, 0)), (slice(6, 9), (1, 0, -1)),
                      (slice(32, 35), (0, 0, 1)), (slice(35, 38), (1, 0, 1)), (slice(38, 41), (0, 1, 0))):
        lr_const[rows] = col
    arrays = {
        "x": lay(x), "adj": lay(adj), "adjT": lay(adj, 0, 2, 1), "eye": np.eye(P, dtype=np.float32), "lr_const": lr_const,
        "w_seT": lay(L0_gnn_w_se, 1, 0), "b_se": lay(L0_gnn_b_se),
        "conv1T": lay(np.asarray(L0_gnn_conv1_w)[:, :, 0], 1, 0),
        "conv2T": lay(L0_gnn_conv2_w, 1, 2, 0).reshape(P, -1),
        "gnn_vecs": np.stack([np.asarray(a).reshape(-1, P)[k] for a in (
            L0_gnn_bn1_g, L0_gnn_bn1_b, L0_gnn_bn1_m, L0_gnn_bn1_v, L0_gnn_bn2_g, L0_gnn_bn2_b, L0_gnn_bn2_m,
            L0_gnn_bn2_v, L0_gnn_b_ih, L0_gnn_b_hh) for k in range(np.asarray(a).size // P)], axis=1),
        "w_msgT": lay(L0_gnn_w_msg, 1, 0), "b_msg": lay(L0_gnn_b_msg),
        "w_ihT": lay(np.asarray(L0_gnn_w_ih).reshape(3 * P, 2, P), 2, 1, 0).reshape(P, -1),
        "w_hhT": lay(L0_gnn_w_hh, 1, 0),
        "w1T": lay(L1_ffn_w1, 2, 0, 1).reshape(P, -1), "w3T": lay(L1_ffn_w3, 2, 0, 1).reshape(P, -1),
        "w2T": lay(L1_ffn_w2, 2, 0, 1).reshape(H, -1), "routerT": lay(L1_ffn_router_w, 1, 0),
        "rev8": np.arange(EX, 0, -1, dtype=np.float32), "before": np.triu(np.ones((P, P), np.float32), 1),
        "tile_no": np.arange(1, NT + 1, dtype=np.float32), "part_no": np.arange(P, dtype=np.float32),
        "slot_iota": np.arange(SLOTS, dtype=np.float32),
        "gcn_w": lay(L1_gnn_weight), "gcn_b": lay(L1_gnn_bias),
        "W_in_zx": lay(np.asarray(L0_ffn_W_in)[:, :DI + XBC]), "W_dt": lay(np.asarray(L0_ffn_W_in)[:, DI + XBC:]),
        "dt_bias": lay(L0_ffn_dt_bias), "A_log": lay(L0_ffn_A_log), "D": lay(L0_ffn_D), "b_lin": lay(L0_ffn_b_lin),
        "W_outT": lay(L0_ffn_W_out, 1, 0), "W_lin": lay(L0_ffn_W_lin),
        "mamba_vecs": np.concatenate([np.asarray(L0_ffn_conv_w).reshape(3, P, TAPS).transpose(1, 0, 2).reshape(P, -1),
                                      np.asarray(L0_ffn_conv_b).reshape(3, P).T, np.asarray(L0_ffn_norm_w).reshape(2, P).T], axis=1),
        "mask": np.concatenate([np.triu(np.ones((P, P), np.float32)), np.ones((P, P), np.float32), np.triu(np.ones((P, P), np.float32))], axis=1),
    }
    nc = bacc.Bacc("TRN2", target_bir_lowering=False, num_devices=1)
    ins = {name: nc.dram_tensor(f"in_{name}", a.shape, F32, kind="ExternalInput").ap() for name, a in arrays.items()}
    out = nc.dram_tensor("out", (BS, N, P), F32, kind="ExternalOutput").ap()
    scratch = {"cum": nc.dram_tensor("cum_scratch", (HEADS, BS * N), F32, kind="Internal").ap(),
               "xn": nc.dram_tensor("xn_scratch", (NT * P, P), F32, kind="Internal").ap(),
               "y": nc.dram_tensor("y_scratch", (TOPK * NT * P, P), F32, kind="Internal").ap()}
    build(nc, ins, out, scratch)
    result = run_bass_kernel_spmd(nc, [{f"in_{name}": a for name, a in arrays.items()}], core_ids=[0])
    return result.results[0]["out"]
```

```python
from contextlib import ExitStack

import concourse.bass as bass
from concourse import mybir

F32 = mybir.dt.float32
F32R = mybir.dt.float32r
ACT = mybir.ActivationFunctionType
ALU = mybir.AluOpType
AX = mybir.AxisListType

P = 128
BS = 32
N = 256
T = 4
G = 2
S = T * P
STEPS = BS * N // S
NT = STEPS * T
EPS = 1e-5


class Step:

    def __init__(self, u, p, steps=STEPS, mod=2):
        self.u, self.p, self.t, self.steps, self.mod = u, p, mod * u + p, steps, mod

    def back(self, lag):
        q = self.p - lag
        return Step(self.u + q // self.mod, q % self.mod, self.steps, self.mod)

    def live(self):
        return not isinstance(self.t, int) or 0 <= self.t < self.steps


def run_steps(eng, body, lags, steps=STEPS, mod=2):
    head = lags // mod + 1
    for t in range(mod * head):
        body(Step(t // mod, t % mod, steps, mod))
    with eng.Fori(head, steps // mod) as u:
        for p in range(mod):
            body(Step(u, p, steps, mod))
    for t in range(steps, steps + lags):
        body(Step(t // mod, t % mod, steps, mod))


def need(eng, sem, count):
    if isinstance(count, int) and count <= 0:
        return
    eng.wait_ge(sem, count)


def hold(eng, sem, count):
    need(eng, sem, count)
    if not isinstance(count, int):
        eng.nop(nofuse=True)


class Pair:

    def __init__(self, hi, lo):
        self.hi, self.lo = hi, lo

    def __getitem__(self, k):
        return Pair(self.hi[k], self.lo[k])


def product(pe, out, lhsT, rhs, start, stop):
    pe.matmul(out, lhsT.hi, rhs.hi, start=start, stop=False)
    pe.matmul(out, lhsT.hi, rhs.lo, start=False, stop=False)
    return pe.matmul(out, lhsT.lo, rhs.hi, start=False, stop=stop)


class Phase:

    def __init__(self, nc, ctx, name):
        self.nc, self.ctx, self.name, self.sems = nc, ctx, name, []
        ctx.callback(self.clear)

    def clear(self):
        self.nc.clear_and_free_semaphores(self.sems)
        self.nc.all_engine_barrier()

    def sb(self, name, shape, dt=F32):
        return self.ctx.enter_context(self.nc.sbuf_tensor(self.name + name, shape, dt))

    def pair(self, name, shape):
        return Pair(self.sb(name + "_hi", shape, F32R), self.sb(name + "_lo", shape, F32R))

    def psum(self, name, shape):
        return self.ctx.enter_context(self.nc.psum_tensor(self.name + name, shape, F32))

    def sem(self, name):
        self.sems.append(self.nc.alloc_semaphore(name=self.name + name))
        return self.sems[-1]


def column(v):
    return v.rearrange("(p a) -> p a", a=1)


def spread(v, parts=P):
    return bass.AP(v.tensor, v.offset, [[0, parts]] + list(v.ap))


def layer_norm_stats(dve, X, s, stats, mv, stats_done, mv_done):
    for j in range(T):
        dve.bn_stats(stats[:, s.p, j, :], X[:, s.t * T + j, :]).then_inc(stats_done, 1)
    for j in range(T):
        hold(dve, stats_done, T * s.t + j + 1)
        dve.bn_aggr(mv[:, s.p, j, :], stats[:, s.p, j, :]).then_inc(mv_done, 1)


def layer_norm_rstd(pool, s, mv, veps, minus_half, rstd, mv_done, veps_done, rstd_done, xn_ready):
    need(pool, xn_ready, T * (s.t - 1))
    hold(pool, mv_done, T * (s.t + 1))
    pool.tensor_scalar(veps[:, s.p], mv[:, s.p, :, 1], EPS, None, ALU.add).then_inc(veps_done, 1)
    need(pool, veps_done, s.t + 1)
    pool.tensor_tensor(rstd[:, s.p], veps[:, s.p], minus_half[:], ALU.pow).then_inc(rstd_done, 1)


def layer_norm_apply(dve, X, s, xn, mv, rstd, rstd_done, xn_ready):
    need(dve, rstd_done, s.t + 1)
    for j in range(T):
        dve.tensor_scalar(xn[:, j, :], X[:, s.t * T + j, :], mv[:, s.p, j, 0:1], rstd[:, s.p, j:j + 1], ALU.subtract, ALU.mult).then_inc(xn_ready, 1)


def gnn_phase(nc, x_dram, adjT_dram, w, X, eye):
    TAPS = 17
    PAD = TAPS // 2
    NP = N + 2 * PAD
    L0, R0, KD = 0, 32, 9
    with ExitStack() as ctx:
        ph = Phase(nc, ctx, "g_")
        sb, pair, sem = ph.sb, ph.pair, ph.sem
        stage = sb("stage", [P, TAPS * P])
        conv1 = pair("conv1", [P, P])
        conv2 = pair("conv2", [P, TAPS * P])
        w_lr = pair("w_lr", [P, 64])
        w_msg = pair("w_msg", [P, P])
        w_ih = pair("w_ih", [P, 2 * 3 * P])
        w_hh = pair("w_hh", [P, 3 * P])
        b_msg = sb("b_msg", [P, P])
        lr_cols = sb("lr_cols", [64, 3])
        vecs = sb("vecs", [P, 14])
        BN = {"g1": 0, "b1": 1, "m1": 2, "v1": 3, "g2": 4, "b2": 5, "m2": 6, "v2": 7}
        B_IH, B_HH = 8, 11
        scales = sb("scales", [P, 8])
        tmp2 = sb("tmp2", [P, 4])
        minus_half = sb("minus_half", [P, 4])
        adjT = sb("adjT", [P, 2, G, 2, N])
        stats = sb("stats", [P, 2, T, 6])
        mv = sb("mv", [P, 2, T, 2])
        veps = sb("veps", [P, 2, T])
        rstd = sb("rstd", [P, 2, T])
        xn = sb("xn", [P, T, P])
        xf = sb("xf", [P, 2, S])
        xs = pair("xs", [P, 2, S])
        h1f = sb("h1f", [P, G, N])
        h1 = pair("h1", [P, G, NP])
        t1 = sb("t1", [64, S])
        t2 = sb("t2", [64, S])
        q = sb("q", [64, S])
        right = sb("right", [KD, S])
        mb = sb("mb", [P, T, P])
        mf = sb("mf", [P, T, P])
        msg = pair("msg", [P, T, P])
        E = sb("E", [P, G, 2, N])
        Am = sb("Am", [P, G, 2, N])
        A = pair("A", [P, G, 2, N])
        v = sb("v", [P, S])
        xcf = sb("xcf", [P, S])
        xc = pair("xc", [P, S])
        nm = pair("nm", [P, S])
        gh = sb("gh", [P, S])
        tr = sb("tr", [P, S])
        tz = sb("tz", [P, S])
        u_ = sb("u", [P, S])
        tn = sb("tn", [P, S])
        d_ = sb("d", [P, S])
        g_ = sb("gg", [P, S])
        hT = sb("hT", [P, S])
        p_conv2 = ph.psum("p_conv2", [P, S])
        p_msg = p_conv2
        p_nmp = ph.psum("p_nmp", [P, S])
        p_lr = p_nmp
        p_xT = ph.psum("p_xT", [P, S])
        p_conv1 = p_xT
        p_dist = ph.psum("p_dist", [P, G, 2, N])
        p_back = p_dist[:, 0, :, :].rearrange("p a b -> p (a b)")
        p_r = ph.psum("p_r", [P, S])
        p_z = ph.psum("p_z", [P, S])
        p_n = ph.psum("p_n", [P, S])

        loaded = sem("loaded")
        w_loaded = sem("w_loaded")
        w_split = sem("w_split")
        stage_clear, w_hi = sem("stage_clear"), sem("w_hi")
        consts = sem("consts")
        bn_ready = sem("bn_ready")
        x_in = [sem(f"x_in{p}") for p in range(2)]
        adj_in = [sem(f"adj_in{p}") for p in range(2)]
        stats_done, mv_done, veps_done, rstd_done = sem("stats_done"), sem("mv_done"), sem("veps_done"), sem("rstd_done")
        xn_ready = sem("xn_ready")
        xT_done, x_hi_f, x_split = sem("xT_done"), sem("x_hi_f"), sem("x_split")
        conv1_done, h1_hi_f, h1_split = sem("conv1_done"), sem("h1_hi_f"), sem("h1_split")
        lr_done, t1_ready, t2_ready, q_ready, right_ready = (sem(s) for s in ("lr_done", "t1_ready", "t2_ready", "q_ready", "right_ready"))
        msg_done, msg_biased, msg_hi_f, msg_split = (sem(s) for s in ("msg_done", "msg_biased", "msg_hi_f", "msg_split"))
        dist_done, exp_done, masked, A_split = (sem(s) for s in ("dist_done", "exp_done", "masked", "A_split"))
        conv2_done, v_ready, xc_hi_f, xc_split = (sem(s) for s in ("conv2_done", "v_ready", "xc_hi_f", "xc_split"))
        nmp_done, nmp_hi, nmp_split = sem("nmp_done"), sem("nmp_hi"), sem("nmp_split")
        ghn_done, gh_ready, r_done, z_done, n_done = (sem(s) for s in ("ghn_done", "gh_ready", "r_done", "z_done", "n_done"))
        tr_ready, tz_ready, rg_ready, u_ready, tn_ready, d_ready, g_ready, hT_ready = (
            sem(s) for s in ("tr_ready", "tz_ready", "rg_ready", "u_ready", "tn_ready", "d_ready", "g_ready", "hT_ready"))
        back_done, x_updated = sem("back_done"), sem("x_updated")

        weights = [(w["conv1T"], conv1), (w["conv2T"], conv2), (w["w_msgT"], w_msg), (w["w_ihT"], w_ih), (w["w_hhT"], w_hh)]
        block = ctx.enter_context(nc.Block())

        @block.sync
        def _(sp):
            sp.dma_start(vecs[:], w["gnn_vecs"]).then_inc(loaded, 16)
            sp.dma_start(b_msg[:], spread(w["b_msg"])).then_inc(loaded, 16)
            sp.dma_start(lr_cols[:], w["lr_const"]).then_inc(consts, 16)
            sp.wait_ge(consts, 16)
            for row in (L0, L0 + 3, R0, R0 + 6):
                sp.dma_start(lr_cols[row:row + 3, 0:1], column(w["b_se"])).then_inc(loaded, 16)
            sp.wait_ge(stage_clear, 1)
            for k, at in enumerate((L0, L0 + 3, R0, R0 + 6)):
                sp.dma_start(stage[:, at:at + 3], w["w_seT"]).then_inc(w_loaded, 16)
            for k, (src, dst) in enumerate(weights):
                sp.wait_ge(w_split, k + 1)
                width = src.shape[1]
                sp.dma_start(stage[:, 0:width], src).then_inc(w_loaded, 16)

            def body(s):
                if s.live():
                    hold(sp, mv_done, T * (s.t - 1))
                    sp.dma_start(X[:, bass.ts(s.t, T), :], x_dram[bass.ts(s.t, T)].rearrange("t p d -> p t d")).then_inc(x_in[s.p], 16)
                    hold(sp, masked, s.t - 1)
                    sp.dma_start(adjT[:, s.p], adjT_dram[bass.ts(s.t, G)].rearrange("g (a m) n -> m g a n", m=P)).then_inc(adj_in[s.p], 16)
            run_steps(sp, body, 0)

        @block.gpsimd
        def _(pool):
            pool.memset(stage[:, 0:64], 0.0).then_inc(stage_clear, 1)
            pool.memset(minus_half[:], -0.5).then_inc(bn_ready, 1)
            for part in (h1.hi, h1.lo):
                pool.memset(part[:].bitcast(F32), 0.0).then_inc(bn_ready, 1)
            pool.wait_ge(loaded, 16 * 6)
            v_cols = vecs[:, BN["v1"]:BN["v2"] + 1:4]
            g_cols = vecs[:, BN["g1"]:BN["g2"] + 1:4]
            b_cols = vecs[:, BN["b1"]:BN["b2"] + 1:4]
            m_cols = vecs[:, BN["m1"]:BN["m2"] + 1:4]
            pool.tensor_scalar(tmp2[:, 0:2], v_cols, EPS, None, ALU.add).then_inc(bn_ready, 1)
            pool.wait_ge(bn_ready, 4)
            pool.tensor_tensor(tmp2[:, 2:4], tmp2[:, 0:2], minus_half[:, 0:2], ALU.pow).then_inc(bn_ready, 1)
            pool.wait_ge(bn_ready, 5)
            pool.tensor_tensor(scales[:, 0:2], tmp2[:, 2:4], g_cols, ALU.mult).then_inc(bn_ready, 1)
            pool.wait_ge(bn_ready, 6)
            pool.tensor_tensor(tmp2[:, 0:2], scales[:, 0:2], m_cols, ALU.mult).then_inc(bn_ready, 1)
            pool.wait_ge(bn_ready, 7)
            pool.tensor_tensor(scales[:, 2:4], b_cols, tmp2[:, 0:2], ALU.subtract).then_inc(bn_ready, 1)
            pool.tensor_tensor(scales[:, 4:6], vecs[:, B_IH:B_IH + 2], vecs[:, B_HH:B_HH + 2], ALU.add).then_inc(bn_ready, 1)
            pool.tensor_scalar(scales[:, 6:7], vecs[:, B_HH + 2:B_HH + 3], 0.5, None, ALU.mult).then_inc(bn_ready, 1)
            pool.wait_ge(bn_ready, 10)
            pool.tensor_scalar(scales[:, 4:6], scales[:, 4:6], 0.5, None, ALU.mult).then_inc(bn_ready, 1)

            def body(s):
                a, b = s.back(1), s.back(2)
                if a.live():
                    pool.wait_ge(x_hi_f, 2 * (a.t + 1))
                    need(pool, n_done, a.t - 1)
                    pool.tensor_tensor(xs.lo[:, a.p], xf[:, a.p], xs.hi[:, a.p].bitcast(F32), ALU.subtract).then_inc(x_split, 1)
                if s.live():
                    layer_norm_rstd(pool, s, mv, veps, minus_half, rstd, mv_done, veps_done, rstd_done, xn_ready)
                if a.live():
                    need(pool, t1_ready, a.t + 1)
                    hold(pool, dist_done, a.t)
                    pool.tensor_scalar(t2[:], t1[:], lr_cols[:, 1:2], lr_cols[:, 2:3], ALU.mult, ALU.add).then_inc(t2_ready, 1)
                    pool.wait_ge(t2_ready, a.t + 1)
                    pool.tensor_tensor(q[:], t1[:], t2[:], ALU.mult).then_inc(q_ready, 1)
                if b.live():
                    pool.wait_ge(tn_ready, b.t + 1)
                    need(pool, g_ready, b.t)
                    pool.tensor_tensor(d_[:], xf[:, b.p], tn[:], ALU.subtract).then_inc(d_ready, 1)
            run_steps(pool, body, 2)

        @block.scalar
        def _(act):
            act.preload_act_table(ACT.Exp)
            act.wait_ge(bn_ready, 11)
            act.wait_ge(loaded, 16 * 6)

            def body(s):
                b = s.back(1)
                if b.live():
                    act.wait_ge(nmp_done, b.t + 1)
                    act.activation(nm.hi[:], p_nmp[:], ACT.Copy).then_inc(nmp_hi, 1)
                    act.wait_ge(v_ready, b.t + 1)
                    need(act, n_done, b.t)
                    act.activation(xcf[:], v[:], ACT.Relu, bias=scales[:, 3:4]).then_inc(xc_hi_f, 1)
                    act.activation(xc.hi[:], v[:], ACT.Relu, bias=scales[:, 3:4]).then_inc(xc_hi_f, 1)
                if s.live():
                    act.wait_ge(xT_done, s.t + 1)
                    need(act, n_done, s.t - 1)
                    need(act, d_ready, s.t - 1)
                    act.activation(xs.hi[:, s.p], p_xT[:], ACT.Copy).then_inc(x_hi_f, 1)
                    act.activation(xf[:, s.p], p_xT[:], ACT.Copy).then_inc(x_hi_f, 1)
                if b.live():
                    act.wait_ge(ghn_done, b.t + 1)
                    need(act, rg_ready, b.t)
                    act.activation(gh[:], p_n[:], ACT.Identity, bias=scales[:, 6:7], scale=0.5).then_inc(gh_ready, 1)
                if s.live():
                    act.wait_ge(conv1_done, s.t + 1)
                    need(act, conv2_done, s.t)
                    p1 = p_conv1[:].rearrange("p (g n) -> p g n", g=G)
                    act.activation(h1f[:], p1, ACT.Relu, bias=scales[:, 2:3], scale=scales[:, 0:1]).then_inc(h1_hi_f, 1)
                    act.activation(h1.hi[:, :, PAD:PAD + N], p1, ACT.Relu, bias=scales[:, 2:3], scale=scales[:, 0:1]).then_inc(h1_hi_f, 1)
                    act.wait_ge(lr_done, s.t + 1)
                    need(act, q_ready, s.t)
                    act.activation(t1[:], p_lr[0:64, :], ACT.Identity, bias=lr_cols[:, 0:1]).then_inc(t1_ready, 1)
                    act.wait_ge(msg_biased, s.t + 1)
                    need(act, nmp_done, s.t)
                    act.activation(mf[:], mb[:], ACT.Relu).then_inc(msg_hi_f, 1)
                    act.activation(msg.hi[:], mb[:], ACT.Relu).then_inc(msg_hi_f, 1)
                    act.wait_ge(q_ready, s.t + 1)
                    need(act, dist_done, s.t)
                    act.activation(right[:], q[R0:R0 + KD, :], ACT.Copy).then_inc(right_ready, 1)
                if b.live():
                    act.wait_ge(r_done, b.t + 1)
                    need(act, rg_ready, b.t)
                    act.activation(tr[:], p_r[:], ACT.Tanh, bias=scales[:, 4:5], scale=0.5).then_inc(tr_ready, 1)
                    act.wait_ge(z_done, b.t + 1)
                    need(act, g_ready, b.t)
                    act.activation(tz[:], p_z[:], ACT.Tanh, bias=scales[:, 5:6], scale=0.5).then_inc(tz_ready, 1)
                    act.wait_ge(u_ready, b.t + 1)
                    need(act, hT_ready, b.t)
                    act.activation(tn[:], u_[:], ACT.Tanh, bias=vecs[:, B_IH + 2:B_IH + 3]).then_inc(tn_ready, 1)
                if s.live():
                    act.wait_ge(dist_done, s.t + 1)
                    need(act, masked, s.t)
                    act.activation(E[:], p_dist[:], ACT.Exp).then_inc(exp_done, 1)
            run_steps(act, body, 1)

        @block.vector
        def _(dve):
            dsts = [(w_lr, 64)] + [(dst, src.shape[1]) for src, dst in weights]
            for k, (dst, width) in enumerate(dsts):
                dve.wait_ge(w_loaded, 16 * (4 + k))
                dve.tensor_copy(dst.hi[:, 0:width], stage[:, 0:width]).then_inc(w_hi, 1)
                dve.wait_ge(w_hi, 1 + k)
                dve.tensor_tensor(dst.lo[:, 0:width], stage[:, 0:width], dst.hi[:, 0:width].bitcast(F32), ALU.subtract).then_inc(w_split, 1)
            dve.wait_ge(bn_ready, 11)
            dve.wait_ge(loaded, 16 * 6)

            def body(s):
                a, b, c = s.back(1), s.back(2), s.back(3)
                if c.live():
                    dve.wait_ge(d_ready, c.t + 1)
                    dve.wait_ge(tz_ready, c.t + 1)
                    dve.scalar_tensor_tensor(out=g_[:], in0=tz[:], scalar=1.0, in1=d_[:], op0=ALU.add, op1=ALU.mult).then_inc(g_ready, 1)
                    dve.wait_ge(g_ready, c.t + 1)
                    need(dve, back_done, c.t)
                    dve.scalar_tensor_tensor(out=hT[:], in0=g_[:], scalar=0.5, in1=tn[:], op0=ALU.mult, op1=ALU.add).then_inc(hT_ready, 1)
                if b.live():
                    dve.wait_ge(exp_done, b.t + 1)
                    dve.wait_ge(adj_in[b.p], 16 * (b.u + 1))
                    dve.tensor_tensor(Am[:], E[:], adjT[:, b.p], ALU.mult).then_inc(masked, 1)
                    dve.wait_ge(masked, b.t + 1)
                    need(dve, nmp_done, b.t)
                    dve.tensor_copy(A.hi[:], Am[:]).then_inc(A_split, 1)
                    dve.wait_ge(A_split, 2 * b.t + 1)
                    dve.tensor_tensor(A.lo[:], Am[:], A.hi[:].bitcast(F32), ALU.subtract).then_inc(A_split, 1)
                if a.live():
                    need(dve, xT_done, a.t)
                    layer_norm_apply(dve, X, a, xn, mv, rstd, rstd_done, xn_ready)
                if s.live():
                    dve.wait_ge(x_in[s.p], 16 * (s.u + 1))
                    layer_norm_stats(dve, X, s, stats, mv, stats_done, mv_done)
                if b.live():
                    dve.wait_ge(conv2_done, b.t + 1)
                    dve.wait_ge(x_hi_f, 2 * (b.t + 1))
                    dve.scalar_tensor_tensor(out=v[:], in0=p_conv2[:], scalar=scales[:, 1:2], in1=xf[:, b.p], op0=ALU.mult, op1=ALU.add).then_inc(v_ready, 1)
                    dve.wait_ge(nmp_hi, b.t + 1)
                    need(dve, n_done, b.t)
                    dve.tensor_tensor(nm.lo[:], p_nmp[:], nm.hi[:].bitcast(F32), ALU.subtract).then_inc(nmp_split, 1)
                    dve.wait_ge(xc_hi_f, 2 * (b.t + 1))
                    dve.tensor_tensor(xc.lo[:], xcf[:], xc.hi[:].bitcast(F32), ALU.subtract).then_inc(xc_split, 1)
                if c.live():
                    dve.wait_ge(back_done, c.t + 1)
                    xt = X[:, bass.ts(c.t, T), :].rearrange("p t d -> p (t d)")
                    dve.tensor_tensor(xt, xt, p_back, ALU.add).then_inc(x_updated, 1)
                if a.live():
                    dve.wait_ge(msg_done, a.t + 1)
                    need(dve, msg_hi_f, 2 * a.t)
                    bb = b_msg[:].rearrange("p (a d) -> p a d", a=1).broadcast_to([P, T, P])
                    dve.tensor_tensor(mb[:], p_msg[:].rearrange("p (t d) -> p t d", t=T), bb, ALU.add).then_inc(msg_biased, 1)
                    dve.wait_ge(h1_hi_f, 2 * (a.t + 1))
                    dve.tensor_tensor(h1.lo[:, :, PAD:PAD + N], h1f[:], h1.hi[:, :, PAD:PAD + N].bitcast(F32), ALU.subtract).then_inc(h1_split, 1)
                    dve.wait_ge(msg_hi_f, 2 * (a.t + 1))
                    dve.tensor_tensor(msg.lo[:], mf[:], msg.hi[:].bitcast(F32), ALU.subtract).then_inc(msg_split, 1)
                if b.live():
                    dve.wait_ge(tr_ready, b.t + 1)
                    dve.wait_ge(gh_ready, b.t + 1)
                    need(dve, u_ready, b.t)
                    dve.scalar_tensor_tensor(out=v[:], in0=tr[:], scalar=1.0, in1=gh[:], op0=ALU.add, op1=ALU.mult).then_inc(rg_ready, 1)
                    dve.wait_ge(rg_ready, b.t + 1)
                    dve.wait_ge(n_done, b.t + 1)
                    need(dve, tn_ready, b.t)
                    dve.tensor_tensor(u_[:], v[:], p_n[:], ALU.add).then_inc(u_ready, 1)
            run_steps(dve, body, 3)

        @block.tensor
        def _(pe):
            pe.wait_ge(w_split, 1 + len(weights))
            pe.wait_ge(bn_ready, 11)

            def body(s):
                b, c = s.back(1), s.back(2)
                if b.live():
                    pe.wait_ge(h1_split, b.t + 1)
                    pe.wait_ge(msg_biased, b.t + 1)
                    out = p_conv2[:].rearrange("p (g n) -> p g n", g=G)
                    for k in range(TAPS):
                        last = product(pe, out, conv2[:, k * P:(k + 1) * P], h1[:, :, k:k + N], k == 0, k == TAPS - 1)
                    last.then_inc(conv2_done, 1)
                if c.live():
                    pe.wait_ge(hT_ready, c.t + 1)
                    need(pe, exp_done, c.t + 2) if b.live() else None
                    for j in range(T):
                        last = pe.transpose(p_back[:, j * P:(j + 1) * P], hT[:, j * P:(j + 1) * P], eye[:])
                    last.then_inc(back_done, 1)
                if b.live():
                    pe.wait_ge(A_split, 2 * (b.t + 1))
                    pe.wait_ge(msg_split, b.t + 1)
                    pe.wait_ge(t1_ready, b.t + 1)
                    for g in range(G):
                        for a in range(2):
                            last = product(pe, p_nmp[:, g * N:(g + 1) * N], msg[:, 2 * g + a, :], A[:, g, a, :], a == 0, a == 1)
                    last.then_inc(nmp_done, 1)
                if s.live():
                    pe.wait_ge(xn_ready, 4 * (s.t + 1))
                    need(pe, h1_hi_f, 2 * s.t)
                    for j in range(T):
                        last = pe.transpose(p_xT[:, j * P:(j + 1) * P], xn[:, j, :], eye[:])
                    last.then_inc(xT_done, 1)
                if b.live():
                    need(pe, u_ready, b.t)
                    need(pe, tz_ready, b.t)
                    xb = xs[:, b.p]
                    product(pe, p_n[:], w_hh[:, 2 * P:3 * P], xb, True, True).then_inc(ghn_done, 1)
                    product(pe, p_r[:], w_hh[:, 0:P], xb, True, False)
                    product(pe, p_z[:], w_hh[:, P:2 * P], xb, True, False)
                if s.live():
                    pe.wait_ge(x_split, s.t + 1)
                    xb = xs[:, s.p]
                    product(pe, p_conv1[:], conv1[:, :], xb, True, True).then_inc(conv1_done, 1)
                    need(pe, nmp_split, s.t)
                    product(pe, p_lr[0:64, :], w_lr[:, :], xb, True, True).then_inc(lr_done, 1)
                    need(pe, v_ready, s.t)
                    for j in range(T):
                        last = product(pe, p_msg[:, j * P:(j + 1) * P], xb[:, j * P:(j + 1) * P], w_msg[:, :], True, True)
                    last.then_inc(msg_done, 1)
                if b.live():
                    pe.wait_ge(xc_split, b.t + 1)
                    pe.wait_ge(nmp_split, b.t + 1)
                    for k, (bank, done) in enumerate(((p_r, r_done), (p_z, z_done), (p_n, n_done))):
                        if bank is p_n:
                            pe.wait_ge(gh_ready, b.t + 1)
                        product(pe, bank[:], w_ih[:, k * P:(k + 1) * P], xc[:, :], bank is p_n, False)
                        product(pe, bank[:], w_ih[:, (3 + k) * P:(4 + k) * P], nm[:, :], False, True).then_inc(done, 1)
                if s.live():
                    pe.wait_ge(right_ready, s.t + 1)
                    need(pe, x_updated, s.t - 1)
                    for g in range(G):
                        for a in range(2):
                            m0 = g * N + a * P
                            last = pe.matmul(p_dist[:, g, a, :], q[0:KD, m0:m0 + P], right[:, g * N:(g + 1) * N], start=True, stop=True)
                    last.then_inc(dist_done, 1)
            run_steps(pe, body, 2)


HEADS = 4
HD = 64
DI = HEADS * HD
DS = 64
XBC = DI + 2 * DS
TAPS = 4
HALF_DT, CUM, OFF = 0, 1, 2


def dt_phase(nc, w, X, XT, table, cum_dram, eye):
    with ExitStack() as ctx:
        ph = Phase(nc, ctx, "t_")
        sb, sem = ph.sb, ph.sem
        w_dt = sb("w_dt", [P, HEADS])
        cols = sb("cols", [HEADS, 4])
        b_lin = sb("b_lin", [P, P])
        minus_half = sb("minus_half", [P, T])
        ones = sb("ones", [HEADS, P])
        stats, mv = sb("stats", [P, 2, T, 6]), sb("mv", [P, 2, T, 2])
        veps, rstd = sb("veps", [P, 2, T]), sb("rstd", [P, 2, T])
        xn = sb("xn", [P, 2, T, P])
        u, absu, e, l, dt, dA = (sb(s, [HEADS, S]) for s in ("u", "absu", "e", "l", "dt", "dA"))
        rows = sb("rows", [P, 2, S])
        p_xT = ph.psum("p_xT", [P, S])
        p_dt = ph.psum("p_dt", [P, S])
        p_tab = ph.psum("p_tab", [P, T, P])
        loaded, consts = sem("loaded"), sem("consts")
        stats_done, mv_done, veps_done, rstd_done = sem("stats_done"), sem("mv_done"), sem("veps_done"), sem("rstd_done")
        xn_ready, xT_done, XT_ready, biased = sem("xn_ready"), sem("xT_done"), sem("XT_ready"), sem("biased")
        dt_done, u_ready, e_ready, l_ready, dt_ready, dA_ready = (
            sem(s) for s in ("dt_done", "u_ready", "e_ready", "l_ready", "dt_ready", "dA_ready"))
        scanned, rows_ready, rows_turned, table_ready = (sem(s) for s in ("scanned", "rows_ready", "rows_turned", "table_ready"))
        written = [sem(f"written{p}") for p in range(2)]
        block = ctx.enter_context(nc.Block())

        @block.sync
        def _(sp):
            sp.dma_start(w_dt[:], w["W_dt"]).then_inc(loaded, 16)
            sp.dma_start(cols[:, 0:1], column(w["dt_bias"])).then_inc(loaded, 16)
            sp.dma_start(cols[:, 1:2], column(w["A_log"])).then_inc(loaded, 16)
            sp.dma_start(b_lin[:], spread(w["b_lin"])).then_inc(loaded, 16)

            def body(s):
                b = s.back(1)
                if b.live():
                    hold(sp, rows_ready, 2 * (b.t + 1))
                    sp.dma_start(cum_dram[:, bass.ts(b.t, S)], rows[32:32 + HEADS, b.p]).then_inc(written[b.p], 16)
            run_steps(sp, body, 1)
            for p in range(2):
                sp.wait_ge(written[p], 16 * STEPS // 2)

        @block.gpsimd
        def _(pool):
            pool.memset(minus_half[:], -0.5).then_inc(consts, 1)
            pool.memset(ones[:], 1.0).then_inc(consts, 1)
            pool.memset(rows[:], 0.0).then_inc(consts, 1)
            pool.wait_ge(consts, 3)
            pool.wait_ge(loaded, 16 * 4)

            def body(s):
                a = s.back(1)
                if s.live():
                    layer_norm_rstd(pool, s, mv, veps, minus_half, rstd, mv_done, veps_done, rstd_done, xn_ready)
                if a.live():
                    hold(pool, xn_ready, T * (a.t + 1))
                    xt = X[:, bass.ts(a.t, T), :]
                    bb = b_lin[:].rearrange("p (a d) -> p a d", a=1).broadcast_to([P, T, P])
                    pool.tensor_tensor(xt, xt, bb, ALU.add).then_inc(biased, 1)
            run_steps(pool, body, 1)

        @block.scalar
        def _(act):
            act.preload_act_table_set("natural_log_exp_and_others")
            act.wait_ge(loaded, 16 * 4)
            act.activation(cols[:, 2:3], cols[:, 1:2], ACT.Exp).then_inc(consts, 1)
            act.wait_ge(consts, 4)

            def body(s):
                b, c = s.back(1), s.back(2)
                if b.live():
                    act.wait_ge(u_ready, b.t + 1)
                    act.activation(absu[:], u[:], ACT.Abs).then_inc(e_ready, 1)
                    act.wait_ge(e_ready, 2 * b.t + 1)
                    act.activation(e[:], absu[:], ACT.Exp, scale=-1.0).then_inc(e_ready, 1)
                    act.wait_ge(e_ready, 2 * (b.t + 1))
                    need(act, dt_ready, 2 * b.t)
                    act.activation(l[:], e[:], ACT.Ln, bias=1.0).then_inc(l_ready, 1)
                if s.live():
                    hold(act, xT_done, s.t + 1)
                    act.activation(XT[:, bass.ts(s.t, S)], p_xT[:], ACT.Copy).then_inc(XT_ready, 1)
                if c.live():
                    hold(act, rows_turned, c.t + 1)
                    groups = p_tab[:, :, 0:96].rearrange("p t (g r) -> p t g r", g=3)[:, :, :, 0:HEADS]
                    act.activation(table[:, bass.ts(c.t, T)], groups, ACT.Copy).then_inc(table_ready, 1)
            run_steps(act, body, 2)

        @block.vector
        def _(dve):
            dve.wait_ge(consts, 4)
            dve.tensor_scalar(cols[:, 3:4], cols[:, 2:3], -1.0, None, ALU.mult).then_inc(consts, 1)
            dve.wait_ge(consts, 5)

            def body(s):
                a, b = s.back(1), s.back(2)
                if b.live():
                    dve.wait_ge(dt_done, b.t + 1)
                    need(dve, dt_ready, 2 * b.t)
                    dve.tensor_scalar(u[:], p_dt[0:HEADS, :], cols[:, 0:1], None, ALU.add).then_inc(u_ready, 1)
                if s.live():
                    layer_norm_stats(dve, X, s, stats, mv, stats_done, mv_done)
                if a.live():
                    need(dve, xT_done, a.t - 1)
                    layer_norm_apply(dve, X, a, xn[:, a.p], mv, rstd, rstd_done, xn_ready)
                if b.live():
                    dve.wait_ge(u_ready, b.t + 1)
                    dve.wait_ge(l_ready, b.t + 1)
                    dve.scalar_tensor_tensor(out=dt[:], in0=u[:], scalar=0.0, in1=l[:], op0=ALU.max, op1=ALU.add).then_inc(dt_ready, 1)
                    need(dve, rows_turned, b.t - 1)
                    need(dve, written[b.p], 16 * b.u)
                    hold(dve, dt_ready, 2 * b.t + 1)
                    dve.tensor_scalar(rows[0:HEADS, b.p], dt[:], 0.5, None, ALU.mult).then_inc(dt_ready, 1)
                    dve.tensor_scalar(dA[:], dt[:], cols[:, 3:4], None, ALU.mult).then_inc(dA_ready, 1)
                    hold(dve, dA_ready, b.t + 1)
                    for j in range(T):
                        dve.tensor_tensor_scan(out=rows[32:32 + HEADS, b.p, j * P:(j + 1) * P], data0=ones[:],
                                               data1=dA[:, j * P:(j + 1) * P], initial=0.0, op0=ALU.mult, op1=ALU.add).then_inc(scanned, 1)
                    hold(dve, scanned, T * (b.t + 1))
                    for g in range(G):
                        cum = rows[32:32 + HEADS, b.p, g * N:g * N + P]
                        dve.tensor_scalar(rows[64:64 + HEADS, b.p, g * N:g * N + P], cum, cum[:, P - 1:P], -1.0,
                                          ALU.subtract, ALU.mult).then_inc(rows_ready, 1)
            run_steps(dve, body, 2)

        @block.tensor
        def _(pe):
            pe.wait_ge(loaded, 16 * 4)

            def body(s):
                b, c = s.back(1), s.back(2)
                if s.live():
                    pe.wait_ge(xn_ready, T * (s.t + 1))
                    need(pe, XT_ready, s.t)
                    for j in range(T):
                        last = pe.transpose(p_xT[:, j * P:(j + 1) * P], xn[:, s.p, j, :], eye[:])
                    last.then_inc(xT_done, 1)
                if c.live():
                    pe.wait_ge(rows_ready, 2 * (c.t + 1))
                    need(pe, table_ready, c.t)
                    for j in range(T):
                        last = pe.transpose(p_tab[:, j, 0:96], rows[0:96, c.p, j * P:(j + 1) * P], eye[0:96, 0:96])
                    last.then_inc(rows_turned, 1)
                if s.live():
                    need(pe, u_ready, s.t)
                    hold(pe, XT_ready, s.t + 1)
                    pe.matmul(p_dt[0:HEADS, :], w_dt[:], XT[:, bass.ts(s.t, S)], start=True, stop=True).then_inc(dt_done, 1)
            run_steps(pe, body, 2)


def mamba_phase(nc, w, X, XT, table, cum_dram, eye):
    NB = 3 * P
    with ExitStack() as ctx:
        ph = Phase(nc, ctx, "m_")
        sb, sem = ph.sb, ph.sem
        w_in = sb("w_in", [P, DI + XBC])
        w_out = sb("w_out", [P, 2, P])
        w_outT = sb("w_outT", [P, DI])
        w_lin = sb("w_lin", [P, P])
        vecs = sb("vecs", [P, 3 * TAPS + 3 + 2])
        half_D = sb("half_D", [P, HEADS])
        mask = sb("mask", [P, NB])
        minus_half = sb("minus_half", [P, T])
        xT = sb("xT", [P, 2, S])
        cum = sb("cum", [P, 2, HEADS, S])
        tab = sb("tab", [P, 2, T, 3, HEADS])
        xp = sb("xp", [P, 3, G, TAPS - 1 + N])
        c_ = sb("c", [P, 2, 3, G, N])
        xs = sb("xs", [P, 3, S])
        Bt, Ct = sb("Bt", [DS, S]), sb("Ct", [DS, S])
        xh = sb("xh", [P, T, DI])
        xdt = sb("xdt", [P, 2, T, DI])
        xD = sb("xD", [P, 2, T, DI])
        Gm = sb("Gm", [P, G, NB])
        dec = sb("dec", [P, G, HEADS, NB])
        W = sb("W", [P, 2, G, HEADS, NB])
        zz = sb("zz", [P, 2, T, DI])
        y1 = sb("y1", [P, T, DI])
        y2 = sb("y2", [P, 2, T, DI])
        sq = sb("sq", [P, 2, DI])
        ss, ms, rs = sb("ss", [P, T]), sb("ms", [P, T]), sb("rs", [P, T])
        half_rs = sb("half_rs", [P, 2, T])
        yT = sb("yT", [P, 2, S])
        banks = [ph.psum(f"bank{k}", [P, S]) for k in range(1)]
        p_x0 = banks[0]
        p_x12 = ph.psum("p_x12", [P, 2, S])
        p_z = ph.psum("p_z", [P, T, DI])
        p_xh = ph.psum("p_xh", [P, T, DI])
        p_o = ph.psum("p_o", [P, S])
        p_yT = p_xh[:].rearrange("p t d -> p (t d)").rearrange("p (c n) -> p c n", c=2)
        p_Y = p_x12[:].rearrange("p a b -> p (a b)").rearrange("p (t d) -> p t d", t=T)
        p_G = (p_o[:, 0:NB], p_x0[:, 0:NB])
        p_x = (p_x0[:], p_x12[:, 0, :], p_x12[:, 1, :])

        names = ("loaded consts w2_done w2_ready tab_ready x_done x_taken taps silu_in tanh_ready silu_ready z_done tz_ready "
                 "zz_ready xh_done xh_ready xdt_ready xD_ready G_done Gm_ready diag_ready off_ready dec_ready W_ready Y_done "
                 "y1_ready y2_ready ss_ready ms_ready rs_ready hrs_ready yT_done yT_ready out_done x_updated")
        q = {s: sem(s) for s in names.split()}
        arrived = [sem(f"arrived{p}") for p in range(2)]
        block = ctx.enter_context(nc.Block())

        @block.sync
        def _(sp):
            for dst, src in ((w_in[:], w["W_in_zx"]), (w_outT[:], w["W_outT"]), (w_lin[:], w["W_lin"]), (vecs[:], w["mamba_vecs"]),
                             (half_D[:], spread(w["D"])), (mask[:], w["mask"])):
                sp.dma_start(dst, src).then_inc(q["loaded"], 16)

            def body(s):
                if s.live():
                    hold(sp, q["z_done"], s.t - 1)
                    hold(sp, q["diag_ready"], 16 * (s.t - 1))
                    hold(sp, q["off_ready"], 8 * (s.t - 1))
                    sp.dma_start(xT[:, s.p], XT[:, bass.ts(s.t, S)]).then_inc(arrived[s.p], 16)
                    src = cum_dram[:, bass.ts(s.t, S)]
                    sp.dma_start(cum[:, s.p], src.partition_broadcast(P)).then_inc(arrived[s.p], 16)
            run_steps(sp, body, 1)

        @block.gpsimd
        def _(pool):
            pool.memset(minus_half[:], -0.5).then_inc(q["consts"], 1)
            pool.memset(xp[:], 0.0).then_inc(q["consts"], 1)
            pool.wait_ge(q["loaded"], 16 * 6)
            pool.tensor_scalar(half_D[:], half_D[:], 0.5, None, ALU.mult).then_inc(q["consts"], 1)
            pool.wait_ge(q["consts"], 3)

            def body(s):
                m, y = s.back(1), s.back(3)
                if s.live():
                    hold(pool, q["dec_ready"], s.t - 1)
                    hold(pool, q["xdt_ready"], s.t - 1)
                    pool.tensor_copy(tab[:, s.p], table[:, bass.ts(s.t, T)]).then_inc(q["tab_ready"], 1)
                if y.live():
                    need(pool, q["zz_ready"], y.t + 1)
                    need(pool, q["yT_done"], y.t - 1)
                    need(pool, q["y1_ready"], y.t + 1)
                    pool.tensor_tensor(y2[:, y.p], y1[:], zz[:, y.p], ALU.mult).then_inc(q["y2_ready"], 1)
                if m.live():
                    need(pool, q["Y_done"], m.t - 1)
                    need(pool, q["tab_ready"], m.t + 1)
                    need(pool, q["xh_ready"], m.t + 1)
                    xh4 = xh[:].rearrange("p t (h d) -> p t h d", h=HEADS)
                    half_dt = tab[:, m.p, :, HALF_DT, :].rearrange("p t (h a) -> p t h a", a=1).broadcast_to([P, T, HEADS, HD])
                    pool.tensor_tensor(xdt[:, m.p].rearrange("p t (h d) -> p t h d", h=HEADS), xh4, half_dt, ALU.mult).then_inc(q["xdt_ready"], 1)
                    need(pool, q["y1_ready"], m.t - 1)
                    for j in range(T):
                        hD = half_D[:].rearrange("p (h a) -> p h a", a=1).broadcast_to([P, HEADS, HD])
                        pool.tensor_tensor(xD[:, m.p, j].rearrange("p (h d) -> p h d", h=HEADS), xh4[:, j], hD, ALU.mult).then_inc(q["xD_ready"], 1)
                    need(pool, q["dec_ready"], m.t + 1)
                    need(pool, q["Gm_ready"], 2 * (m.t + 1))
                    g1 = Gm[:, 1].rearrange("p (a n) -> p a n", a=1).broadcast_to([P, HEADS, NB])
                    pool.tensor_tensor(W[:, m.p, 1], dec[:, 1], g1, ALU.mult).then_inc(q["W_ready"], 1)
                if y.live():
                    need(pool, q["rs_ready"], y.t)
                    hold(pool, q["ss_ready"], T * (y.t + 1))
                    pool.tensor_scalar(ms[:], ss[:], 1.0 / (4 * DI), EPS, ALU.mult, ALU.add).then_inc(q["ms_ready"], 1)
                    need(pool, q["hrs_ready"], y.t)
                    need(pool, q["ms_ready"], y.t + 1)
                    pool.tensor_tensor(rs[:], ms[:], minus_half[:], ALU.pow).then_inc(q["rs_ready"], 1)
                    need(pool, q["x_updated"], T * (y.t - 1))
                    hold(pool, q["rs_ready"], y.t + 1)
                    pool.tensor_scalar(half_rs[:, y.p], rs[:], 0.5, None, ALU.mult).then_inc(q["hrs_ready"], 1)
            run_steps(pool, body, 3)

        @block.scalar
        def _(act):
            act.preload_act_table(ACT.Exp)
            act.wait_ge(q["loaded"], 16 * 6)
            act.wait_ge(q["consts"], 3)
            act.wait_ge(q["w2_done"], 1)
            for k in range(2):
                act.activation(w_out[:, k, :], p_z[:, k, 0:P], ACT.Copy, scale=vecs[:, 15 + k:16 + k]).then_inc(q["w2_ready"], 1)

            def body(s):
                m, y, o = s.back(1), s.back(3), s.back(4)
                if o.live():
                    need(act, q["out_done"], o.t)
                    need(act, q["yT_done"], o.t + 1)
                    act.activation(yT[:], p_yT, ACT.Copy).then_inc(q["yT_ready"], 1)
                if s.live():
                    need(act, q["silu_ready"], 3 * (s.t - 1))
                    need(act, q["taps"], 9 * s.t)
                    for k in range(3):
                        act.wait_ge(q["x_done"], 3 * s.t + k + 1)
                        px = p_x[k].rearrange("p (g n) -> p g n", g=G)
                        act.activation(xp[:, k, :, TAPS - 1:], px, ACT.Copy).then_inc(q["x_taken"], 1)
                        last_tap = k * TAPS + TAPS - 1
                        act.activation(c_[:, s.p, k], px, ACT.Identity, scale=vecs[:, last_tap:last_tap + 1],
                                       bias=vecs[:, 3 * TAPS + k:3 * TAPS + k + 1]).then_inc(q["x_taken"], 1)
                if m.live():
                    act.wait_ge(arrived[m.p], 32 * (m.u + 1))
                    need(act, q["W_ready"], 2 * m.t)
                    act.wait_ge(q["tab_ready"], m.t + 1)
                    for g in range(G):
                        for h in range(HEADS):
                            act.activation(dec[:, g, h, P:2 * P], cum[:, m.p, h, g * N + P:(g + 1) * N], ACT.Exp,
                                           bias=tab[:, m.p, 2 * g, OFF, h:h + 1]).then_inc(q["off_ready"], 1)
                    act.wait_ge(q["diag_ready"], 16 * (m.t + 1))
                    diag = dec[:].rearrange("p g h (b n) -> p (g h) b n", b=3)[:, :, 0:3:2, :]
                    act.activation(diag, diag, ACT.Exp).then_inc(q["dec_ready"], 1)
                    need(act, q["z_done"], m.t + 1)
                    need(act, q["y2_ready"], m.t - 1)
                    act.activation(zz[:, m.p], p_z[:], ACT.Tanh, scale=0.5).then_inc(q["tz_ready"], 1)
                    need(act, q["xdt_ready"], m.t)
                    need(act, q["xD_ready"], T * m.t)
                    need(act, q["xh_done"], m.t + 1)
                    act.activation(xh[:], p_xh[:], ACT.Copy).then_inc(q["xh_ready"], 1)
                if y.live():
                    need(act, q["ms_ready"], y.t)
                    need(act, q["y2_ready"], y.t + 1)
                    for j in range(T):
                        need(act, q["ss_ready"], T * y.t + j - 1)
                        act.activation(sq[:, j % 2], y2[:, y.p, j], ACT.Square, accum_out=ss[:, j:j + 1]).then_inc(q["ss_ready"], 1)
                if s.live():
                    act.wait_ge(q["taps"], 9 * (s.t + 1))
                    act.activation(xs[:], c_[:, s.p].rearrange("p k g n -> p k (g n)"), ACT.Tanh, scale=0.5).then_inc(q["tanh_ready"], 1)
            run_steps(act, body, 4)

        @block.vector
        def _(dve):
            dve.wait_ge(q["loaded"], 16 * 6)
            dve.wait_ge(q["consts"], 3)

            def body(s):
                m, v, o = s.back(1), s.back(2), s.back(4)
                if m.live():
                    dve.wait_ge(arrived[m.p], 32 * (m.u + 1))
                    need(dve, q["W_ready"], 2 * m.t)
                    dve.wait_ge(q["tab_ready"], m.t + 1)
                    for g in range(G):
                        for b in range(2):
                            for h in range(HEADS):
                                l0 = g * N + b * P
                                dve.tensor_scalar(dec[:, g, h, 2 * b * P:(2 * b + 1) * P], cum[:, m.p, h, l0:l0 + P],
                                                  tab[:, m.p, 2 * g + b, CUM, h:h + 1], 0.0, ALU.subtract, ALU.min).then_inc(q["diag_ready"], 1)
                if o.live():
                    need(dve, q["hrs_ready"], o.t + 1)
                    dve.wait_ge(q["out_done"], o.t + 1)
                    for j in range(T):
                        xt = X[:, o.t * T + j, :]
                        dve.scalar_tensor_tensor(out=xt, in0=p_o[:, j * P:(j + 1) * P], scalar=half_rs[:, o.p, j:j + 1], in1=xt,
                                                 op0=ALU.mult, op1=ALU.add).then_inc(q["x_updated"], 1)
                if s.live():
                    for n, tap in enumerate(range(TAPS - 1)):
                        for k in range(3):
                            if n == 0:
                                dve.wait_ge(q["x_taken"], 6 * s.t + 2 * (k + 1))
                            else:
                                dve.wait_ge(q["taps"], 9 * s.t + 3 * (n - 1) + k + 1)
                            dve.scalar_tensor_tensor(out=c_[:, s.p, k], in0=xp[:, k, :, tap:tap + N], scalar=vecs[:, k * TAPS + tap:k * TAPS + tap + 1],
                                                     in1=c_[:, s.p, k], op0=ALU.mult, op1=ALU.add).then_inc(q["taps"], 1)
                if m.live():
                    dve.wait_ge(q["tz_ready"], m.t + 1)
                    dve.scalar_tensor_tensor(out=zz[:, m.p].rearrange("p t d -> p (t d)"), in0=zz[:, m.p].rearrange("p t d -> p (t d)"), scalar=1.0,
                                             in1=p_z[:].rearrange("p t d -> p (t d)"), op0=ALU.add, op1=ALU.mult).then_inc(q["zz_ready"], 1)
                    need(dve, q["W_ready"], 2 * m.t)
                    dve.wait_ge(q["G_done"], m.t + 1)
                    for g in range(G):
                        dve.scalar_tensor_tensor(out=Gm[:, g], in0=p_G[g], scalar=0.25, in1=mask[:], op0=ALU.mult, op1=ALU.mult).then_inc(q["Gm_ready"], 1)
                    dve.wait_ge(q["dec_ready"], m.t + 1)
                    need(dve, q["Y_done"], m.t - 1)
                    dve.wait_ge(q["Gm_ready"], 2 * m.t + 1)
                    g0 = Gm[:, 0].rearrange("p (a n) -> p a n", a=1).broadcast_to([P, HEADS, NB])
                    dve.tensor_tensor(W[:, m.p, 0], dec[:, 0], g0, ALU.mult).then_inc(q["W_ready"], 1)
                if v.live():
                    need(dve, q["xD_ready"], T * (v.t + 1))
                    need(dve, q["y2_ready"], v.t)
                    need(dve, q["Y_done"], v.t + 1)
                    dve.tensor_tensor(y1[:], p_Y, xD[:, v.p], ALU.add).then_inc(q["y1_ready"], 1)
                if s.live():
                    need(dve, q["xh_done"], s.t)
                    need(dve, q["G_done"], s.t)
                    dve.wait_ge(q["tanh_ready"], s.t + 1)
                    cc = c_[:, s.p].rearrange("p k g n -> p k (g n)")
                    dve.scalar_tensor_tensor(out=Bt[:], in0=xs[0:DS, 2, :], scalar=1.0, in1=cc[0:DS, 2, :], op0=ALU.add, op1=ALU.mult).then_inc(q["silu_ready"], 1)
                    dve.scalar_tensor_tensor(out=Ct[:], in0=xs[DS:P, 2, :], scalar=1.0, in1=cc[DS:P, 2, :], op0=ALU.add, op1=ALU.mult).then_inc(q["silu_ready"], 1)
                    dve.scalar_tensor_tensor(out=xs[:, 0:2, :], in0=xs[:, 0:2, :], scalar=1.0, in1=cc[:, 0:2, :], op0=ALU.add, op1=ALU.mult).then_inc(q["silu_ready"], 1)
            run_steps(dve, body, 4)

        @block.tensor
        def _(pe):
            pe.wait_ge(q["loaded"], 16 * 6)
            for k in range(2):
                last = pe.matmul(p_z[:, k, 0:P], w_outT[:, k * P:(k + 1) * P], w_lin[:], start=True, stop=True)
            last.then_inc(q["w2_done"], 1)
            pe.wait_ge(q["w2_ready"], 2)

            def body(s):
                m, v, o = s.back(1), s.back(2), s.back(4)
                if o.live():
                    need(pe, q["xh_ready"], o.t + 3) if v.live() else None
                    need(pe, q["yT_ready"], o.t)
                    need(pe, q["y2_ready"], o.t + 1)
                    for k in range(2):
                        for j in range(T):
                            last = pe.transpose(p_yT[:, k, j * P:(j + 1) * P], y2[:, o.p, j, k * P:(k + 1) * P], eye[:])
                    last.then_inc(q["yT_done"], 1)
                if m.live():
                    need(pe, q["zz_ready"], m.t)
                    for j in range(T):
                        last = pe.matmul(p_z[:, j, :], xT[:, m.p, j * P:(j + 1) * P], w_in[:, 0:DI], start=True, stop=True)
                    last.then_inc(q["z_done"], 1)
                if o.live():
                    need(pe, q["Gm_ready"], 2 * (o.t + 3)) if v.live() else None
                    if not m.live():
                        need(pe, q["x_updated"], T * o.t)
                    pe.wait_ge(q["yT_ready"], o.t + 1)
                    for j in range(T):
                        for k in range(2):
                            last = pe.matmul(p_o[:, j * P:(j + 1) * P], yT[:, k, j * P:(j + 1) * P], w_out[:, k, :], start=k == 0, stop=k == 1)
                    last.then_inc(q["out_done"], 1)
                if s.live():
                    need(pe, q["Gm_ready"], 2 * (s.t - 1))
                    need(pe, q["y1_ready"], s.t - 2)
                    need(pe, q["x_taken"], 6 * s.t)
                    pe.wait_ge(arrived[s.p], 32 * (s.u + 1))
                    for k in range(3):
                        pe.matmul(p_x[k], w_in[:, DI + k * P:DI + (k + 1) * P], xT[:, s.p], start=True, stop=True).then_inc(q["x_done"], 1)
                if m.live():
                    need(pe, q["yT_ready"], m.t - 2)
                    pe.wait_ge(q["silu_ready"], 3 * (m.t + 1))
                    for j in range(T):
                        for k in range(2):
                            last = pe.transpose(p_xh[:, j, k * P:(k + 1) * P], xs[:, k, j * P:(j + 1) * P], eye[:])
                    last.then_inc(q["xh_done"], 1)
                if v.live():
                    if s.live():
                        pe.wait_ge(q["x_taken"], 6 * (s.t + 1))
                    need(pe, q["y1_ready"], v.t)
                    pe.wait_ge(q["W_ready"], 2 * (v.t + 1))
                    pe.wait_ge(q["xdt_ready"], v.t + 1)
                    for g in range(G):
                        for h in range(HEADS):
                            hs = slice(h * HD, (h + 1) * HD)
                            Wh = W[:, v.p, g, h]
                            pe.matmul(p_Y[:, 2 * g, hs], Wh[:, 0:P], xdt[:, v.p, 2 * g, hs], start=True, stop=True)
                            pe.matmul(p_Y[:, 2 * g + 1, hs], Wh[:, P:2 * P], xdt[:, v.p, 2 * g, hs], start=True, stop=False)
                            last = pe.matmul(p_Y[:, 2 * g + 1, hs], Wh[:, 2 * P:NB], xdt[:, v.p, 2 * g + 1, hs], start=False, stop=True)
                    last.then_inc(q["Y_done"], 1)
                if m.live():
                    need(pe, q["x_updated"], T * (m.t - 2))
                    if s.live():
                        pe.wait_ge(q["x_taken"], 6 * s.t + 2)
                    for g in range(G):
                        l0 = g * N
                        pe.matmul(p_G[g][:, 0:N], Bt[:, l0:l0 + P], Ct[:, l0:l0 + N], start=True, stop=True)
                        last = pe.matmul(p_G[g][:, N:NB], Bt[:, l0 + P:l0 + N], Ct[:, l0 + P:l0 + N], start=True, stop=True)
                    last.then_inc(q["G_done"], 1)
            run_steps(pe, body, 4)


def graph_phase(nc, w, X, adj_dram, adjT_dram, eye):
    with ExitStack() as ctx:
        ph = Phase(nc, ctx, "c_")
        sb, sem = ph.sb, ph.sem
        weight = sb("weight", [P, P])
        bias = sb("bias", [P, P])
        minus_half = sb("minus_half", [P, T])
        adj = sb("adj", [P, 2, T, N])
        adjT = sb("adjT", [P, 2, G, 2, N])
        stats, mv = sb("stats", [P, 2, T, 6]), sb("mv", [P, 2, T, 2])
        veps, rstd = sb("veps", [P, 2, T]), sb("rstd", [P, 2, T])
        xn = sb("xn", [P, 2, T, P])
        xT = sb("xT", [P, S])
        deg, deps = sb("deg", [P, T]), sb("deps", [P, T])
        dinv = sb("dinv", [P, 2, T])
        sup = sb("sup", [P, 2, T, P])
        p_xT = ph.psum("p_xT", [P, S])
        p_sup = ph.psum("p_sup", [P, S])
        p_agg = ph.psum("p_agg", [P, S])
        loaded, consts = sem("loaded"), sem("consts")
        stats_done, mv_done, veps_done, rstd_done = sem("stats_done"), sem("mv_done"), sem("veps_done"), sem("rstd_done")
        xn_ready, xT_done, xT_ready, biased = sem("xn_ready"), sem("xT_done"), sem("xT_ready"), sem("biased")
        deg_ready, deps_ready, dinv_ready = sem("deg_ready"), sem("deps_ready"), sem("dinv_ready")
        sup_done, sup_ready, agg_done, x_updated = (sem(s) for s in ("sup_done", "sup_ready", "agg_done", "x_updated"))
        adj_in = [sem(f"adj_in{p}") for p in range(2)]
        adjT_in = [sem(f"adjT_in{p}") for p in range(2)]
        block = ctx.enter_context(nc.Block())

        @block.sync
        def _(sp):
            sp.dma_start(weight[:], w["gcn_w"]).then_inc(loaded, 16)
            sp.dma_start(bias[:], spread(w["gcn_b"])).then_inc(loaded, 16)

            def body(s):
                if s.live():
                    hold(sp, deg_ready, s.t - 1)
                    sp.dma_start(adj[:, s.p], adj_dram[bass.ts(s.t, G)].rearrange("g (a n) m -> n (g a) m", n=P)).then_inc(adj_in[s.p], 16)
                    hold(sp, agg_done, s.t - 1)
                    sp.dma_start(adjT[:, s.p], adjT_dram[bass.ts(s.t, G)].rearrange("g (a m) n -> m g a n", m=P)).then_inc(adjT_in[s.p], 16)
            run_steps(sp, body, 1)

        @block.gpsimd
        def _(pool):
            pool.memset(minus_half[:], -0.5).then_inc(consts, 1)
            pool.wait_ge(consts, 1)
            pool.wait_ge(loaded, 32)

            def body(s):
                b = s.back(1)
                if s.live():
                    layer_norm_rstd(pool, s, mv, veps, minus_half, rstd, mv_done, veps_done, rstd_done, xn_ready)
                if b.live():
                    need(pool, dinv_ready, b.t)
                    hold(pool, deg_ready, b.t + 1)
                    pool.tensor_scalar(deps[:], deg[:], EPS, None, ALU.add).then_inc(deps_ready, 1)
                    need(pool, x_updated, T * (b.t - 1))
                    need(pool, deps_ready, b.t + 1)
                    pool.tensor_tensor(dinv[:, b.p], deps[:], minus_half[:], ALU.pow).then_inc(dinv_ready, 1)
                    hold(pool, xn_ready, T * (b.t + 1))
                    xt = X[:, bass.ts(b.t, T), :]
                    bb = bias[:].rearrange("p (a d) -> p a d", a=1).broadcast_to([P, T, P])
                    pool.tensor_tensor(xt, xt, bb, ALU.add).then_inc(biased, 1)
            run_steps(pool, body, 1)

        @block.scalar
        def _(act):
            act.preload_act_table(ACT.Exp)

            def body(s):
                b = s.back(1)
                if b.live():
                    act.wait_ge(dinv_ready, b.t + 1)
                    need(act, agg_done, b.t - 1)
                    act.wait_ge(sup_done, b.t + 1)
                    for j in range(T):
                        act.activation(sup[:, b.p, j], p_sup[:, j * P:(j + 1) * P], ACT.Copy, scale=dinv[:, b.p, j:j + 1]).then_inc(sup_ready, 1)
                if s.live():
                    need(act, sup_done, s.t)
                    need(act, xT_done, s.t + 1)
                    act.activation(xT[:], p_xT[:], ACT.Copy).then_inc(xT_ready, 1)
            run_steps(act, body, 1)

        @block.vector
        def _(dve):
            def body(s):
                a, c = s.back(1), s.back(3)
                if s.live():
                    layer_norm_stats(dve, X, s, stats, mv, stats_done, mv_done)
                if a.live():
                    need(dve, xT_done, a.t - 1)
                    layer_norm_apply(dve, X, a, xn[:, a.p], mv, rstd, rstd_done, xn_ready)
                if a.live():
                    need(dve, deps_ready, a.t)
                    dve.wait_ge(adj_in[a.p], 16 * (a.u + 1))
                    dve.tensor_reduce(deg[:], adj[:, a.p], AX.X, ALU.add).then_inc(deg_ready, 1)
                if c.live():
                    need(dve, biased, c.t + 1)
                    need(dve, agg_done, c.t + 1)
                    for j in range(T):
                        xt = X[:, c.t * T + j, :]
                        dve.scalar_tensor_tensor(out=xt, in0=p_agg[:, j * P:(j + 1) * P], scalar=dinv[:, c.p, j:j + 1], in1=xt,
                                                 op0=ALU.mult, op1=ALU.add).then_inc(x_updated, 1)
            run_steps(dve, body, 3)

        @block.tensor
        def _(pe):
            pe.wait_ge(loaded, 32)

            def body(s):
                b, c = s.back(1), s.back(2)
                if c.live():
                    need(pe, x_updated, T * c.t)
                    need(pe, adjT_in[c.p], 16 * (c.u + 1))
                    need(pe, sup_ready, T * (c.t + 1))
                    for j in range(T):
                        for a in range(2):
                            n0 = (j % 2) * P
                            last = pe.matmul(p_agg[:, j * P:(j + 1) * P], adjT[:, c.p, j // 2, a, n0:n0 + P], sup[:, c.p, 2 * (j // 2) + a], start=a == 0, stop=a == 1)
                    last.then_inc(agg_done, 1)
                if b.live():
                    need(pe, sup_ready, T * b.t)
                    need(pe, xT_ready, b.t + 1)
                    for j in range(T):
                        last = pe.matmul(p_sup[:, j * P:(j + 1) * P], xT[:, j * P:(j + 1) * P], weight[:], start=True, stop=True)
                    last.then_inc(sup_done, 1)
                if s.live():
                    need(pe, xT_ready, s.t)
                    need(pe, xn_ready, T * (s.t + 1))
                    for j in range(T):
                        last = pe.transpose(p_xT[:, j * P:(j + 1) * P], xn[:, s.p, j, :], eye[:])
                    last.then_inc(xT_done, 1)
            run_steps(pe, body, 2)


BF16 = mybir.dt.bfloat16
I32 = mybir.dt.int32
EX = 8
TOPK = 2
H = 341
HP = H + 1
CH = [(0, P), (P, P), (2 * P, H - 2 * P)]
SLOTS = TOPK * NT + EX
MEMBERS = [(j, k) for j in range(T) for k in range(TOPK)]
MEM = len(MEMBERS)
QUAD = 4
NO_ROW = 1 << 20


def route_phase(nc, w, X, gate, gather_rows, scatter_rows, tile_expert, xn_dram, eye):
    with ExitStack() as ctx:
        ph = Phase(nc, ctx, "r_")
        sb, sem = ph.sb, ph.sem
        router = sb("router", [P, EX])
        rev = sb("rev", [P, EX])
        before = sb("before", [P, P])
        ones = sb("ones", [P, P])
        tile_no = sb("tile_no", [P, NT])
        part_no = sb("part_no", [P, 1])
        slot_iota = sb("slot_iota", [P, SLOTS])
        slot_bf = sb("slot_bf", [P, SLOTS], BF16)
        row_bf = sb("row_bf", [P, P], BF16)
        minus_half = sb("minus_half", [P, T])
        stats, mv = sb("stats", [P, 2, T, 6]), sb("mv", [P, 2, T, 2])
        veps, rstd = sb("veps", [P, 2, T]), sb("rstd", [P, 2, T])
        xn = sb("xn", [P, 2, T, P])
        xT = sb("xT", [P, 2, S])
        full = [P, NT, EX]
        logits, hot1, hot2, work, work2, both = (sb(s, full) for s in ("logits", "hot1", "hot2", "work", "work2", "both"))
        m1, m2, f1, z, rz, e2, p2, den, gsum = (sb(s, [P, NT]) for s in ("m1", "m2", "f1", "z", "rz", "e2", "p2", "den", "gsum"))
        total = sb("total", [P, EX, NT])
        upto = sb("upto", [P, EX, NT])
        pos = sb("pos", [P, NT, EX])
        padded = sb("padded", [P, EX])
        padded_i = sb("padded_i", [P, EX], I32)
        ends = sb("ends", [P, EX])
        dest = sb("dest", [P, TOPK, NT])
        dest_i, tile_i = sb("dest_i", [P, TOPK, NT], I32), sb("tile_i", [P, TOPK, NT], I32)
        dest_tile, dest_row = sb("dest_tile", [P, TOPK, NT]), sb("dest_row", [P, TOPK, NT])
        tile_k = sb("tile_k", [P, TOPK, NT])
        slot_hot = sb("slot_hot", [P, 2, MEM, SLOTS], BF16)
        B = sb("B", [P, 2, MEM, P], BF16)
        A = sb("A", [P, 2, 2, MEM, SLOTS], BF16)
        hi_no, lo_no = sb("hi_no", [P, SLOTS]), sb("lo_no", [P, SLOTS])
        row_f, off_f, exp_f = sb("row_f", [P, SLOTS]), sb("off_f", [P, SLOTS]), sb("exp_f", [P, SLOTS])
        p_xT = ph.psum("p_xT", [P, S])
        p_log = ph.psum("p_log", [P, T, EX])
        p_rank = ph.psum("p_rank", full)
        p_total = ph.psum("p_total", full)
        p_inv = ph.psum("p_inv", [P, 2, SLOTS])
        names = ("consts stats_done mv_done veps_done rstd_done xn_ready xT_done xT_ready log_done log_ready chain ex_ready "
                 "ranked hot_ready B_ready A_hi_ready A_lo_ready inv_done")
        q = {s: sem(s) for s in names.split()}
        written = [sem(f"written{p}") for p in range(2)]
        block = ctx.enter_context(nc.Block())

        @block.sync
        def _(sp):
            for dst, src in ((router[:], w["routerT"]), (rev[:], spread(w["rev8"])), (before[:], w["before"]), (tile_no[:], spread(w["tile_no"])),
                             (part_no[:], column(w["part_no"])), (slot_iota[:], spread(w["slot_iota"]))):
                sp.dma_start(dst, src).then_inc(q["consts"], 16)
            sp.dma_start(tile_k[:, 0, :], spread(w["tile_no"])).then_inc(q["consts"], 16)

            def body(s):
                if s.live():
                    hold(sp, q["xn_ready"], T * (s.t + 1))
                    sp.dma_start(xn_dram[bass.ts(s.t, T)].rearrange("t p d -> p t d"), xn[:, s.p]).then_inc(written[s.p], 16)
            run_steps(sp, body, 1)
            for p in range(2):
                sp.wait_ge(written[p], 16 * STEPS // 2)

        @block.gpsimd
        def _(pool):
            pool.memset(minus_half[:], -0.5).then_inc(q["consts"], 1)
            pool.memset(ones[:], 1.0).then_inc(q["consts"], 1)
            pool.iota(row_i := sb("row_i", [P, P], I32)[:], [[1, P]], base=0, channel_multiplier=0).then_inc(q["consts"], 1)
            pool.wait_ge(q["consts"], 16 * 7 + 3)
            pool.tensor_copy(row_bf[:], row_i).then_inc(q["consts"], 1)

            def body(s):
                if s.live():
                    layer_norm_rstd(pool, s, mv, veps, minus_half, rstd, q["mv_done"], q["veps_done"], q["rstd_done"], q["xn_ready"])
            run_steps(pool, body, 0)

            def invert(s):
                if s.live():
                    need(pool, q["inv_done"], s.t - 1)
                    hold(pool, q["hot_ready"], MEM * (s.t + 1))
                    pool.tensor_scalar(A[:, s.p, 1], slot_hot[:, s.p], part_no[:, 0:1], None, ALU.mult).then_inc(q["A_lo_ready"], 1)
            run_steps(pool, invert, 0)

        @block.scalar
        def _(act):
            act.preload_act_table(ACT.Exp)

            def body(s):
                b = s.back(1)
                if s.live():
                    need(act, q["log_done"], s.t - 1)
                    need(act, q["xT_done"], s.t + 1)
                    act.activation(xT[:, s.p], p_xT[:], ACT.Copy).then_inc(q["xT_ready"], 1)
                if b.live():
                    hold(act, q["log_done"], b.t + 1)
                    act.activation(logits[:, bass.ts(b.t, T), :], p_log[:], ACT.Copy).then_inc(q["log_ready"], 1)
            run_steps(act, body, 1)
            act.wait_ge(q["chain"], 2)
            act.activation(work2[:], work[:], ACT.Exp).then_inc(q["ex_ready"], 1)
            act.wait_ge(q["chain"], 9)
            act.activation(e2[:], f1[:], ACT.Exp).then_inc(q["ex_ready"], 1)

            def invert(s):
                if s.live():
                    need(act, q["inv_done"], s.t - 1)
                    hold(act, q["hot_ready"], MEM * (s.t + 1))
                    for m, (j, k) in enumerate(MEMBERS):
                        act.activation(A[:, s.p, 0, m], slot_hot[:, s.p, m], ACT.Copy, scale=tile_k[:, k, bass.ds(s.t * T + j, 1)]).then_inc(q["A_hi_ready"], 1)
            run_steps(act, invert, 0)

        @block.vector
        def _(dve):
            def body(s):
                a = s.back(1)
                if s.live():
                    layer_norm_stats(dve, X, s, stats, mv, q["stats_done"], q["mv_done"])
                if a.live():
                    need(dve, q["xT_done"], a.t - 1)
                    need(dve, written[a.p], 16 * a.u)
                    layer_norm_apply(dve, X, a, xn[:, a.p], mv, rstd, q["rstd_done"], q["xn_ready"])
            run_steps(dve, body, 1)

            n = [0]

            def then(ins):
                n[0] += 1
                ins.then_inc(q["chain"], 1)
                dve.wait_ge(q["chain"], n[0])

            def wide(v):
                return v.rearrange("p (t a) -> p t a", a=1).broadcast_to(full)
            revw = rev[:].rearrange("p (a e) -> p a e", a=1).broadcast_to(full)

            def first_best(value, best, hot):
                then(dve.tensor_tensor(hot[:], value, wide(best), ALU.is_equal))
                then(dve.tensor_tensor(hot[:], hot[:], revw, ALU.mult))
                then(dve.tensor_reduce(gsum[:], hot[:], AX.X, ALU.max))
                then(dve.tensor_tensor(hot[:], hot[:], wide(gsum[:]), ALU.is_equal))

            dve.wait_ge(q["consts"], 16 * 7 + 4)
            dve.wait_ge(q["log_ready"], STEPS)
            then(dve.tensor_reduce(m1[:], logits[:], AX.X, ALU.max))
            then(dve.tensor_tensor(work[:], logits[:], wide(m1[:]), ALU.subtract))
            first_best(logits[:], m1[:], hot1)
            then(dve.scalar_tensor_tensor(out=both[:], in0=hot1[:], scalar=-3.0e38, in1=logits[:], op0=ALU.mult, op1=ALU.add))
            then(dve.tensor_reduce(m2[:], both[:], AX.X, ALU.max))
            then(dve.tensor_tensor(f1[:], m2[:], m1[:], ALU.subtract))
            first_best(both[:], m2[:], hot2)
            then(dve.tensor_tensor(both[:], hot1[:], hot2[:], ALU.add))
            dve.wait_ge(q["ex_ready"], 2)
            then(dve.tensor_reduce(z[:], work2[:], AX.X, ALU.add))
            then(dve.reciprocal(rz[:], z[:]))
            then(dve.tensor_tensor(p2[:], e2[:], rz[:], ALU.mult))
            then(dve.scalar_tensor_tensor(out=den[:], in0=p2[:], scalar=1e-9, in1=rz[:], op0=ALU.add, op1=ALU.add))
            then(dve.reciprocal(gsum[:], den[:]))
            then(dve.tensor_tensor(gate[:, 0, :], rz[:], gsum[:], ALU.mult))
            then(dve.tensor_tensor(gate[:, 1, :], p2[:], gsum[:], ALU.mult))
            dve.wait_ge(q["ranked"], 2)
            then(dve.tensor_copy(total[:], p_total[:].rearrange("p t e -> p e t")))
            for e in range(EX):
                then(dve.tensor_tensor_scan(out=upto[:, e, :], data0=ones[:, 0:NT], data1=total[:, e, :], initial=0.0, op0=ALU.mult, op1=ALU.add))
            then(dve.tensor_scalar(padded[:], upto[:, :, NT - 1], float(P - 1), None, ALU.add))
            then(dve.tensor_copy(padded_i[:], padded[:]))
            then(dve.tensor_scalar(padded_i[:], padded_i[:], 7, 7, ALU.arith_shift_right, ALU.logical_shift_left))
            then(dve.tensor_copy(padded[:], padded_i[:]))
            then(dve.tensor_tensor_scan(out=ends[:], data0=ones[:, 0:EX], data1=padded[:], initial=0.0, op0=ALU.mult, op1=ALU.add))
            then(dve.tensor_tensor(padded[:], ends[:], padded[:], ALU.subtract))
            then(dve.tensor_tensor(upto[:], upto[:], total[:], ALU.subtract))
            first = padded[:].rearrange("p (e a) -> p e a", a=1).broadcast_to([P, EX, NT])
            then(dve.tensor_tensor(upto[:], upto[:], first, ALU.add))
            then(dve.tensor_tensor(pos[:], p_rank[:], upto[:].rearrange("p e t -> p t e"), ALU.add))
            for k, chosen in enumerate((hot1, hot2)):
                then(dve.tensor_tensor(work[:], chosen[:], pos[:], ALU.mult))
                then(dve.tensor_reduce(dest[:, k, :], work[:], AX.X, ALU.add))
            then(dve.tensor_copy(dest_i[:], dest[:]))
            then(dve.tensor_scalar(tile_i[:], dest_i[:], 7, None, ALU.arith_shift_right))
            then(dve.tensor_copy(dest_tile[:], tile_i[:]))
            then(dve.scalar_tensor_tensor(out=dest_row[:], in0=dest_tile[:], scalar=-float(P), in1=dest[:], op0=ALU.mult, op1=ALU.add))
            then(dve.tensor_scalar(row_f[:], slot_iota[:], float(P), None, ALU.mult))
            then(dve.tensor_scalar(exp_f[:], row_f[:], ends[:, 0:1], None, ALU.is_ge))
            for e in range(1, EX - 1):
                then(dve.scalar_tensor_tensor(out=exp_f[:], in0=row_f[:], scalar=ends[:, e:e + 1], in1=exp_f[:], op0=ALU.is_ge, op1=ALU.add))
            quad = exp_f[:].rearrange("p (u j) -> p u j", j=QUAD)
            for j in reversed(range(QUAD - 1)):
                then(dve.scalar_tensor_tensor(out=quad[:, :, j], in0=quad[:, :, j + 1], scalar=float(EX), in1=quad[:, :, j], op0=ALU.mult, op1=ALU.add))
            then(dve.tensor_copy(tile_expert[:], quad[:, :, 0]))
            then(dve.tensor_copy(slot_bf[:], slot_iota[:]))
            then(dve.tensor_scalar(tile_k[:, 1, :], tile_k[:, 0, :], float(NT), None, ALU.add))

            def invert(s):
                if s.live():
                    need(dve, q["A_hi_ready"], MEM * (s.t - 1))
                    hold(dve, q["A_lo_ready"], s.t - 1)
                    for m, (j, k) in enumerate(MEMBERS):
                        dve.tensor_scalar(slot_hot[:, s.p, m], slot_bf[:], dest_tile[:, k, bass.ds(s.t * T + j, 1)], None, ALU.is_equal).then_inc(q["hot_ready"], 1)
                    hold(dve, q["inv_done"], s.t - 1)
                    for m, (j, k) in enumerate(MEMBERS):
                        dve.tensor_scalar(B[:, s.p, m], row_bf[:], dest_row[:, k, bass.ds(s.t * T + j, 1)], None, ALU.is_equal).then_inc(q["B_ready"], 1)
            run_steps(dve, invert, 0)
            dve.wait_ge(q["inv_done"], STEPS)
            then(dve.tensor_copy(hi_no[:], p_inv[:, 0, :]))
            then(dve.tensor_copy(lo_no[:], p_inv[:, 1, :]))
            then(dve.tensor_scalar(row_f[:], hi_no[:], float(P), -float(P), ALU.mult, ALU.add))
            then(dve.tensor_tensor(row_f[:], row_f[:], lo_no[:], ALU.add))
            then(dve.tensor_scalar(off_f[:], hi_no[:], 0.0, float(NO_ROW), ALU.is_equal, ALU.mult))
            then(dve.tensor_tensor(off_f[:], off_f[:], row_f[:], ALU.add))
            then(dve.tensor_copy(scatter_rows[:], off_f[:]))
            then(dve.tensor_scalar(off_f[:], row_f[:], float(NT * P), -float(NT * P), ALU.is_ge, ALU.mult))
            then(dve.tensor_tensor(off_f[:], off_f[:], row_f[:], ALU.add))
            then(dve.tensor_scalar(off_f[:], off_f[:], 0.0, None, ALU.max))
            then(dve.tensor_copy(gather_rows[:], off_f[:]))

        @block.tensor
        def _(pe):
            pe.wait_ge(q["consts"], 16 * 7 + 4)

            def body(s):
                b = s.back(1)
                if s.live():
                    need(pe, q["xT_ready"], s.t)
                    need(pe, q["xn_ready"], T * (s.t + 1))
                    for j in range(T):
                        last = pe.transpose(p_xT[:, j * P:(j + 1) * P], xn[:, s.p, j, :], eye[:])
                    last.then_inc(q["xT_done"], 1)
                if b.live():
                    need(pe, q["log_ready"], b.t)
                    need(pe, q["xT_ready"], b.t + 1)
                    for j in range(T):
                        last = pe.matmul(p_log[:, j, :], xT[:, b.p, j * P:(j + 1) * P], router[:], start=True, stop=True)
                    last.then_inc(q["log_done"], 1)
            run_steps(pe, body, 1)
            pe.wait_ge(q["chain"], 14)
            chosen = both[:].rearrange("p t e -> p (t e)")
            pe.matmul(p_rank[:].rearrange("p t e -> p (t e)"), before[:], chosen, start=True, stop=True).then_inc(q["ranked"], 1)
            pe.matmul(p_total[:].rearrange("p t e -> p (t e)"), ones[:], chosen, start=True, stop=True).then_inc(q["ranked"], 1)

            def invert(s):
                if s.live():
                    need(pe, q["B_ready"], MEM * (s.t + 1))
                    need(pe, q["A_hi_ready"], MEM * (s.t + 1))
                    need(pe, q["A_lo_ready"], s.t + 1)
                    for m in range(MEM):
                        first = isinstance(s.t, int) and s.t == 0 and m == 0
                        last = pe.matmul(p_inv[:].rearrange("p a b -> p (a b)"), B[:, s.p, m], A[:, s.p, :, m], start=first, stop=False, skip_group_check=True)
                    last.then_inc(q["inv_done"], 1)
            run_steps(pe, invert, 0)


def expert_phase(nc, w, gather_rows, scatter_rows, tile_expert, xn_dram, y_dram, eye):
    MOD = QUAD
    GATHER, TURN, UP, TURN_G, DOWN, SCATTER = 1, 4, 5, 7, 8, 9
    with ExitStack() as ctx:
        ph = Phase(nc, ctx, "e_")
        sb, pair, sem = ph.sb, ph.pair, ph.sem
        w1, w3 = pair("w1", [P, EX, HP]), pair("w3", [P, EX, HP])
        w2 = pair("w2", [P, len(CH), EX * P])
        stage = sb("stage", [P, EX * H])
        rows_in = sb("rows_in", [P, MOD, 1], I32)
        rows_out = sb("rows_out", [P, MOD, 1], I32)
        xg = sb("xg", [P, MOD, P])
        xT = pair("xT", [P, 2, P])
        sl = sb("sl", [P, MOD, HP])
        g = sb("g", [P, MOD, HP])
        gT = pair("gT", [P, 2, len(CH), P])
        y = sb("y", [P, MOD, P])
        p_x = ph.psum("p_x", [P, S])
        p_h1, p_h3 = ([ph.psum(f"p_{n}{k}", [P, S]) for k in range(2)] for n in ("h1", "h3"))
        p_g = ph.psum("p_g", [P, len(CH), P])
        p_y = ph.psum("p_y", [P, S])
        names = ("p_g_clear w_loaded w_hi w_split in_ready out_ready x_done x_hi x_split h1_done h3_done sl_ready g_ready gT_done gT_hi "
                 "gT_split y_done y_ready")
        q = {s: sem(s) for s in names.split()}
        gathered = [sem(f"gathered{p}") for p in range(MOD)]
        scattered = [sem(f"scattered{p}") for p in range(MOD)]
        loads = [(w["w1T"], w1[:, :, 0:H], True), (w["w3T"], w3[:, :, 0:H], True)] + [(w["w2T"][r0:r0 + n], w2[:, k], False) for k, (r0, n) in enumerate(CH)]
        block = ctx.enter_context(nc.Block())

        @block.sync
        def _(sp):
            for k, (src, dst, _) in enumerate(loads):
                if k:
                    sp.wait_ge(q["w_split"], k)
                sp.dma_start(stage[0:src.shape[0], 0:src.shape[1]], src).then_inc(q["w_loaded"], 16)

        @block.gpsimd
        def _(pool):
            for part in (w1.hi, w1.lo, w3.hi, w3.lo):
                pool.memset(part[:, :, H:HP].bitcast(F32), 0.0).then_inc(q["w_hi"], 1)

            def body(s):
                i, o = s.back(GATHER), s.back(SCATTER)
                if i.live():
                    need(pool, q["in_ready"], i.t + 1)
                    hold(pool, q["x_done"], i.t - 3)
                    pool.indirect_dma_start(xg[:, i.p], None, xn_dram, bass.IndirectOffsetOnAxis(ap=rows_in[:, i.p], axis=0)).then_inc(gathered[i.p], 16)
                if o.live():
                    need(pool, q["out_ready"], o.t + 1)
                    hold(pool, q["y_ready"], o.t + 1)
                    pool.indirect_dma_start(y_dram, bass.IndirectOffsetOnAxis(ap=rows_out[:, o.p], axis=0), y[:, o.p], None,
                                            bounds_check=TOPK * NT * P - 1, oob_is_err=False).then_inc(scattered[o.p], 16)
            run_steps(pool, body, SCATTER, SLOTS, MOD)
            for p in range(MOD):
                pool.wait_ge(scattered[p], 16 * SLOTS // MOD)

        @block.scalar
        def _(act):
            act.preload_act_table(ACT.Silu)

            def body(s):
                a, b, c, d = s.back(TURN), s.back(UP), s.back(TURN_G), s.back(DOWN)
                if a.live():
                    need(act, q["h3_done"], a.t - 1)
                    need(act, q["x_done"], a.t + 1)
                    act.activation(xT.hi[:, a.p % 2], p_x[:, 0:P], ACT.Copy).then_inc(q["x_hi"], 1)
                if c.live():
                    need(act, q["y_done"], c.t - 1)
                    need(act, q["gT_done"], c.t + 1)
                    act.activation(gT.hi[:, c.p % 2], p_g[:], ACT.Copy).then_inc(q["gT_hi"], 1)
                if b.live():
                    need(act, q["g_ready"], b.t - 3)
                    need(act, q["h1_done"], b.t + 1)
                    act.activation(sl[:, b.p], p_h1[b.p % 2][:, 0:HP], ACT.Silu).then_inc(q["sl_ready"], 1)
                if d.live():
                    need(act, scattered[d.p], 16 * d.u)
                    need(act, q["y_done"], d.t + 1)
                    act.activation(y[:, d.p], p_y[:, 0:P], ACT.Copy).then_inc(q["y_ready"], 1)
            run_steps(act, body, DOWN, SLOTS, MOD)

        @block.vector
        def _(dve):
            dve.memset(p_g[:], 0.0).then_inc(q["p_g_clear"], 1)
            for k, (src, dst, wide) in enumerate(loads):
                n, width = src.shape
                from_ = stage[0:n, 0:width]
                if wide:
                    from_ = from_.rearrange("p (e h) -> p e h", e=EX)
                dve.wait_ge(q["w_loaded"], 16 * (k + 1))
                dve.tensor_copy(dst.hi[0:n], from_).then_inc(q["w_hi"], 1)
                dve.wait_ge(q["w_hi"], 4 + k + 1)
                dve.tensor_tensor(dst.lo[0:n], from_, dst.hi[0:n].bitcast(F32), ALU.subtract).then_inc(q["w_split"], 1)

            def body(s):
                a, b, c, d = s.back(TURN), s.back(UP), s.back(TURN_G), s.back(DOWN)
                if s.live():
                    need(dve, gathered[s.p], 16 * s.u)
                    dve.tensor_copy(rows_in[:, s.p], gather_rows[:, bass.ds(s.t, 1)]).then_inc(q["in_ready"], 1)
                if a.live():
                    need(dve, q["h3_done"], a.t - 1)
                    need(dve, q["x_hi"], a.t + 1)
                    dve.tensor_tensor(xT.lo[:, a.p % 2], p_x[:, 0:P], xT.hi[:, a.p % 2].bitcast(F32), ALU.subtract).then_inc(q["x_split"], 1)
                if c.live():
                    need(dve, q["y_done"], c.t - 1)
                    need(dve, q["gT_hi"], c.t + 1)
                    dve.tensor_tensor(gT.lo[:, c.p % 2], p_g[:], gT.hi[:, c.p % 2].bitcast(F32), ALU.subtract).then_inc(q["gT_split"], 1)
                if b.live():
                    need(dve, q["gT_done"], b.t - 3)
                    need(dve, q["h3_done"], b.t + 1)
                    need(dve, q["sl_ready"], b.t + 1)
                    dve.tensor_tensor(g[:, b.p], sl[:, b.p], p_h3[b.p % 2][:, 0:HP], ALU.mult).then_inc(q["g_ready"], 1)
                if d.live():
                    need(dve, scattered[d.p], 16 * d.u)
                    dve.tensor_copy(rows_out[:, d.p], scatter_rows[:, bass.ds(d.t, 1)]).then_inc(q["out_ready"], 1)
            run_steps(dve, body, DOWN, SLOTS, MOD)

        @block.tensor
        def _(pe):
            pe.wait_ge(q["w_split"], len(loads))
            pe.wait_ge(q["w_hi"], 4 + len(loads))
            pe.wait_ge(q["p_g_clear"], 1)
            up_word, down_word = pe.alloc_register("up_word"), pe.alloc_register("down_word")

            def expert_of(word, p):
                return pe.snap((pe.snap(word) // EX ** p) % EX, min_val=0, max_val=EX - 1)

            def body(s):
                a, b, c, d = s.back(TURN), s.back(UP), s.back(TURN_G), s.back(DOWN)
                if a.live():
                    need(pe, q["x_split"], a.t)
                    need(pe, gathered[a.p], 16 * (a.u + 1))
                    pe.transpose(p_x[:, 0:P], xg[:, a.p], eye[:]).then_inc(q["x_done"], 1)
                if c.live():
                    need(pe, q["gT_split"], c.t)
                    need(pe, q["g_ready"], c.t + 1)
                    for k, (h0, r) in enumerate(CH):
                        last = pe.transpose(p_g[0:r, k, :], g[:, c.p, h0:h0 + r], eye[:])
                    last.then_inc(q["gT_done"], 1)
                if b.live():
                    need(pe, q["g_ready"], b.t - 1)
                    hold(pe, q["x_split"], b.t + 1)
                    if b.p == 0:
                        pe.reg_load(up_word, tile_expert[0:1, bass.ds(b.u, 1)])
                    e = expert_of(up_word, b.p)
                    for bank, wk, done in ((p_h1, w1, "h1_done"), (p_h3, w3, "h3_done")):
                        rhs = Pair(wk.hi[:].rearrange("p e h -> p (e h)"), wk.lo[:].rearrange("p e h -> p (e h)"))[:, bass.ts(e, HP)]
                        product(pe, bank[b.p % 2][:, 0:HP], xT[:, b.p % 2], rhs, True, True).then_inc(q[done], 1)
                if d.live():
                    need(pe, q["y_ready"], d.t)
                    hold(pe, q["gT_split"], d.t + 1)
                    if d.p == 0:
                        pe.reg_mov(down_word, up_word)
                    e = expert_of(down_word, d.p)
                    for k, (_, r) in enumerate(CH):
                        last = product(pe, p_y[:, 0:P], gT[0:r, d.p % 2, k], w2[0:r, k, bass.ts(e, P)], k == 0, k == len(CH) - 1)
                    last.then_inc(q["y_done"], 1)
            run_steps(pe, body, DOWN, SLOTS, MOD)


def combine_phase(nc, X, gate, y_dram, out_dram):
    with ExitStack() as ctx:
        ph = Phase(nc, ctx, "o_")
        sb, sem = ph.sb, ph.sem
        y = sb("y", [P, 2, TOPK, T, P])
        y_in = [sem(f"y_in{p}") for p in range(2)]
        written = [sem(f"written{p}") for p in range(2)]
        summed = sem("summed")
        block = ctx.enter_context(nc.Block())

        @block.sync
        def _(sp):
            def body(s):
                if s.live():
                    hold(sp, summed, TOPK * T * (s.t - 1))
                    for k in range(TOPK):
                        sp.dma_start(y[:, s.p, k], y_dram[bass.ds(k * NT * P + s.t * S, S)].rearrange("(t p) d -> p t d", p=P)).then_inc(y_in[s.p], 16)
            run_steps(sp, body, 1)

        @block.scalar
        def _(act):
            def body(s):
                if s.live():
                    hold(act, summed, TOPK * T * (s.t + 1))
                    act.dma_start(out_dram[bass.ts(s.t, T)].rearrange("t p d -> p t d"), X[:, bass.ts(s.t, T), :]).then_inc(written[s.p], 16)
            run_steps(act, body, 0)
            for p in range(2):
                act.wait_ge(written[p], 16 * STEPS // 2)

        @block.vector
        def _(dve):
            def body(s):
                if s.live():
                    dve.wait_ge(y_in[s.p], 32 * (s.u + 1))
                    for k in range(TOPK):
                        for j in range(T):
                            if k:
                                need(dve, summed, TOPK * T * s.t + j + 1)
                            xt = X[:, s.t * T + j, :]
                            dve.scalar_tensor_tensor(out=xt, in0=y[:, s.p, k, j], scalar=gate[:, k, bass.ds(s.t * T + j, 1)], in1=xt,
                                                     op0=ALU.mult, op1=ALU.add).then_inc(summed, 1)
            run_steps(dve, body, 0)


def build(nc, ins, out_dram, scratch):
    with ExitStack() as ctx:
        X = ctx.enter_context(nc.sbuf_tensor("x_tokens", [P, NT, P], F32))
        eye = ctx.enter_context(nc.sbuf_tensor("eye", [P, P], F32))
        eye_in = ctx.enter_context(nc.semaphore("eye_in"))
        x_dram = ins["x"].rearrange("b (t p) d -> (b t) p d", p=P)
        with nc.Block() as block:
            @block.sync
            def _(sp):
                sp.dma_start(eye[:], ins["eye"]).then_inc(eye_in, 16)
                sp.wait_ge(eye_in, 16)
        gnn_phase(nc, x_dram, ins["adjT"], ins, X, eye)
        table_ctx = ExitStack()
        with table_ctx:
            XT = table_ctx.enter_context(nc.sbuf_tensor("xT_all", [P, NT * P], F32))
            table = table_ctx.enter_context(nc.sbuf_tensor("table", [P, NT, 3, HEADS], F32))
            dt_phase(nc, ins, X, XT, table, scratch["cum"], eye)
            mamba_phase(nc, ins, X, XT, table, scratch["cum"], eye)
        graph_phase(nc, ins, X, ins["adj"], ins["adjT"], eye)
        gate = ctx.enter_context(nc.sbuf_tensor("gate", [P, TOPK, NT], F32))
        gather_rows = ctx.enter_context(nc.sbuf_tensor("gather_rows", [P, SLOTS], I32))
        scatter_rows = ctx.enter_context(nc.sbuf_tensor("scatter_rows", [P, SLOTS], I32))
        tile_expert = ctx.enter_context(nc.sbuf_tensor("tile_expert", [P, SLOTS // QUAD], I32))
        xn_tiles = scratch["xn"].rearrange("(t p) d -> t p d", p=P)
        route_phase(nc, ins, X, gate, gather_rows, scatter_rows, tile_expert, xn_tiles, eye)
        expert_phase(nc, ins, gather_rows, scatter_rows, tile_expert, scratch["xn"], scratch["y"], eye)
        combine_phase(nc, X, gate, scratch["y"], out_dram.rearrange("b (t p) d -> (b t) p d", p=P))


def kernel(x, adj, L0_gnn_w_se, L0_gnn_b_se, L0_gnn_conv1_w, L0_gnn_bn1_g, L0_gnn_bn1_b, L0_gnn_bn1_m, L0_gnn_bn1_v,
           L0_gnn_conv2_w, L0_gnn_bn2_g, L0_gnn_bn2_b, L0_gnn_bn2_m, L0_gnn_bn2_v, L0_gnn_w_msg, L0_gnn_b_msg,
           L0_gnn_w_ih, L0_gnn_b_ih, L0_gnn_w_hh, L0_gnn_b_hh, L0_ffn_W_in, L0_ffn_conv_w, L0_ffn_conv_b,
           L0_ffn_dt_bias, L0_ffn_A_log, L0_ffn_D, L0_ffn_norm_w, L0_ffn_W_out, L0_ffn_W_lin, L0_ffn_b_lin,
           L1_gnn_weight, L1_gnn_bias, L1_ffn_router_w, L1_ffn_w1, L1_ffn_w2, L1_ffn_w3):
    import numpy as np
    import concourse.bacc as bacc
    from concourse.bass_utils import run_bass_kernel_spmd

    def lay(a, *order):
        a = np.asarray(a)
        return np.ascontiguousarray(a.transpose(*order) if order else a)

    lr_const = np.zeros((64, 3), np.float32)
    for rows, col in ((slice(0, 3), (0, 0, 2)), (slice(3, 6), (0, -1, 0)), (slice(6, 9), (1, 0, -1)),
                      (slice(32, 35), (0, 0, 1)), (slice(35, 38), (1, 0, 1)), (slice(38, 41), (0, 1, 0))):
        lr_const[rows] = col
    arrays = {
        "x": lay(x), "adj": lay(adj), "adjT": lay(adj, 0, 2, 1), "eye": np.eye(P, dtype=np.float32), "lr_const": lr_const,
        "w_seT": lay(L0_gnn_w_se, 1, 0), "b_se": lay(L0_gnn_b_se),
        "conv1T": lay(np.asarray(L0_gnn_conv1_w)[:, :, 0], 1, 0),
        "conv2T": lay(L0_gnn_conv2_w, 1, 2, 0).reshape(P, -1),
        "gnn_vecs": np.stack([np.asarray(a).reshape(-1, P)[k] for a in (
            L0_gnn_bn1_g, L0_gnn_bn1_b, L0_gnn_bn1_m, L0_gnn_bn1_v, L0_gnn_bn2_g, L0_gnn_bn2_b, L0_gnn_bn2_m,
            L0_gnn_bn2_v, L0_gnn_b_ih, L0_gnn_b_hh) for k in range(np.asarray(a).size // P)], axis=1),
        "w_msgT": lay(L0_gnn_w_msg, 1, 0), "b_msg": lay(L0_gnn_b_msg),
        "w_ihT": lay(np.asarray(L0_gnn_w_ih).reshape(3 * P, 2, P), 2, 1, 0).reshape(P, -1),
        "w_hhT": lay(L0_gnn_w_hh, 1, 0),
        "w1T": lay(L1_ffn_w1, 2, 0, 1).reshape(P, -1), "w3T": lay(L1_ffn_w3, 2, 0, 1).reshape(P, -1),
        "w2T": lay(L1_ffn_w2, 2, 0, 1).reshape(H, -1), "routerT": lay(L1_ffn_router_w, 1, 0),
        "rev8": np.arange(EX, 0, -1, dtype=np.float32), "before": np.triu(np.ones((P, P), np.float32), 1),
        "tile_no": np.arange(1, NT + 1, dtype=np.float32), "part_no": np.arange(P, dtype=np.float32),
        "slot_iota": np.arange(SLOTS, dtype=np.float32),
        "gcn_w": lay(L1_gnn_weight), "gcn_b": lay(L1_gnn_bias),
        "W_in_zx": lay(np.asarray(L0_ffn_W_in)[:, :DI + XBC]), "W_dt": lay(np.asarray(L0_ffn_W_in)[:, DI + XBC:]),
        "dt_bias": lay(L0_ffn_dt_bias), "A_log": lay(L0_ffn_A_log), "D": lay(L0_ffn_D), "b_lin": lay(L0_ffn_b_lin),
        "W_outT": lay(L0_ffn_W_out, 1, 0), "W_lin": lay(L0_ffn_W_lin),
        "mamba_vecs": np.concatenate([np.asarray(L0_ffn_conv_w).reshape(3, P, TAPS).transpose(1, 0, 2).reshape(P, -1),
                                      np.asarray(L0_ffn_conv_b).reshape(3, P).T, np.asarray(L0_ffn_norm_w).reshape(2, P).T], axis=1),
        "mask": np.concatenate([np.triu(np.ones((P, P), np.float32)), np.ones((P, P), np.float32), np.triu(np.ones((P, P), np.float32))], axis=1),
    }
    nc = bacc.Bacc("TRN2", target_bir_lowering=False, num_devices=1)
    ins = {name: nc.dram_tensor(f"in_{name}", a.shape, F32, kind="ExternalInput").ap() for name, a in arrays.items()}
    out = nc.dram_tensor("out", (BS, N, P), F32, kind="ExternalOutput").ap()
    scratch = {"cum": nc.dram_tensor("cum_scratch", (HEADS, BS * N), F32, kind="Internal").ap(),
               "xn": nc.dram_tensor("xn_scratch", (NT * P, P), F32, kind="Internal").ap(),
               "y": nc.dram_tensor("y_scratch", (TOPK * NT * P, P), F32, kind="Internal").ap()}
    build(nc, ins, out, scratch)
    result = run_bass_kernel_spmd(nc, [{f"in_{name}": a for name, a in arrays.items()}], core_ids=[0])
    return result.results[0]["out"]
```

```python
from contextlib import ExitStack

import concourse.bass as bass
from concourse import mybir

F32 = mybir.dt.float32
F32R = mybir.dt.float32r
ACT = mybir.ActivationFunctionType
ALU = mybir.AluOpType
AX = mybir.AxisListType

P = 128
BS = 32
N = 256
T = 4
G = 2
S = T * P
STEPS = BS * N // S
NT = STEPS * T
EPS = 1e-5


class Step:

    def __init__(self, u, p, steps=STEPS, mod=2):
        self.u, self.p, self.t, self.steps, self.mod = u, p, mod * u + p, steps, mod

    def back(self, lag):
        q = self.p - lag
        return Step(self.u + q // self.mod, q % self.mod, self.steps, self.mod)

    def live(self):
        return not isinstance(self.t, int) or 0 <= self.t < self.steps


def run_steps(eng, body, lags, steps=STEPS, mod=2):
    head = lags // mod + 1
    for t in range(mod * head):
        body(Step(t // mod, t % mod, steps, mod))
    with eng.Fori(head, steps // mod) as u:
        for p in range(mod):
            body(Step(u, p, steps, mod))
    for t in range(steps, steps + lags):
        body(Step(t // mod, t % mod, steps, mod))


def need(eng, sem, count):
    if isinstance(count, int) and count <= 0:
        return
    eng.wait_ge(sem, count)


def hold(eng, sem, count):
    need(eng, sem, count)
    if not isinstance(count, int):
        eng.nop(nofuse=True)


class Pair:

    def __init__(self, hi, lo):
        self.hi, self.lo = hi, lo

    def __getitem__(self, k):
        return Pair(self.hi[k], self.lo[k])


def product(pe, out, lhsT, rhs, start, stop):
    pe.matmul(out, lhsT.hi, rhs.hi, start=start, stop=False)
    pe.matmul(out, lhsT.hi, rhs.lo, start=False, stop=False)
    return pe.matmul(out, lhsT.lo, rhs.hi, start=False, stop=stop)


class Phase:

    def __init__(self, nc, ctx, name):
        self.nc, self.ctx, self.name, self.sems = nc, ctx, name, []
        ctx.callback(self.clear)

    def clear(self):
        self.nc.clear_and_free_semaphores(self.sems)
        self.nc.all_engine_barrier()

    def sb(self, name, shape, dt=F32):
        return self.ctx.enter_context(self.nc.sbuf_tensor(self.name + name, shape, dt))

    def pair(self, name, shape):
        return Pair(self.sb(name + "_hi", shape, F32R), self.sb(name + "_lo", shape, F32R))

    def psum(self, name, shape):
        return self.ctx.enter_context(self.nc.psum_tensor(self.name + name, shape, F32))

    def sem(self, name):
        self.sems.append(self.nc.alloc_semaphore(name=self.name + name))
        return self.sems[-1]


def column(v):
    return v.rearrange("(p a) -> p a", a=1)


def spread(v, parts=P):
    return bass.AP(v.tensor, v.offset, [[0, parts]] + list(v.ap))


def layer_norm_stats(dve, X, s, stats, mv, stats_done, mv_done):
    for j in range(T):
        dve.bn_stats(stats[:, s.p, j, :], X[:, s.t * T + j, :]).then_inc(stats_done, 1)
    for j in range(T):
        hold(dve, stats_done, T * s.t + j + 1)
        dve.bn_aggr(mv[:, s.p, j, :], stats[:, s.p, j, :]).then_inc(mv_done, 1)


def layer_norm_rstd(pool, s, mv, veps, minus_half, rstd, mv_done, veps_done, rstd_done, xn_ready):
    need(pool, xn_ready, T * (s.t - 1))
    hold(pool, mv_done, T * (s.t + 1))
    pool.tensor_scalar(veps[:, s.p], mv[:, s.p, :, 1], EPS, None, ALU.add).then_inc(veps_done, 1)
    need(pool, veps_done, s.t + 1)
    pool.tensor_tensor(rstd[:, s.p], veps[:, s.p], minus_half[:], ALU.pow).then_inc(rstd_done, 1)


def layer_norm_apply(dve, X, s, xn, mv, rstd, rstd_done, xn_ready):
    need(dve, rstd_done, s.t + 1)
    for j in range(T):
        dve.tensor_scalar(xn[:, j, :], X[:, s.t * T + j, :], mv[:, s.p, j, 0:1], rstd[:, s.p, j:j + 1], ALU.subtract, ALU.mult).then_inc(xn_ready, 1)


def gnn_phase(nc, x_dram, adjT_dram, w, X, eye):
    TAPS = 17
    EVEN, ODD = (TAPS + 1) // 2, TAPS // 2
    PAD = TAPS // 2
    M = N // 2
    MS = M + EVEN - 1
    MP = MS + 2
    INNER = slice(PAD // 2, PAD // 2 + M)
    ME = M + 2
    L0, R0, KD = 0, 32, 9
    with ExitStack() as ctx:
        ph = Phase(nc, ctx, "g_")
        sb, pair, sem = ph.sb, ph.pair, ph.sem
        conv1 = pair("conv1", [P, P])
        conv2 = pair("conv2", [P, TAPS * P])
        tap_sums = sb("tap_sums", [P, EVEN * P])
        conv2s = pair("conv2s", [P, EVEN * P])
        w_lr = pair("w_lr", [P, 64])
        w_msg = pair("w_msg", [P, P])
        w_ih = pair("w_ih", [P, 2 * 3 * P])
        w_hh = pair("w_hh", [P, 3 * P])
        b_msg = sb("b_msg", [P, P])
        lr_cols = sb("lr_cols", [64, 3])
        vecs = sb("vecs", [P, 14])
        BN = {"g1": 0, "b1": 1, "m1": 2, "v1": 3, "g2": 4, "b2": 5, "m2": 6, "v2": 7}
        B_IH, B_HH = 8, 11
        scales = sb("scales", [P, 8])
        tmp2 = sb("tmp2", [P, 4])
        minus_half = sb("minus_half", [P, 4])
        adjT = sb("adjT", [P, 2, G, 2, N])
        stats = sb("stats", [P, 2, T, 6])
        mv = sb("mv", [P, 2, T, 2])
        veps = sb("veps", [P, 2, T])
        rstd = sb("rstd", [P, 2, T])
        xn = sb("xn", [P, T, P])
        xf = sb("xf", [P, 2, S])
        xs = pair("xs", [P, 2, S])
        h1f = sb("h1f", [P, 2, G, MP])
        h1 = pair("h1", [P, 2, G, MP])
        hsf = sb("hsf", [P, G, MS])
        hs = pair("hs", [P, G, MS])
        Bo = sb("Bo", [P, G, M])
        even, odd = sb("even", [P, G, M]), sb("odd", [P, G, M])
        t1 = sb("t1", [64, S])
        t2 = sb("t2", [64, S])
        q = sb("q", [64, S])
        right = sb("right", [KD, S])
        mb = sb("mb", [P, T, P])
        mf = sb("mf", [P, T, P])
        msg = pair("msg", [P, T, P])
        E = sb("E", [P, G, 2, N])
        Am = sb("Am", [P, G, 2, N])
        A = pair("A", [P, G, 2, N])
        v = sb("v", [P, S])
        xcf = sb("xcf", [P, S])
        xc = pair("xc", [P, S])
        nm = pair("nm", [P, S])
        gh = sb("gh", [P, S])
        tr = sb("tr", [P, S])
        tz = sb("tz", [P, S])
        n_arg = sb("n_arg", [P, S])
        tn = sb("tn", [P, S])
        xd = sb("xd", [P, S])
        zd = sb("zd", [P, S])
        hT = sb("hT", [P, S])
        p_conv2 = ph.psum("p_conv2", [P, S])
        p_sum, p_Bo = (p_conv2[:, k * G * M:(k + 1) * G * M].rearrange("p (g m) -> p g m", g=G) for k in range(2))
        p_msg = p_conv2
        p_nmp = ph.psum("p_nmp", [P, S])
        p_lr = p_nmp
        p_xT = ph.psum("p_xT", [P, S])
        p_conv1 = p_xT
        p_dist = ph.psum("p_dist", [P, G, 2, N])
        p_Ae = p_dist[:, 1].rearrange("p a n -> p (a n)")[:, 0:G * ME].rearrange("p (g m) -> p g m", g=G)
        p_back = p_dist[:, 0, :, :].rearrange("p a b -> p (a b)")
        p_r = ph.psum("p_r", [P, S])
        p_z = ph.psum("p_z", [P, S])
        p_n = ph.psum("p_n", [P, S])

        loaded, vecs_in = sem("loaded"), sem("vecs_in")
        stage_clear, w_hi, w_split_first, w_split_rest = sem("stage_clear"), sem("w_hi"), sem("w_split_first"), sem("w_split_rest")
        consts = sem("consts")
        bn_ready = sem("bn_ready")
        x_in = [sem(f"x_in{p}") for p in range(2)]
        adj_in = [sem(f"adj_in{p}") for p in range(2)]
        stats_done, mv_done, veps_done, rstd_done = sem("stats_done"), sem("mv_done"), sem("veps_done"), sem("rstd_done")
        xn_ready = sem("xn_ready")
        xT_done, x_hi_f, x_split = sem("xT_done"), sem("x_hi_f"), sem("x_split")
        pad_clear, sums_ready, hs_ready, hs_hi, hs_split, Bo_ready, conv_summed = (
            sem(s) for s in ("pad_clear", "sums_ready", "hs_ready", "hs_hi", "hs_split", "Bo_ready", "conv_summed"))
        conv1_done, h1_hi_f, h1_split = sem("conv1_done"), sem("h1_hi_f"), sem("h1_split")
        lr_done, t1_ready, t2_ready, q_ready, right_ready = (sem(s) for s in ("lr_done", "t1_ready", "t2_ready", "q_ready", "right_ready"))
        msg_done, msg_biased, msg_hi_f, msg_split = (sem(s) for s in ("msg_done", "msg_biased", "msg_hi_f", "msg_split"))
        dist_done, exp_done, masked, A_split = (sem(s) for s in ("dist_done", "exp_done", "masked", "A_split"))
        conv2_done, v_ready, xc_hi_f, xc_split = (sem(s) for s in ("conv2_done", "v_ready", "xc_hi_f", "xc_split"))
        nmp_done, nmp_hi, nmp_split = sem("nmp_done"), sem("nmp_hi"), sem("nmp_split")
        ghn_done, gh_ready, r_done, z_done, n_done = (sem(s) for s in ("ghn_done", "gh_ready", "r_done", "z_done", "n_done"))
        tr_ready, tz_ready, rg_ready, u_ready, tn_ready, d_ready, g_ready, hT_ready = (
            sem(s) for s in ("tr_ready", "tz_ready", "rg_ready", "u_ready", "tn_ready", "d_ready", "g_ready", "hT_ready"))
        back_done, x_updated = sem("back_done"), sem("x_updated")

        weights = [(w_lr, None), (conv1, w["conv1T"]), (w_msg, w["w_msgT"]), (conv2, w["conv2T"]), (w_hh, w["w_hhT"]), (w_ih, w["w_ihT"])]
        FIRST, CONV2 = 3, 3
        stages = [sb(f"stage{k}", [P, dst.hi.shape[1]]) for k, (dst, _) in enumerate(weights)]
        w_in = [sem(f"w_in{k}") for k in range(len(weights))]
        block = ctx.enter_context(nc.Block())

        @block.sync
        def _(sp):
            sp.dma_start(vecs[:], w["gnn_vecs"]).then_inc(vecs_in, 16)
            sp.dma_start(lr_cols[:], w["lr_const"]).then_inc(consts, 16)
            sp.wait_ge(stage_clear, 1)
            for at in (L0, L0 + 3, R0, R0 + 6):
                sp.dma_start(stages[0][:, at:at + 3], w["w_seT"]).then_inc(w_in[0], 16)

            def body(s):
                if s.live():
                    hold(sp, mv_done, T * (s.t - 1))
                    sp.dma_start(X[:, bass.ts(s.t, T), :], x_dram[bass.ts(s.t, T)].rearrange("t p d -> p t d")).then_inc(x_in[s.p], 16)
                    hold(sp, masked, s.t - 1)
                    sp.dma_start(adjT[:, s.p], adjT_dram[bass.ts(s.t, G)].rearrange("g (a m) n -> m g a n", m=P)).then_inc(adj_in[s.p], 16)
                if isinstance(s.t, int) and s.t == 0:
                    sp.dma_start(b_msg[:], spread(w["b_msg"])).then_inc(loaded, 16)
                    sp.wait_ge(consts, 16)
                    for row in (L0, L0 + 3, R0, R0 + 6):
                        sp.dma_start(lr_cols[row:row + 3, 0:1], column(w["b_se"])).then_inc(loaded, 16)
            run_steps(sp, body, 0)

        @block.gpsimd
        def _(pool):
            pool.memset(stages[0][:], 0.0).then_inc(stage_clear, 1)
            pool.memset(minus_half[:], -0.5).then_inc(bn_ready, 1)
            pool.memset(h1f[:], 0.0).then_inc(pad_clear, 1)
            for part in (h1.hi, h1.lo):
                pool.memset(part[:].bitcast(F32), 0.0).then_inc(bn_ready, 1)
            pool.wait_ge(vecs_in, 16)
            v_cols = vecs[:, BN["v1"]:BN["v2"] + 1:4]
            g_cols = vecs[:, BN["g1"]:BN["g2"] + 1:4]
            b_cols = vecs[:, BN["b1"]:BN["b2"] + 1:4]
            m_cols = vecs[:, BN["m1"]:BN["m2"] + 1:4]
            pool.tensor_scalar(tmp2[:, 0:2], v_cols, EPS, None, ALU.add).then_inc(bn_ready, 1)
            pool.wait_ge(bn_ready, 4)
            pool.tensor_tensor(tmp2[:, 2:4], tmp2[:, 0:2], minus_half[:, 0:2], ALU.pow).then_inc(bn_ready, 1)
            pool.wait_ge(bn_ready, 5)
            pool.tensor_tensor(scales[:, 0:2], tmp2[:, 2:4], g_cols, ALU.mult).then_inc(bn_ready, 1)
            pool.wait_ge(bn_ready, 6)
            pool.tensor_tensor(tmp2[:, 0:2], scales[:, 0:2], m_cols, ALU.mult).then_inc(bn_ready, 1)
            pool.wait_ge(bn_ready, 7)
            pool.tensor_tensor(scales[:, 2:4], b_cols, tmp2[:, 0:2], ALU.subtract).then_inc(bn_ready, 1)
            pool.tensor_tensor(scales[:, 4:6], vecs[:, B_IH:B_IH + 2], vecs[:, B_HH:B_HH + 2], ALU.add).then_inc(bn_ready, 1)
            pool.tensor_scalar(scales[:, 6:7], vecs[:, B_HH + 2:B_HH + 3], 0.5, None, ALU.mult).then_inc(bn_ready, 1)
            pool.wait_ge(bn_ready, 10)
            pool.tensor_scalar(scales[:, 4:6], scales[:, 4:6], 0.5, None, ALU.mult).then_inc(bn_ready, 1)
            pool.wait_ge(w_in[CONV2], 16)
            taps = stages[CONV2][:].rearrange("p (k d) -> p k d", k=TAPS)
            sums = tap_sums[:].rearrange("p (k d) -> p k d", k=EVEN)
            pool.tensor_tensor(sums[:, 0:ODD], taps[:, 0:2 * ODD:2], taps[:, 1:2 * ODD:2], ALU.add).then_inc(sums_ready, 1)
            pool.tensor_copy(sums[:, ODD], taps[:, 2 * ODD]).then_inc(sums_ready, 1)
            pool.wait_ge(pad_clear, 1)

            def body(s):
                a, b = s.back(1), s.back(2)
                if s.live():
                    layer_norm_rstd(pool, s, mv, veps, minus_half, rstd, mv_done, veps_done, rstd_done, xn_ready)
                if a.live():
                    need(pool, t1_ready, a.t + 1)
                    hold(pool, dist_done, a.t)
                    pool.tensor_scalar(t2[:], t1[:], lr_cols[:, 1:2], lr_cols[:, 2:3], ALU.mult, ALU.add).then_inc(t2_ready, 1)
                    pool.wait_ge(t2_ready, a.t + 1)
                    pool.tensor_tensor(q[:], t1[:], t2[:], ALU.mult).then_inc(q_ready, 1)
                    pool.wait_ge(h1_hi_f, 2 * (a.t + 1))
                    pool.tensor_tensor(hsf[:], h1f[:, 1, :, 0:MS], h1f[:, 0, :, 1:1 + MS], ALU.add).then_inc(hs_ready, 1)
                    pool.wait_ge(hs_hi, a.t + 1)
                    need(pool, conv2_done, 2 * a.t)
                    pool.tensor_tensor(hs.lo[:], hsf[:], hs.hi[:].bitcast(F32), ALU.subtract).then_inc(hs_split, 1)
                if b.live():
                    pool.wait_ge(tn_ready, b.t + 1)
                    need(pool, g_ready, b.t)
                    pool.tensor_tensor(xd[:], xf[:, b.p], tn[:], ALU.subtract).then_inc(d_ready, 1)
            run_steps(pool, body, 2)

        @block.scalar
        def _(act):
            for k, (_, src) in enumerate(weights):
                if src is not None:
                    act.dma_start(stages[k][:], src).then_inc(w_in[k], 16)
            act.preload_act_table(ACT.Exp)
            for k, (dst, src) in enumerate(weights):
                act.wait_ge(w_in[k], 16 if src is not None else 16 * 4)
                act.activation(dst.hi[:], stages[k][:], ACT.Copy).then_inc(w_hi, 1)
            act.wait_ge(sums_ready, 2)
            act.activation(conv2s.hi[:], tap_sums[:], ACT.Copy).then_inc(w_hi, 1)
            act.wait_ge(bn_ready, 11)
            act.wait_ge(loaded, 16 * 5)

            def body(s):
                b = s.back(1)
                if b.live():
                    act.wait_ge(conv2_done, 2 * b.t + 1)
                    need(act, conv_summed, 3 * b.t)
                    act.activation(Bo[:], p_Bo, ACT.Copy).then_inc(Bo_ready, 1)
                    act.wait_ge(nmp_done, b.t + 1)
                    act.activation(nm.hi[:], p_nmp[:], ACT.Copy).then_inc(nmp_hi, 1)
                if s.live():
                    act.wait_ge(xT_done, s.t + 1)
                    need(act, n_done, s.t - 1)
                    need(act, d_ready, s.t - 1)
                    act.activation(xs.hi[:, s.p], p_xT[:], ACT.Copy).then_inc(x_hi_f, 1)
                    act.activation(xf[:, s.p], p_xT[:], ACT.Copy).then_inc(x_hi_f, 1)
                if b.live():
                    act.wait_ge(v_ready, 2 * (b.t + 1))
                    need(act, n_done, b.t)
                    act.activation(xcf[:], v[:], ACT.Relu, bias=scales[:, 3:4]).then_inc(xc_hi_f, 1)
                    act.activation(xc.hi[:], v[:], ACT.Relu, bias=scales[:, 3:4]).then_inc(xc_hi_f, 1)
                if b.live():
                    act.wait_ge(ghn_done, b.t + 1)
                    need(act, rg_ready, b.t)
                    act.activation(gh[:], p_n[:], ACT.Identity, bias=scales[:, 6:7], scale=0.5).then_inc(gh_ready, 1)
                if s.live():
                    act.wait_ge(conv1_done, s.t + 1)
                    need(act, conv2_done, 2 * s.t)
                    need(act, hs_ready, s.t)
                    p1 = p_conv1[:].rearrange("p (g m e) -> p e g m", g=G, e=2)
                    for h in (h1f, h1.hi):
                        act.activation(h[:, :, :, INNER], p1, ACT.Relu, bias=scales[:, 2:3], scale=scales[:, 0:1]).then_inc(h1_hi_f, 1)
                    act.wait_ge(lr_done, s.t + 1)
                    need(act, q_ready, s.t)
                    act.activation(t1[:], p_lr[0:64, :], ACT.Identity, bias=lr_cols[:, 0:1]).then_inc(t1_ready, 1)
                    act.wait_ge(msg_biased, s.t + 1)
                    need(act, nmp_done, s.t)
                    act.activation(mf[:], mb[:], ACT.Relu).then_inc(msg_hi_f, 1)
                    act.activation(msg.hi[:], mb[:], ACT.Relu).then_inc(msg_hi_f, 1)
                    act.wait_ge(q_ready, s.t + 1)
                    need(act, dist_done, s.t)
                    act.activation(right[:], q[R0:R0 + KD, :], ACT.Copy).then_inc(right_ready, 1)
                    act.wait_ge(hs_ready, s.t + 1)
                    need(act, hs_split, s.t)
                    act.activation(hs.hi[:], hsf[:], ACT.Copy).then_inc(hs_hi, 1)
                if b.live():
                    act.wait_ge(r_done, b.t + 1)
                    need(act, rg_ready, b.t)
                    act.activation(tr[:], p_r[:], ACT.Tanh, bias=scales[:, 4:5], scale=0.5).then_inc(tr_ready, 1)
                    act.wait_ge(z_done, b.t + 1)
                    need(act, g_ready, b.t)
                    act.activation(tz[:], p_z[:], ACT.Tanh, bias=scales[:, 5:6], scale=0.5).then_inc(tz_ready, 1)
                    act.wait_ge(u_ready, b.t + 1)
                    need(act, hT_ready, b.t)
                    act.activation(tn[:], n_arg[:], ACT.Tanh, bias=vecs[:, B_IH + 2:B_IH + 3]).then_inc(tn_ready, 1)
                if s.live():
                    act.wait_ge(dist_done, s.t + 1)
                    need(act, masked, s.t)
                    act.activation(E[:], p_dist[:], ACT.Exp).then_inc(exp_done, 1)
            run_steps(act, body, 1)

        @block.vector
        def _(dve):
            def body(s):
                a, b, c = s.back(1), s.back(2), s.back(3)
                if isinstance(a.t, int) and a.t == 0:
                    for k in range(FIRST):
                        dst = weights[k][0]
                        dve.wait_ge(w_hi, k + 1)
                        dve.tensor_tensor(dst.lo[:], stages[k][:], dst.hi[:].bitcast(F32), ALU.subtract).then_inc(w_split_first, 1)
                    dve.wait_ge(bn_ready, 11)
                    dve.wait_ge(loaded, 16 * 5)
                if c.live():
                    dve.wait_ge(d_ready, c.t + 1)
                    dve.wait_ge(tz_ready, c.t + 1)
                    dve.scalar_tensor_tensor(out=zd[:], in0=tz[:], scalar=1.0, in1=xd[:], op0=ALU.add, op1=ALU.mult).then_inc(g_ready, 1)
                    dve.wait_ge(g_ready, c.t + 1)
                    need(dve, back_done, c.t)
                    dve.scalar_tensor_tensor(out=hT[:], in0=zd[:], scalar=0.5, in1=tn[:], op0=ALU.mult, op1=ALU.add).then_inc(hT_ready, 1)
                if b.live():
                    dve.wait_ge(exp_done, b.t + 1)
                    dve.wait_ge(adj_in[b.p], 16 * (b.u + 1))
                    dve.tensor_tensor(Am[:], E[:], adjT[:, b.p], ALU.mult).then_inc(masked, 1)
                    dve.wait_ge(masked, b.t + 1)
                    need(dve, nmp_done, b.t)
                    dve.tensor_copy(A.hi[:], Am[:]).then_inc(A_split, 1)
                    dve.wait_ge(A_split, 2 * b.t + 1)
                    dve.tensor_tensor(A.lo[:], Am[:], A.hi[:].bitcast(F32), ALU.subtract).then_inc(A_split, 1)
                if a.live():
                    need(dve, xT_done, a.t)
                    layer_norm_apply(dve, X, a, xn, mv, rstd, rstd_done, xn_ready)
                if s.live():
                    dve.wait_ge(x_in[s.p], 16 * (s.u + 1))
                    layer_norm_stats(dve, X, s, stats, mv, stats_done, mv_done)
                if b.live():
                    dve.wait_ge(conv2_done, 2 * (b.t + 1))
                    dve.wait_ge(Bo_ready, b.t + 1)
                    dve.tensor_tensor(even[:], p_Ae[:, :, 0:M], Bo[:], ALU.add).then_inc(conv_summed, 1)
                    dve.tensor_tensor(odd[:], p_Ae[:, :, 1:1 + M], Bo[:], ALU.add).then_inc(conv_summed, 1)
                    dve.wait_ge(conv_summed, 3 * b.t + 2)
                    dve.tensor_tensor(odd[:], p_sum, odd[:], ALU.subtract).then_inc(conv_summed, 1)
                    dve.wait_ge(x_hi_f, 2 * (b.t + 1))
                    v4, x4 = (r.rearrange("p (g m e) -> p e g m", g=G, e=2) for r in (v[:], xf[:, b.p]))
                    for e, (y, count) in enumerate(((even, 1), (odd, 3))):
                        dve.wait_ge(conv_summed, 3 * b.t + count)
                        dve.scalar_tensor_tensor(out=v4[:, e], in0=y[:], scalar=scales[:, 1:2], in1=x4[:, e], op0=ALU.mult, op1=ALU.add).then_inc(v_ready, 1)
                    dve.wait_ge(nmp_hi, b.t + 1)
                    need(dve, n_done, b.t)
                    dve.tensor_tensor(nm.lo[:], p_nmp[:], nm.hi[:].bitcast(F32), ALU.subtract).then_inc(nmp_split, 1)
                if a.live():
                    dve.wait_ge(x_hi_f, 2 * (a.t + 1))
                    need(dve, n_done, a.t - 1)
                    dve.tensor_tensor(xs.lo[:, a.p], p_xT[:], xs.hi[:, a.p].bitcast(F32), ALU.subtract).then_inc(x_split, 1)
                if isinstance(a.t, int) and a.t == 0:
                    dve.wait_ge(w_hi, len(weights) + 1)
                    for dst, src in [(weights[k][0], stages[k]) for k in range(FIRST, len(weights))] + [(conv2s, tap_sums)]:
                        dve.tensor_tensor(dst.lo[:], src[:], dst.hi[:].bitcast(F32), ALU.subtract).then_inc(w_split_rest, 1)
                if b.live():
                    dve.wait_ge(xc_hi_f, 2 * (b.t + 1))
                    dve.tensor_tensor(xc.lo[:], xcf[:], xc.hi[:].bitcast(F32), ALU.subtract).then_inc(xc_split, 1)
                if c.live():
                    dve.wait_ge(back_done, c.t + 1)
                    xt = X[:, bass.ts(c.t, T), :].rearrange("p t d -> p (t d)")
                    dve.tensor_tensor(xt, xt, p_back, ALU.add).then_inc(x_updated, 1)
                if a.live():
                    dve.wait_ge(msg_done, a.t + 1)
                    need(dve, msg_hi_f, 2 * a.t)
                    bb = b_msg[:].rearrange("p (a d) -> p a d", a=1).broadcast_to([P, T, P])
                    dve.tensor_tensor(mb[:], p_msg[:].rearrange("p (t d) -> p t d", t=T), bb, ALU.add).then_inc(msg_biased, 1)
                    dve.wait_ge(h1_hi_f, 2 * (a.t + 1))
                    dve.tensor_tensor(h1.lo[:, :, :, INNER], h1f[:, :, :, INNER], h1.hi[:, :, :, INNER].bitcast(F32), ALU.subtract).then_inc(h1_split, 1)
                    dve.wait_ge(msg_hi_f, 2 * (a.t + 1))
                    dve.tensor_tensor(msg.lo[:], mf[:], msg.hi[:].bitcast(F32), ALU.subtract).then_inc(msg_split, 1)
                if b.live():
                    dve.wait_ge(tr_ready, b.t + 1)
                    dve.wait_ge(gh_ready, b.t + 1)
                    need(dve, u_ready, b.t)
                    dve.scalar_tensor_tensor(out=v[:], in0=tr[:], scalar=1.0, in1=gh[:], op0=ALU.add, op1=ALU.mult).then_inc(rg_ready, 1)
                    dve.wait_ge(rg_ready, b.t + 1)
                    dve.wait_ge(n_done, b.t + 1)
                    need(dve, tn_ready, b.t)
                    dve.tensor_tensor(n_arg[:], v[:], p_n[:], ALU.add).then_inc(u_ready, 1)
            run_steps(dve, body, 3)

        @block.tensor
        def _(pe):
            pe.wait_ge(w_split_first, FIRST)
            pe.wait_ge(bn_ready, 11)

            def body(s):
                b, c = s.back(1), s.back(2)
                if isinstance(b.t, int) and b.t == 0:
                    pe.wait_ge(w_split_rest, len(weights) - FIRST + 1)
                if b.live():
                    pe.wait_ge(h1_split, b.t + 1)
                    pe.wait_ge(msg_biased, b.t + 1)
                    for j in range(ODD):
                        product(pe, p_Bo, conv2[:, (2 * j + 1) * P:(2 * j + 2) * P], h1[:, 1, :, j:j + M], j == 0, j == ODD - 1)
                    pe.wait_ge(hs_split, b.t + 1)
                    for j in range(EVEN):
                        last = product(pe, p_sum, conv2s[:, j * P:(j + 1) * P], hs[:, :, j:j + M], j == 0, j == EVEN - 1)
                    last.then_inc(conv2_done, 1)
                    pe.wait_ge(exp_done, b.t + 1)
                    for j in range(EVEN):
                        last = product(pe, p_Ae, conv2[:, 2 * j * P:(2 * j + 1) * P], h1[:, 0, :, j:j + ME], j == 0, j == EVEN - 1)
                    last.then_inc(conv2_done, 1)
                if c.live():
                    pe.wait_ge(hT_ready, c.t + 1)
                    if b.live():
                        need(pe, exp_done, c.t + 2)
                    for j in range(T):
                        last = pe.transpose(p_back[:, j * P:(j + 1) * P], hT[:, j * P:(j + 1) * P], eye[:])
                    last.then_inc(back_done, 1)
                if b.live():
                    pe.wait_ge(A_split, 2 * (b.t + 1))
                    pe.wait_ge(msg_split, b.t + 1)
                    pe.wait_ge(t1_ready, b.t + 1)
                    for g in range(G):
                        for a in range(2):
                            last = product(pe, p_nmp[:, g * N:(g + 1) * N], msg[:, 2 * g + a, :], A[:, g, a, :], a == 0, a == 1)
                    last.then_inc(nmp_done, 1)
                if s.live():
                    pe.wait_ge(xn_ready, 4 * (s.t + 1))
                    need(pe, h1_hi_f, 2 * s.t)
                    for j in range(T):
                        last = pe.transpose(p_xT[:, j * P:(j + 1) * P], xn[:, j, :], eye[:])
                    last.then_inc(xT_done, 1)
                if b.live():
                    need(pe, u_ready, b.t)
                    need(pe, tz_ready, b.t)
                    xb = xs[:, b.p]
                    product(pe, p_n[:], w_hh[:, 2 * P:3 * P], xb, True, True).then_inc(ghn_done, 1)
                    product(pe, p_r[:], w_hh[:, 0:P], xb, True, False)
                    product(pe, p_z[:], w_hh[:, P:2 * P], xb, True, False)
                if s.live():
                    pe.wait_ge(x_split, s.t + 1)
                    pe.wait_ge(x_hi_f, 2 * (s.t + 1))
                    xb = xs[:, s.p]
                    product(pe, p_conv1[:], conv1[:, :], xb, True, True).then_inc(conv1_done, 1)
                    need(pe, nmp_split, s.t)
                    product(pe, p_lr[0:64, :], w_lr[:, :], xb, True, True).then_inc(lr_done, 1)
                    need(pe, v_ready, 2 * s.t)
                    for j in range(T):
                        last = product(pe, p_msg[:, j * P:(j + 1) * P], xb[:, j * P:(j + 1) * P], w_msg[:, :], True, True)
                    last.then_inc(msg_done, 1)
                if b.live():
                    pe.wait_ge(xc_split, b.t + 1)
                    pe.wait_ge(nmp_split, b.t + 1)
                    for k, (bank, done) in enumerate(((p_r, r_done), (p_z, z_done), (p_n, n_done))):
                        if bank is p_n:
                            pe.wait_ge(gh_ready, b.t + 1)
                        product(pe, bank[:], w_ih[:, k * P:(k + 1) * P], xc[:, :], bank is p_n, False)
                        product(pe, bank[:], w_ih[:, (3 + k) * P:(4 + k) * P], nm[:, :], False, True).then_inc(done, 1)
                if s.live():
                    pe.wait_ge(right_ready, s.t + 1)
                    need(pe, x_updated, s.t - 1)
                    need(pe, v_ready, 2 * s.t)
                    for g in range(G):
                        for a in range(2):
                            m0 = g * N + a * P
                            last = pe.matmul(p_dist[:, g, a, :], q[0:KD, m0:m0 + P], right[:, g * N:(g + 1) * N], start=True, stop=True)
                    last.then_inc(dist_done, 1)
            run_steps(pe, body, 2)


HEADS = 4
HD = 64
DI = HEADS * HD
DS = 64
XBC = DI + 2 * DS
TAPS = 4
HALF_DT, CUM, OFF = 0, 1, 2


def mamba_weights(nc, ctx, w):
    shapes = {
        "w_in": ([P, DI + XBC], w["W_in_zx"]),
        "w_outT": ([P, DI], w["W_outT"]),
        "w_lin": ([P, P], w["W_lin"]),
        "vecs": ([P, 3 * TAPS + 3 + 2], w["mamba_vecs"]),
        "half_D": ([P, HEADS], spread(w["D"])),
        "mask": ([P, 3 * P], w["mask"]),
    }
    return {name: (ctx.enter_context(nc.sbuf_tensor("m_" + name, shape, F32)), src) for name, (shape, src) in shapes.items()}


def dt_phase(nc, w, X, XT, table, next_weights, cum_dram, eye):
    with ExitStack() as ctx:
        ph = Phase(nc, ctx, "t_")
        sb, sem = ph.sb, ph.sem
        w_dt = sb("w_dt", [P, HEADS])
        cols = sb("cols", [HEADS, 4])
        b_lin = sb("b_lin", [P, P])
        minus_half = sb("minus_half", [P, T])
        ones = sb("ones", [HEADS, P])
        stats, mv = sb("stats", [P, 2, T, 6]), sb("mv", [P, 2, T, 2])
        veps, rstd = sb("veps", [P, 2, T]), sb("rstd", [P, 2, T])
        xn = sb("xn", [P, 2, T, P])
        u, absu, e, l, dt, dA = (sb(s, [HEADS, S]) for s in ("u", "absu", "e", "l", "dt", "dA"))
        rows = sb("rows", [P, 2, S])
        p_xT = ph.psum("p_xT", [P, S])
        p_dt = [ph.psum(f"p_dt{p}", [P, S]) for p in range(2)]
        p_tab = ph.psum("p_tab", [P, T, P])
        loaded, next_loaded, consts = sem("loaded"), sem("next_loaded"), sem("consts")
        stats_done, mv_done, veps_done, rstd_done = sem("stats_done"), sem("mv_done"), sem("veps_done"), sem("rstd_done")
        xn_ready, xT_done, XT_ready, biased = sem("xn_ready"), sem("xT_done"), sem("XT_ready"), sem("biased")
        dt_done, u_ready, e_ready, l_ready, dt_ready, dA_ready = (
            sem(s) for s in ("dt_done", "u_ready", "e_ready", "l_ready", "dt_ready", "dA_ready"))
        scanned, rows_ready, rows_turned, table_ready = (sem(s) for s in ("scanned", "rows_ready", "rows_turned", "table_ready"))
        half_ready = sem("half_ready")
        written = [sem(f"written{p}") for p in range(2)]
        block = ctx.enter_context(nc.Block())

        @block.sync
        def _(sp):
            sp.dma_start(w_dt[:], w["W_dt"]).then_inc(loaded, 16)
            sp.dma_start(cols[:, 0:1], column(w["dt_bias"])).then_inc(loaded, 16)
            sp.dma_start(cols[:, 1:2], column(w["A_log"])).then_inc(loaded, 16)
            sp.dma_start(b_lin[:], spread(w["b_lin"])).then_inc(loaded, 16)
            for dst, src in next_weights.values():
                sp.dma_start(dst[:], src).then_inc(next_loaded, 16)

            def body(s):
                b = s.back(1)
                if b.live():
                    hold(sp, rows_ready, 2 * (b.t + 1))
                    sp.dma_start(cum_dram[:, bass.ts(b.t, S)], rows[32:32 + HEADS, b.p]).then_inc(written[b.p], 16)
            run_steps(sp, body, 1)
            sp.wait_ge(next_loaded, 16 * len(next_weights))
            for p in range(2):
                sp.wait_ge(written[p], 16 * STEPS // 2)

        @block.gpsimd
        def _(pool):
            pool.memset(minus_half[:], -0.5).then_inc(consts, 1)
            pool.memset(ones[:], 1.0).then_inc(consts, 1)
            pool.memset(rows[:], 0.0).then_inc(consts, 1)
            pool.wait_ge(consts, 3)
            pool.wait_ge(loaded, 16 * 4)

            def body(s):
                a = s.back(1)
                if s.live():
                    layer_norm_rstd(pool, s, mv, veps, minus_half, rstd, mv_done, veps_done, rstd_done, xn_ready)
                if a.live():
                    hold(pool, xn_ready, T * (a.t + 1))
                    xt = X[:, bass.ts(a.t, T), :]
                    bb = b_lin[:].rearrange("p (a d) -> p a d", a=1).broadcast_to([P, T, P])
                    pool.tensor_tensor(xt, xt, bb, ALU.add).then_inc(biased, 1)
            run_steps(pool, body, 1)

        @block.scalar
        def _(act):
            act.preload_act_table_set("natural_log_exp_and_others")
            act.wait_ge(loaded, 16 * 4)
            act.activation(cols[:, 2:3], cols[:, 1:2], ACT.Exp).then_inc(consts, 1)
            act.wait_ge(consts, 4)

            def body(s):
                b, c = s.back(2), s.back(3)
                if b.live():
                    act.wait_ge(u_ready, b.t + 1)
                    act.activation(absu[:], u[:], ACT.Abs).then_inc(e_ready, 1)
                    act.wait_ge(e_ready, 2 * b.t + 1)
                    act.activation(e[:], absu[:], ACT.Exp, scale=-1.0).then_inc(e_ready, 1)
                    act.wait_ge(e_ready, 2 * (b.t + 1))
                    need(act, dt_ready, b.t)
                    act.activation(l[:], e[:], ACT.Ln, bias=1.0).then_inc(l_ready, 1)
                if s.live():
                    hold(act, xT_done, s.t + 1)
                    act.activation(XT[:, bass.ts(s.t, S)], p_xT[:], ACT.Copy).then_inc(XT_ready, 1)
                if b.live():
                    need(act, rows_turned, b.t - 1)
                    need(act, dt_ready, b.t + 1)
                    act.activation(rows[0:HEADS, b.p], dt[:], ACT.Copy, scale=0.5).then_inc(half_ready, 1)
                if c.live():
                    hold(act, rows_turned, c.t + 1)
                    groups = p_tab[:, :, 0:96].rearrange("p t (g r) -> p t g r", g=3)[:, :, :, 0:HEADS]
                    act.activation(table[:, bass.ts(c.t, T)], groups, ACT.Copy).then_inc(table_ready, 1)
            run_steps(act, body, 3)

        @block.vector
        def _(dve):
            dve.wait_ge(consts, 4)
            dve.tensor_scalar(cols[:, 3:4], cols[:, 2:3], -1.0, None, ALU.mult).then_inc(consts, 1)
            dve.wait_ge(consts, 5)

            def body(s):
                a, b = s.back(1), s.back(3)
                if b.live():
                    dve.wait_ge(dt_done, b.t + 1)
                    need(dve, dt_ready, b.t)
                    dve.tensor_scalar(u[:], p_dt[b.p][0:HEADS, :], cols[:, 0:1], None, ALU.add).then_inc(u_ready, 1)
                if s.live():
                    layer_norm_stats(dve, X, s, stats, mv, stats_done, mv_done)
                if a.live():
                    need(dve, xT_done, a.t - 1)
                    layer_norm_apply(dve, X, a, xn[:, a.p], mv, rstd, rstd_done, xn_ready)
                if b.live():
                    dve.wait_ge(u_ready, b.t + 1)
                    need(dve, half_ready, b.t)
                    dve.wait_ge(l_ready, b.t + 1)
                    dve.scalar_tensor_tensor(out=dt[:], in0=u[:], scalar=0.0, in1=l[:], op0=ALU.max, op1=ALU.add).then_inc(dt_ready, 1)
                    need(dve, dt_ready, b.t + 1)
                    dve.tensor_scalar(dA[:], dt[:], cols[:, 3:4], None, ALU.mult).then_inc(dA_ready, 1)
                    need(dve, rows_turned, b.t - 1)
                    need(dve, written[b.p], 16 * b.u)
                    hold(dve, dA_ready, b.t + 1)
                    for j in range(T):
                        dve.tensor_tensor_scan(out=rows[32:32 + HEADS, b.p, j * P:(j + 1) * P], data0=ones[:],
                                               data1=dA[:, j * P:(j + 1) * P], initial=0.0, op0=ALU.mult, op1=ALU.add).then_inc(scanned, 1)
                    hold(dve, scanned, T * (b.t + 1))
                    for g in range(G):
                        cum = rows[32:32 + HEADS, b.p, g * N:g * N + P]
                        dve.tensor_scalar(rows[64:64 + HEADS, b.p, g * N:g * N + P], cum, cum[:, P - 1:P], -1.0,
                                          ALU.subtract, ALU.mult).then_inc(rows_ready, 1)
            run_steps(dve, body, 3)

        @block.tensor
        def _(pe):
            pe.wait_ge(loaded, 16 * 4)

            def body(s):
                c = s.back(3)
                if s.live():
                    pe.wait_ge(xn_ready, T * (s.t + 1))
                    need(pe, XT_ready, s.t)
                    for j in range(T):
                        last = pe.transpose(p_xT[:, j * P:(j + 1) * P], xn[:, s.p, j, :], eye[:])
                    last.then_inc(xT_done, 1)
                if c.live():
                    pe.wait_ge(rows_ready, 2 * (c.t + 1))
                    need(pe, half_ready, c.t + 1)
                    need(pe, table_ready, c.t)
                    for j in range(T):
                        last = pe.transpose(p_tab[:, j, 0:96], rows[0:96, c.p, j * P:(j + 1) * P], eye[0:96, 0:96])
                    last.then_inc(rows_turned, 1)
                if s.live():
                    need(pe, u_ready, s.t - 1)
                    hold(pe, XT_ready, s.t + 1)
                    pe.matmul(p_dt[s.p][0:HEADS, :], w_dt[:], XT[:, bass.ts(s.t, S)], start=True, stop=True).then_inc(dt_done, 1)
            run_steps(pe, body, 3)


def mamba_phase(nc, weights, X, XT, table, cum_dram, eye):
    CHUNKS = (1, 2, 0)
    NB = 3 * P
    with ExitStack() as ctx:
        ph = Phase(nc, ctx, "m_")
        sb, sem = ph.sb, ph.sem
        w_in, w_outT, w_lin, vecs, half_D, mask = (weights[name][0] for name in ("w_in", "w_outT", "w_lin", "vecs", "half_D", "mask"))
        w_out = sb("w_out", [P, 2, P])
        minus_half = sb("minus_half", [P, T])
        xT = sb("xT", [P, 2, S])
        cum = sb("cum", [P, 2, HEADS, S])
        tab = sb("tab", [P, 2, T, 3, HEADS])
        xp = sb("xp", [P, 3, G, TAPS - 1 + N])
        c_ = sb("c", [P, 2, 3, G, N])
        xs = sb("xs", [P, 2, S])
        BC = sb("BC", [P, 2, S])
        Ct = sb("Ct", [DS, S])
        xh = sb("xh", [P, T, DI])
        xdt = sb("xdt", [P, 2, T, DI])
        xD = sb("xD", [P, 2, T, DI])
        Gm = sb("Gm", [P, G, NB])
        dec = sb("dec", [P, G, HEADS, NB])
        W = sb("W", [P, 2, G, HEADS, NB])
        zz = sb("zz", [P, 2, T, DI])
        y1 = sb("y1", [P, T, DI])
        y2 = sb("y2", [P, 2, T, DI])
        sq = sb("sq", [P, 2, DI])
        ss, ms, rs = sb("ss", [P, T]), sb("ms", [P, T]), sb("rs", [P, T])
        half_rs = sb("half_rs", [P, 2, T])
        yT = sb("yT", [P, 2, S])
        p_x0 = ph.psum("p_x0", [P, S])
        p_x12 = ph.psum("p_x12", [P, 2, S])
        p_z = ph.psum("p_z", [P, T, DI])
        p_xh = ph.psum("p_xh", [P, T, DI])
        p_o = ph.psum("p_o", [P, S])
        p_yT = p_xh[:].rearrange("p t d -> p (t d)").rearrange("p (c n) -> p c n", c=2)
        p_Y = p_x12[:].rearrange("p a b -> p (a b)").rearrange("p (t d) -> p t d", t=T)
        p_G = (p_o[:, 0:NB], p_x0[:, 0:NB])
        p_x = (p_x0[:], p_x12[:, 0, :], p_x12[:, 1, :])

        names = ("Ct_ready consts w2_done w2_ready tab_ready x_done x_taken taps tanh_ready silu_ready z_done tz_ready "
                 "zz_ready xh_done xh_ready xdt_ready xD_ready G_done Gm_ready diag_ready off_ready dec_ready W_ready Y_done "
                 "y1_ready y2_ready ss_ready ms_ready rs_ready hrs_ready yT_done yT_ready out_done x_updated")
        q = {s: sem(s) for s in names.split()}
        xT_in, cum_in = ([sem(f"{name}_in{p}") for p in range(2)] for name in ("xT", "cum"))
        block = ctx.enter_context(nc.Block())

        @block.sync
        def _(sp):
            def body(s):
                if s.live():
                    hold(sp, q["z_done"], s.t - 1)
                    hold(sp, q["diag_ready"], 16 * (s.t - 1))
                    hold(sp, q["off_ready"], 8 * (s.t - 1))
                    sp.dma_start(xT[:, s.p], XT[:, bass.ts(s.t, S)]).then_inc(xT_in[s.p], 16)
                    src = cum_dram[:, bass.ts(s.t, S)]
                    sp.dma_start(cum[:, s.p], src.partition_broadcast(P)).then_inc(cum_in[s.p], 16)
            run_steps(sp, body, 1)

        @block.gpsimd
        def _(pool):
            pool.memset(minus_half[:], -0.5).then_inc(q["consts"], 1)
            pool.memset(xp[:], 0.0).then_inc(q["consts"], 1)
            pool.tensor_scalar(half_D[:], half_D[:], 0.5, None, ALU.mult).then_inc(q["consts"], 1)
            pool.wait_ge(q["consts"], 3)

            def body(s):
                m, y = s.back(1), s.back(3)
                if s.live():
                    hold(pool, q["dec_ready"], s.t - 1)
                    hold(pool, q["xdt_ready"], s.t - 1)
                    pool.tensor_copy(tab[:, s.p], table[:, bass.ts(s.t, T)]).then_inc(q["tab_ready"], 1)
                if y.live():
                    need(pool, q["zz_ready"], y.t + 1)
                    need(pool, q["yT_done"], y.t - 1)
                    need(pool, q["y1_ready"], y.t + 1)
                    pool.tensor_tensor(y2[:, y.p], y1[:], zz[:, y.p], ALU.mult).then_inc(q["y2_ready"], 1)
                if m.live():
                    need(pool, q["Y_done"], m.t - 1)
                    need(pool, q["tab_ready"], m.t + 1)
                    need(pool, q["xh_ready"], m.t + 1)
                    xh4 = xh[:].rearrange("p t (h d) -> p t h d", h=HEADS)
                    half_dt = tab[:, m.p, :, HALF_DT, :].rearrange("p t (h a) -> p t h a", a=1).broadcast_to([P, T, HEADS, HD])
                    pool.tensor_tensor(xdt[:, m.p].rearrange("p t (h d) -> p t h d", h=HEADS), xh4, half_dt, ALU.mult).then_inc(q["xdt_ready"], 1)
                    need(pool, q["y1_ready"], m.t - 1)
                    for j in range(T):
                        hD = half_D[:].rearrange("p (h a) -> p h a", a=1).broadcast_to([P, HEADS, HD])
                        pool.tensor_tensor(xD[:, m.p, j].rearrange("p (h d) -> p h d", h=HEADS), xh4[:, j], hD, ALU.mult).then_inc(q["xD_ready"], 1)
                    need(pool, q["dec_ready"], m.t + 1)
                    need(pool, q["Gm_ready"], 2 * (m.t + 1))
                    g1 = Gm[:, 1].rearrange("p (a n) -> p a n", a=1).broadcast_to([P, HEADS, NB])
                    pool.tensor_tensor(W[:, m.p, 1], dec[:, 1], g1, ALU.mult).then_inc(q["W_ready"], 1)
                if y.live():
                    need(pool, q["rs_ready"], y.t)
                    hold(pool, q["ss_ready"], T * (y.t + 1))
                    pool.tensor_scalar(ms[:], ss[:], 1.0 / (4 * DI), EPS, ALU.mult, ALU.add).then_inc(q["ms_ready"], 1)
                    need(pool, q["hrs_ready"], y.t)
                    need(pool, q["ms_ready"], y.t + 1)
                    pool.tensor_tensor(rs[:], ms[:], minus_half[:], ALU.pow).then_inc(q["rs_ready"], 1)
                    need(pool, q["x_updated"], T * (y.t - 1))
                    hold(pool, q["rs_ready"], y.t + 1)
                    pool.tensor_scalar(half_rs[:, y.p], rs[:], 0.5, None, ALU.mult).then_inc(q["hrs_ready"], 1)
            run_steps(pool, body, 3)

        @block.scalar
        def _(act):
            act.preload_act_table(ACT.Exp)
            act.wait_ge(q["consts"], 3)
            act.wait_ge(q["w2_done"], 1)
            for k in range(2):
                act.activation(w_out[:, k, :], p_z[:, k, 0:P], ACT.Copy, scale=vecs[:, 15 + k:16 + k]).then_inc(q["w2_ready"], 1)

            def body(s):
                m, y, o = s.back(1), s.back(3), s.back(4)
                if o.live():
                    need(act, q["out_done"], o.t)
                    need(act, q["yT_done"], o.t + 1)
                    act.activation(yT[:], p_yT, ACT.Copy).then_inc(q["yT_ready"], 1)
                if m.live():
                    need(act, q["G_done"], m.t)
                    need(act, q["silu_ready"], 2 * m.t + 1)
                    act.activation(Ct[:], BC[DS:P, m.p, :], ACT.Copy).then_inc(q["Ct_ready"], 1)
                if s.live():
                    need(act, q["silu_ready"], 2 * (s.t - 1))
                    need(act, q["taps"], 9 * s.t)
                    for i, k in enumerate(CHUNKS):
                        act.wait_ge(q["x_done"], 3 * s.t + i + 1)
                        px = p_x[k].rearrange("p (g n) -> p g n", g=G)
                        act.activation(xp[:, k, :, TAPS - 1:], px, ACT.Copy).then_inc(q["x_taken"], 1)
                        last_tap = k * TAPS + TAPS - 1
                        act.activation(c_[:, s.p, k], px, ACT.Identity, scale=vecs[:, last_tap:last_tap + 1],
                                       bias=vecs[:, 3 * TAPS + k:3 * TAPS + k + 1]).then_inc(q["x_taken"], 1)
                if m.live():
                    act.wait_ge(cum_in[m.p], 16 * (m.u + 1))
                    need(act, q["W_ready"], 2 * m.t)
                    act.wait_ge(q["tab_ready"], m.t + 1)
                    for g in range(G):
                        for h in range(HEADS):
                            act.activation(dec[:, g, h, P:2 * P], cum[:, m.p, h, g * N + P:(g + 1) * N], ACT.Exp,
                                           bias=tab[:, m.p, 2 * g, OFF, h:h + 1]).then_inc(q["off_ready"], 1)
                    act.wait_ge(q["diag_ready"], 16 * (m.t + 1))
                    diag = dec[:].rearrange("p g h (b n) -> p (g h) b n", b=3)[:, :, 0:3:2, :]
                    act.activation(diag, diag, ACT.Exp).then_inc(q["dec_ready"], 1)
                    need(act, q["z_done"], m.t + 1)
                    need(act, q["y2_ready"], m.t - 1)
                    act.activation(zz[:, m.p], p_z[:], ACT.Tanh, scale=0.5).then_inc(q["tz_ready"], 1)
                    need(act, q["xdt_ready"], m.t)
                    need(act, q["xD_ready"], T * m.t)
                    need(act, q["xh_done"], m.t + 1)
                    act.activation(xh[:], p_xh[:], ACT.Copy).then_inc(q["xh_ready"], 1)
                if y.live():
                    need(act, q["ms_ready"], y.t)
                    need(act, q["y2_ready"], y.t + 1)
                    for j in range(T):
                        need(act, q["ss_ready"], T * y.t + j - 1)
                        act.activation(sq[:, j % 2], y2[:, y.p, j], ACT.Square, accum_out=ss[:, j:j + 1]).then_inc(q["ss_ready"], 1)
                if s.live():
                    need(act, q["xh_done"], s.t)
                    need(act, q["G_done"], s.t - 1)
                    act.wait_ge(q["taps"], 9 * (s.t + 1))
                    cc = c_[:, s.p].rearrange("p k g n -> p k (g n)")
                    act.activation(BC[:, s.p], cc[:, 2], ACT.Tanh, scale=0.5).then_inc(q["tanh_ready"], 1)
                    act.activation(xs[:], cc[:, 0:2], ACT.Tanh, scale=0.5).then_inc(q["tanh_ready"], 1)
            run_steps(act, body, 4)

        @block.vector
        def _(dve):
            dve.wait_ge(q["consts"], 3)

            def body(s):
                m, v, o = s.back(1), s.back(2), s.back(4)
                if m.live():
                    dve.wait_ge(cum_in[m.p], 16 * (m.u + 1))
                    need(dve, q["W_ready"], 2 * m.t)
                    dve.wait_ge(q["tab_ready"], m.t + 1)
                    for g in range(G):
                        for b in range(2):
                            for h in range(HEADS):
                                l0 = g * N + b * P
                                dve.tensor_scalar(dec[:, g, h, 2 * b * P:(2 * b + 1) * P], cum[:, m.p, h, l0:l0 + P],
                                                  tab[:, m.p, 2 * g + b, CUM, h:h + 1], 0.0, ALU.subtract, ALU.min).then_inc(q["diag_ready"], 1)
                if o.live():
                    need(dve, q["hrs_ready"], o.t + 1)
                    dve.wait_ge(q["out_done"], o.t + 1)
                    for j in range(T):
                        xt = X[:, o.t * T + j, :]
                        dve.scalar_tensor_tensor(out=xt, in0=p_o[:, j * P:(j + 1) * P], scalar=half_rs[:, o.p, j:j + 1], in1=xt,
                                                 op0=ALU.mult, op1=ALU.add).then_inc(q["x_updated"], 1)
                if s.live():
                    for n, tap in enumerate(range(TAPS - 1)):
                        for i, k in enumerate(CHUNKS):
                            if n == 0:
                                dve.wait_ge(q["x_taken"], 6 * s.t + 2 * (i + 1))
                            else:
                                dve.wait_ge(q["taps"], 9 * s.t + 3 * (n - 1) + i + 1)
                            dve.scalar_tensor_tensor(out=c_[:, s.p, k], in0=xp[:, k, :, tap:tap + N], scalar=vecs[:, k * TAPS + tap:k * TAPS + tap + 1],
                                                     in1=c_[:, s.p, k], op0=ALU.mult, op1=ALU.add).then_inc(q["taps"], 1)
                if m.live():
                    dve.wait_ge(q["tz_ready"], m.t + 1)
                    dve.scalar_tensor_tensor(out=zz[:, m.p].rearrange("p t d -> p (t d)"), in0=zz[:, m.p].rearrange("p t d -> p (t d)"), scalar=1.0,
                                             in1=p_z[:].rearrange("p t d -> p (t d)"), op0=ALU.add, op1=ALU.mult).then_inc(q["zz_ready"], 1)
                    need(dve, q["W_ready"], 2 * m.t)
                    dve.wait_ge(q["G_done"], m.t + 1)
                    for g in range(G):
                        dve.scalar_tensor_tensor(out=Gm[:, g], in0=p_G[g], scalar=0.25, in1=mask[:], op0=ALU.mult, op1=ALU.mult).then_inc(q["Gm_ready"], 1)
                    dve.wait_ge(q["dec_ready"], m.t + 1)
                    need(dve, q["Y_done"], m.t - 1)
                    dve.wait_ge(q["Gm_ready"], 2 * m.t + 1)
                    g0 = Gm[:, 0].rearrange("p (a n) -> p a n", a=1).broadcast_to([P, HEADS, NB])
                    dve.tensor_tensor(W[:, m.p, 0], dec[:, 0], g0, ALU.mult).then_inc(q["W_ready"], 1)
                if v.live():
                    need(dve, q["xD_ready"], T * (v.t + 1))
                    need(dve, q["y2_ready"], v.t)
                    need(dve, q["Y_done"], v.t + 1)
                    dve.tensor_tensor(y1[:], p_Y, xD[:, v.p], ALU.add).then_inc(q["y1_ready"], 1)
                if s.live():
                    cc = c_[:, s.p].rearrange("p k g n -> p k (g n)")
                    for k, (v_, c) in enumerate(((BC[:, s.p], cc[:, 2]), (xs[:], cc[:, 0:2]))):
                        dve.wait_ge(q["tanh_ready"], 2 * s.t + k + 1)
                        dve.scalar_tensor_tensor(out=v_, in0=v_, scalar=1.0, in1=c, op0=ALU.add, op1=ALU.mult).then_inc(q["silu_ready"], 1)
            run_steps(dve, body, 4)

        @block.tensor
        def _(pe):
            for k in range(2):
                last = pe.matmul(p_z[:, k, 0:P], w_outT[:, k * P:(k + 1) * P], w_lin[:], start=True, stop=True)
            last.then_inc(q["w2_done"], 1)
            pe.wait_ge(q["w2_ready"], 2)

            def body(s):
                m, v, o = s.back(1), s.back(2), s.back(4)
                if o.live():
                    if v.live():
                        need(pe, q["xh_ready"], o.t + 3)
                    need(pe, q["yT_ready"], o.t)
                    need(pe, q["y2_ready"], o.t + 1)
                    for k in range(2):
                        for j in range(T):
                            last = pe.transpose(p_yT[:, k, j * P:(j + 1) * P], y2[:, o.p, j, k * P:(k + 1) * P], eye[:])
                    last.then_inc(q["yT_done"], 1)
                if m.live():
                    need(pe, q["zz_ready"], m.t)
                    for j in range(T):
                        last = pe.matmul(p_z[:, j, :], xT[:, m.p, j * P:(j + 1) * P], w_in[:, 0:DI], start=True, stop=True)
                    last.then_inc(q["z_done"], 1)
                if o.live():
                    if v.live():
                        need(pe, q["Gm_ready"], 2 * (o.t + 3))
                    if not m.live():
                        need(pe, q["x_updated"], T * o.t)
                    pe.wait_ge(q["yT_ready"], o.t + 1)
                    for j in range(T):
                        for k in range(2):
                            last = pe.matmul(p_o[:, j * P:(j + 1) * P], yT[:, k, j * P:(j + 1) * P], w_out[:, k, :], start=k == 0, stop=k == 1)
                    last.then_inc(q["out_done"], 1)
                if s.live():
                    need(pe, q["Gm_ready"], 2 * (s.t - 1))
                    need(pe, q["y1_ready"], s.t - 2)
                    need(pe, q["x_taken"], 6 * s.t)
                    pe.wait_ge(xT_in[s.p], 16 * (s.u + 1))
                    for k in CHUNKS:
                        pe.matmul(p_x[k], w_in[:, DI + k * P:DI + (k + 1) * P], xT[:, s.p], start=True, stop=True).then_inc(q["x_done"], 1)
                if m.live():
                    need(pe, q["yT_ready"], m.t - 2)
                    pe.wait_ge(q["silu_ready"], 2 * (m.t + 1))
                    for j in range(T):
                        for k in range(2):
                            last = pe.transpose(p_xh[:, j, k * P:(k + 1) * P], xs[:, k, j * P:(j + 1) * P], eye[:])
                    last.then_inc(q["xh_done"], 1)
                if v.live():
                    if s.live():
                        pe.wait_ge(q["x_taken"], 6 * s.t + 4)
                    need(pe, q["y1_ready"], v.t)
                    pe.wait_ge(q["W_ready"], 2 * (v.t + 1))
                    pe.wait_ge(q["xdt_ready"], v.t + 1)
                    for g in range(G):
                        for h in range(HEADS):
                            hs = slice(h * HD, (h + 1) * HD)
                            Wh = W[:, v.p, g, h]
                            pe.matmul(p_Y[:, 2 * g, hs], Wh[:, 0:P], xdt[:, v.p, 2 * g, hs], start=True, stop=True)
                            pe.matmul(p_Y[:, 2 * g + 1, hs], Wh[:, P:2 * P], xdt[:, v.p, 2 * g, hs], start=True, stop=False)
                            last = pe.matmul(p_Y[:, 2 * g + 1, hs], Wh[:, 2 * P:NB], xdt[:, v.p, 2 * g + 1, hs], start=False, stop=True)
                    last.then_inc(q["Y_done"], 1)
                if m.live():
                    need(pe, q["x_updated"], T * (m.t - 2))
                    need(pe, q["Ct_ready"], m.t + 1)
                    if s.live():
                        pe.wait_ge(q["x_taken"], 6 * (s.t + 1))
                    for g in range(G):
                        l0 = g * N
                        pe.matmul(p_G[g][:, 0:N], BC[0:DS, m.p, l0:l0 + P], Ct[:, l0:l0 + N], start=True, stop=True)
                        last = pe.matmul(p_G[g][:, N:NB], BC[0:DS, m.p, l0 + P:l0 + N], Ct[:, l0 + P:l0 + N], start=True, stop=True)
                    last.then_inc(q["G_done"], 1)
            run_steps(pe, body, 4)


def graph_phase(nc, w, X, adjT_dram, eye):
    MOD = 4
    with ExitStack() as ctx:
        ph = Phase(nc, ctx, "c_")
        sb, sem = ph.sb, ph.sem
        weight = sb("weight", [P, P])
        bias = sb("bias", [P, P])
        minus_half = sb("minus_half", [P, T])
        ones = sb("ones", [P, 1])
        adjT = sb("adjT", [P, MOD, G, 2, N])
        stats, mv = sb("stats", [P, MOD, T, 6]), sb("mv", [P, MOD, T, 2])
        veps, deps = sb("veps", [P, T]), sb("deps", [P, T])
        rstd, dinv = sb("rstd", [P, MOD, T]), sb("dinv", [P, MOD, T])
        xn = sb("xn", [P, 2, T, P])
        xT = sb("xT", [P, S])
        sup = sb("sup", [P, 2, T, P])
        p_xT = ph.psum("p_xT", [P, S])
        p_sup = ph.psum("p_sup", [P, S])
        p_agg = [ph.psum(f"p_agg{p}", [P, S]) for p in range(2)]
        p_deg = ph.psum("p_deg", [P, T])
        loaded, consts = sem("loaded"), sem("consts")
        stats_done, mv_done, deg_done, veps_done, rstd_done = (sem(s) for s in ("stats_done", "mv_done", "deg_done", "veps_done", "rstd_done"))
        deps_done, dinv_done = sem("deps_done"), sem("dinv_done")
        xn_ready, xT_done, xT_ready, biased = sem("xn_ready"), sem("xT_done"), sem("xT_ready"), sem("biased")
        sup_done, sup_ready, agg_done, x_updated = (sem(s) for s in ("sup_done", "sup_ready", "agg_done", "x_updated"))
        adjT_in = [sem(f"adjT_in{p}") for p in range(MOD)]
        block = ctx.enter_context(nc.Block())

        @block.sync
        def _(sp):
            sp.dma_start(weight[:], w["gcn_w"]).then_inc(loaded, 16)
            sp.dma_start(bias[:], spread(w["gcn_b"])).then_inc(loaded, 16)

            def body(s):
                if s.live():
                    hold(sp, agg_done, s.t - MOD + 1)
                    sp.dma_start(adjT[:, s.p], adjT_dram[bass.ts(s.t, G)].rearrange("g (a m) n -> m g a n", m=P)).then_inc(adjT_in[s.p], 16)
            run_steps(sp, body, MOD - 1, mod=MOD)

        @block.gpsimd
        def _(pool):
            pool.memset(minus_half[:], -0.5).then_inc(consts, 1)
            pool.memset(ones[:], 1.0).then_inc(consts, 1)
            pool.wait_ge(consts, 2)
            pool.wait_ge(loaded, 32)

            def body(s):
                b = s.back(1)
                if s.live():
                    need(pool, xn_ready, T * (s.t - 3))
                    need(pool, veps_done, s.t + 1)
                    pool.tensor_tensor(rstd[:, s.p], veps[:], minus_half[:], ALU.pow).then_inc(rstd_done, 1)
                if b.live():
                    need(pool, x_updated, T * (b.t - 3))
                    need(pool, deps_done, b.t + 1)
                    pool.tensor_tensor(dinv[:, b.p], deps[:], minus_half[:], ALU.pow).then_inc(dinv_done, 1)
                if b.live():
                    hold(pool, xn_ready, T * (b.t + 1))
                    xt = X[:, bass.ts(b.t, T), :]
                    bb = bias[:].rearrange("p (a d) -> p a d", a=1).broadcast_to([P, T, P])
                    pool.tensor_tensor(xt, xt, bb, ALU.add).then_inc(biased, 1)
            run_steps(pool, body, 1, mod=MOD)

        @block.scalar
        def _(act):
            act.preload_act_table(ACT.Exp)

            def body(s):
                b = s.back(1)
                if b.live():
                    act.wait_ge(dinv_done, b.t + 1)
                    need(act, agg_done, b.t - 1)
                    act.wait_ge(sup_done, b.t + 1)
                    for j in range(T):
                        act.activation(sup[:, b.p % 2, j], p_sup[:, j * P:(j + 1) * P], ACT.Copy, scale=dinv[:, b.p, j:j + 1]).then_inc(sup_ready, 1)
                if s.live():
                    need(act, sup_done, s.t)
                    need(act, xT_done, s.t + 1)
                    act.activation(xT[:], p_xT[:], ACT.Copy).then_inc(xT_ready, 1)
            run_steps(act, body, 1, mod=MOD)

        @block.vector
        def _(dve):
            def body(s):
                a, c = s.back(1), s.back(3)
                if s.live():
                    layer_norm_stats(dve, X, s, stats, mv, stats_done, mv_done)
                if s.live():
                    need(dve, rstd_done, s.t)
                    need(dve, mv_done, T * (s.t + 1))
                    dve.tensor_scalar(veps[:], mv[:, s.p, :, 1], EPS, None, ALU.add).then_inc(veps_done, 1)
                if a.live():
                    need(dve, xT_done, a.t - 1)
                    layer_norm_apply(dve, X, a, xn[:, a.p % 2], mv, rstd, rstd_done, xn_ready)
                if c.live():
                    need(dve, biased, c.t + 1)
                    need(dve, agg_done, c.t + 1)
                    for j in range(T):
                        xt = X[:, c.t * T + j, :]
                        dve.scalar_tensor_tensor(out=xt, in0=p_agg[c.p % 2][:, j * P:(j + 1) * P], scalar=dinv[:, c.p, j:j + 1], in1=xt,
                                                 op0=ALU.mult, op1=ALU.add).then_inc(x_updated, 1)
                if a.live():
                    need(dve, dinv_done, a.t)
                    need(dve, deg_done, a.t + 1)
                    dve.tensor_scalar(deps[:], p_deg[:], EPS, None, ALU.add).then_inc(deps_done, 1)
            run_steps(dve, body, 3, mod=MOD)

        @block.tensor
        def _(pe):
            pe.wait_ge(loaded, 32)
            pe.wait_ge(consts, 2)

            def body(s):
                b, c = s.back(1), s.back(2)
                if c.live():
                    need(pe, x_updated, T * (c.t - 1))
                    need(pe, sup_ready, T * (c.t + 1))
                    need(pe, adjT_in[c.p], 16 * (c.u + 1))
                    for j in range(T):
                        for a in range(2):
                            n0 = (j % 2) * P
                            last = pe.matmul(p_agg[c.p % 2][:, j * P:(j + 1) * P], adjT[:, c.p, j // 2, a, n0:n0 + P], sup[:, c.p % 2, 2 * (j // 2) + a], start=a == 0, stop=a == 1)
                    last.then_inc(agg_done, 1)
                if b.live():
                    need(pe, sup_ready, T * b.t)
                    need(pe, xT_ready, b.t + 1)
                    for j in range(T):
                        last = pe.matmul(p_sup[:, j * P:(j + 1) * P], xT[:, j * P:(j + 1) * P], weight[:], start=True, stop=True)
                    last.then_inc(sup_done, 1)
                if s.live():
                    need(pe, deps_done, s.t)
                    need(pe, adjT_in[s.p], 16 * (s.u + 1))
                    for j in range(T):
                        for a in range(2):
                            n0 = (j % 2) * P
                            last = pe.matmul(p_deg[:, j:j + 1], adjT[:, s.p, j // 2, a, n0:n0 + P], ones[:], start=a == 0, stop=a == 1)
                    last.then_inc(deg_done, 1)
                if s.live():
                    need(pe, xT_ready, s.t)
                    need(pe, xn_ready, T * (s.t + 1))
                    for j in range(T):
                        last = pe.transpose(p_xT[:, j * P:(j + 1) * P], xn[:, s.p % 2, j, :], eye[:])
                    last.then_inc(xT_done, 1)
            run_steps(pe, body, 2, mod=MOD)


BF16 = mybir.dt.bfloat16
I32 = mybir.dt.int32
EX = 8
TOPK = 2
H = 341
HP = H + 1
CH = [(0, P), (P, P), (2 * P, H - 2 * P)]
SLOTS = TOPK * NT + EX
MEMBERS = [(j, k) for k in range(TOPK) for j in range(T)]
MEM = len(MEMBERS)
QUAD = 4
NO_ROW = 1 << 20


def expert_weights(nc, ctx):
    def pair(name, shape):
        return Pair(*(ctx.enter_context(nc.sbuf_tensor(f"{name}_{part}", shape, F32R)) for part in ("hi", "lo")))
    w2 = ctx.enter_context(nc.sbuf_tensor("w2", [P, len(CH), EX, 2, P], F32R))
    return pair("w1", [P, EX, HP]), pair("w3", [P, EX, HP]), w2


def route_phase(nc, w, X, gate, gather_rows, scatter_rows, tile_expert, experts, xn_dram, eye):
    w1, w3, w2 = experts
    with ExitStack() as ctx:
        ph = Phase(nc, ctx, "r_")
        sb, sem = ph.sb, ph.sem
        router = sb("router", [P, EX])
        rev = sb("rev", [P, EX])
        before = sb("before", [P, P])
        ones = sb("ones", [P, P])
        part_no = sb("part_no", [P, 1])
        slot_iota = sb("slot_iota", [P, SLOTS])
        slot_bf = sb("slot_bf", [P, SLOTS], BF16)
        row_bf = sb("row_bf", [P, P], BF16)
        minus_half = sb("minus_half", [P, T])
        stats, mv = sb("stats", [P, 2, T, 6]), sb("mv", [P, 2, T, 2])
        veps, rstd = sb("veps", [P, 2, T]), sb("rstd", [P, 2, T])
        xn = sb("xn", [P, 2, T, P])
        xT = sb("xT", [P, 2, S])
        full = [P, NT, EX]
        logits, hot1, hot2, work, work2, both = (sb(s, full) for s in ("logits", "hot1", "hot2", "work", "work2", "both"))
        m1, m2, f1, z, rz, e2, p2, den, gsum = (sb(s, [P, NT]) for s in ("m1", "m2", "f1", "z", "rz", "e2", "p2", "den", "gsum"))
        total = sb("total", [P, EX, NT])
        upto = sb("upto", [P, EX, NT])
        pos = sb("pos", [P, NT, EX])
        padded = sb("padded", [P, EX])
        padded_i = sb("padded_i", [P, EX], I32)
        ends = sb("ends", [P, EX])
        dest = sb("dest", [P, TOPK, NT])
        dest_i, tile_i = sb("dest_i", [P, TOPK, NT], I32), sb("tile_i", [P, TOPK, NT], I32)
        dest_tile, dest_row = sb("dest_tile", [P, TOPK, NT]), sb("dest_row", [P, TOPK, NT])
        tile_bf, destrow_bf = sb("tile_bf", [P, TOPK, NT], BF16), sb("destrow_bf", [P, TOPK, NT], BF16)
        tile_k = sb("tile_k", [P, TOPK, NT])
        slot_hot = sb("slot_hot", [P, 2, MEM, SLOTS], BF16)
        B = sb("B", [P, 2, MEM, P], BF16)
        A = sb("A", [P, 2, 2, MEM, SLOTS], BF16)
        hi_no, lo_no = sb("hi_no", [P, SLOTS]), sb("lo_no", [P, SLOTS])
        row_f, off_f, exp_f = sb("row_f", [P, SLOTS]), sb("off_f", [P, SLOTS]), sb("exp_f", [P, SLOTS])
        p_xT = ph.psum("p_xT", [P, S])
        p_log = ph.psum("p_log", [P, T, EX])
        p_rank = ph.psum("p_rank", full)
        p_total = ph.psum("p_total", full)
        p_inv = ph.psum("p_inv", [P, 2, SLOTS])
        names = ("consts stats_done mv_done veps_done rstd_done xn_ready xT_done xT_ready log_done log_ready chain ex_ready "
                 "w_loaded w_hi w_split ranked hot_ready B_ready A_hi_ready A_lo_ready inv_done")
        q = {s: sem(s) for s in names.split()}
        written = [sem(f"written{p}") for p in range(2)]
        stage13, stage2 = sb("stage13", [P, 2, EX * H]), sb("stage2", [P, len(CH), EX * P])
        rest = CH[-1][1]
        weights = [(stage13[:, k].rearrange("p (e h) -> p e h", e=EX), wk[:, :, 0:H]) for k, wk in enumerate((w1, w3))]
        for rows, k in ((P, slice(0, 2)), (rest, slice(2, 3))):
            weights.append((stage2[0:rows, k].rearrange("p k (e d) -> p k e d", e=EX), Pair(w2[0:rows, k, :, 0], w2[0:rows, k, :, 1])))
        block = ctx.enter_context(nc.Block())

        @block.sync
        def _(sp):
            for dst, src in ((router[:], w["routerT"]), (rev[:], spread(w["rev8"])), (before[:], w["before"]),
                             (part_no[:], column(w["part_no"])), (slot_iota[:], spread(w["slot_iota"]))):
                sp.dma_start(dst, src).then_inc(q["consts"], 16)
            sp.dma_start(tile_k[:, 0, :], spread(w["tile_no"])).then_inc(q["consts"], 16)
            sp.dma_start(stage13[:, 0], w["w1T"]).then_inc(q["w_loaded"], 16)
            sp.dma_start(stage13[:, 1], w["w3T"]).then_inc(q["w_loaded"], 16)
            for k, (h0, r) in enumerate(CH):
                sp.dma_start(stage2[0:r, k], w["w2T"][h0:h0 + r]).then_inc(q["w_loaded"], 16)

            def body(s):
                if s.live():
                    hold(sp, q["xn_ready"], T * (s.t + 1))
                    sp.dma_start(xn_dram[bass.ts(s.t, T)].rearrange("t p d -> p t d"), xn[:, s.p]).then_inc(written[s.p], 16)
            run_steps(sp, body, 1)
            for p in range(2):
                sp.wait_ge(written[p], 16 * STEPS // 2)

        @block.gpsimd
        def _(pool):
            pool.memset(minus_half[:], -0.5).then_inc(q["consts"], 1)
            pool.memset(ones[:], 1.0).then_inc(q["consts"], 1)
            for part in (w1.hi, w1.lo, w3.hi, w3.lo):
                pool.memset(part[:, :, H:HP].bitcast(F32), 0.0).then_inc(q["w_hi"], 1)
            pool.iota(row_i := sb("row_i", [P, P], I32)[:], [[1, P]], base=0, channel_multiplier=0).then_inc(q["consts"], 1)

            def body(s):
                if s.live():
                    layer_norm_rstd(pool, s, mv, veps, minus_half, rstd, q["mv_done"], q["veps_done"], q["rstd_done"], q["xn_ready"])
            run_steps(pool, body, 0)
            pool.wait_ge(q["consts"], 16 * 6 + 3)
            pool.tensor_copy(row_bf[:], row_i).then_inc(q["consts"], 1)
            for n, (src, dst) in enumerate(weights):
                pool.wait_ge(q["w_hi"], 4 + n + 1)
                pool.tensor_tensor(dst.lo, src, dst.hi.bitcast(F32), ALU.subtract).then_inc(q["w_split"], 1)
            pool.wait_ge(q["w_split"], len(weights))

        @block.scalar
        def _(act):
            act.preload_act_table(ACT.Exp)

            def body(s):
                b = s.back(1)
                if s.live():
                    need(act, q["log_done"], s.t - 1)
                    need(act, q["xT_done"], s.t + 1)
                    act.activation(xT[:, s.p], p_xT[:], ACT.Copy).then_inc(q["xT_ready"], 1)
                if b.live():
                    hold(act, q["log_done"], b.t + 1)
                    act.activation(logits[:, bass.ts(b.t, T), :], p_log[:], ACT.Copy).then_inc(q["log_ready"], 1)
            run_steps(act, body, 1)
            act.wait_ge(q["chain"], 2)
            act.activation(work2[:], work[:], ACT.Exp).then_inc(q["ex_ready"], 1)
            act.wait_ge(q["chain"], 9)
            act.activation(e2[:], f1[:], ACT.Exp).then_inc(q["ex_ready"], 1)
            act.wait_ge(q["w_loaded"], 16 * 5)
            act.wait_ge(q["w_hi"], 4)
            for src, dst in weights:
                act.activation(dst.hi, src, ACT.Copy).then_inc(q["w_hi"], 1)

            def invert(s):
                if s.live():
                    need(act, q["inv_done"], s.t - 1)
                    hold(act, q["hot_ready"], TOPK * (s.t + 1))
                    for m, (j, k) in enumerate(MEMBERS):
                        act.activation(A[:, s.p, 0, m], slot_hot[:, s.p, m], ACT.Copy, scale=tile_k[:, k, bass.ds(s.t * T + j, 1)]).then_inc(q["A_hi_ready"], 1)
            run_steps(act, invert, 0)

        @block.vector
        def _(dve):
            def body(s):
                a = s.back(1)
                if s.live():
                    layer_norm_stats(dve, X, s, stats, mv, q["stats_done"], q["mv_done"])
                if a.live():
                    need(dve, q["xT_done"], a.t - 1)
                    need(dve, written[a.p], 16 * a.u)
                    layer_norm_apply(dve, X, a, xn[:, a.p], mv, rstd, q["rstd_done"], q["xn_ready"])
            run_steps(dve, body, 1)

            n = [0]

            def then(ins):
                n[0] += 1
                ins.then_inc(q["chain"], 1)
                dve.wait_ge(q["chain"], n[0])

            def wide(v):
                return v.rearrange("p (t a) -> p t a", a=1).broadcast_to(full)
            revw = rev[:].rearrange("p (a e) -> p a e", a=1).broadcast_to(full)

            def first_best(value, best, hot):
                then(dve.tensor_tensor(hot[:], value, wide(best), ALU.is_equal))
                then(dve.tensor_tensor(hot[:], hot[:], revw, ALU.mult))
                then(dve.tensor_reduce(gsum[:], hot[:], AX.X, ALU.max))
                then(dve.tensor_tensor(hot[:], hot[:], wide(gsum[:]), ALU.is_equal))

            dve.wait_ge(q["consts"], 16 * 6 + 4)
            dve.wait_ge(q["log_ready"], STEPS)
            then(dve.tensor_reduce(m1[:], logits[:], AX.X, ALU.max))
            then(dve.tensor_tensor(work[:], logits[:], wide(m1[:]), ALU.subtract))
            first_best(logits[:], m1[:], hot1)
            then(dve.scalar_tensor_tensor(out=both[:], in0=hot1[:], scalar=-3.0e38, in1=logits[:], op0=ALU.mult, op1=ALU.add))
            then(dve.tensor_reduce(m2[:], both[:], AX.X, ALU.max))
            then(dve.tensor_tensor(f1[:], m2[:], m1[:], ALU.subtract))
            first_best(both[:], m2[:], hot2)
            then(dve.tensor_tensor(both[:], hot1[:], hot2[:], ALU.add))
            dve.wait_ge(q["ex_ready"], 2)
            then(dve.tensor_reduce(z[:], work2[:], AX.X, ALU.add))
            then(dve.reciprocal(rz[:], z[:]))
            then(dve.tensor_tensor(p2[:], e2[:], rz[:], ALU.mult))
            then(dve.scalar_tensor_tensor(out=den[:], in0=p2[:], scalar=1e-9, in1=rz[:], op0=ALU.add, op1=ALU.add))
            then(dve.reciprocal(gsum[:], den[:]))
            then(dve.tensor_tensor(gate[:, 0, :], rz[:], gsum[:], ALU.mult))
            then(dve.tensor_tensor(gate[:, 1, :], p2[:], gsum[:], ALU.mult))
            dve.wait_ge(q["ranked"], 2)
            then(dve.tensor_copy(total[:], p_total[:].rearrange("p t e -> p e t")))
            for e in range(EX):
                then(dve.tensor_tensor_scan(out=upto[:, e, :], data0=ones[:, 0:NT], data1=total[:, e, :], initial=0.0, op0=ALU.mult, op1=ALU.add))
            then(dve.tensor_scalar(padded[:], upto[:, :, NT - 1], float(P - 1), None, ALU.add))
            then(dve.tensor_copy(padded_i[:], padded[:]))
            then(dve.tensor_scalar(padded_i[:], padded_i[:], 7, 7, ALU.arith_shift_right, ALU.logical_shift_left))
            then(dve.tensor_copy(padded[:], padded_i[:]))
            then(dve.tensor_tensor_scan(out=ends[:], data0=ones[:, 0:EX], data1=padded[:], initial=0.0, op0=ALU.mult, op1=ALU.add))
            then(dve.tensor_tensor(padded[:], ends[:], padded[:], ALU.subtract))
            then(dve.tensor_tensor(upto[:], upto[:], total[:], ALU.subtract))
            first = padded[:].rearrange("p (e a) -> p e a", a=1).broadcast_to([P, EX, NT])
            then(dve.tensor_tensor(upto[:], upto[:], first, ALU.add))
            then(dve.tensor_tensor(pos[:], p_rank[:], upto[:].rearrange("p e t -> p t e"), ALU.add))
            for k, chosen in enumerate((hot1, hot2)):
                then(dve.tensor_tensor(work[:], chosen[:], pos[:], ALU.mult))
                then(dve.tensor_reduce(dest[:, k, :], work[:], AX.X, ALU.add))
            then(dve.tensor_copy(dest_i[:], dest[:]))
            then(dve.tensor_scalar(tile_i[:], dest_i[:], 7, None, ALU.arith_shift_right))
            then(dve.tensor_copy(dest_tile[:], tile_i[:]))
            then(dve.scalar_tensor_tensor(out=dest_row[:], in0=dest_tile[:], scalar=-float(P), in1=dest[:], op0=ALU.mult, op1=ALU.add))
            then(dve.tensor_scalar(row_f[:], slot_iota[:], float(P), None, ALU.mult))
            then(dve.tensor_scalar(exp_f[:], row_f[:], ends[:, 0:1], None, ALU.is_ge))
            for e in range(1, EX - 1):
                then(dve.scalar_tensor_tensor(out=exp_f[:], in0=row_f[:], scalar=ends[:, e:e + 1], in1=exp_f[:], op0=ALU.is_ge, op1=ALU.add))
            quad = exp_f[:].rearrange("p (u j) -> p u j", j=QUAD)
            for j in reversed(range(QUAD - 1)):
                then(dve.scalar_tensor_tensor(out=quad[:, :, j], in0=quad[:, :, j + 1], scalar=float(EX), in1=quad[:, :, j], op0=ALU.mult, op1=ALU.add))
            then(dve.tensor_copy(tile_expert[:], quad[:, :, 0]))
            then(dve.tensor_copy(slot_bf[:], slot_iota[:]))
            then(dve.tensor_copy(tile_bf[:], dest_tile[:]))
            then(dve.tensor_copy(destrow_bf[:], dest_row[:]))
            then(dve.tensor_scalar(tile_k[:, 1, :], tile_k[:, 0, :], float(NT), None, ALU.add))

            def along(v, n):
                return v[:].rearrange("p (a n) -> p a n", a=1).broadcast_to([P, T, n])

            def across(v, k, s, n):
                return v[:, k, bass.ts(s.t, T)].rearrange("p (t a) -> p t a", a=1).broadcast_to([P, T, n])

            def invert(s):
                if s.live():
                    hold(dve, q["A_hi_ready"], MEM * (s.t - 1))
                    for k in range(TOPK):
                        dve.tensor_tensor(slot_hot[:, s.p, k * T:(k + 1) * T], along(slot_bf, SLOTS), across(tile_bf, k, s, SLOTS), ALU.is_equal).then_inc(q["hot_ready"], 1)
                    need(dve, q["inv_done"], s.t - 1)
                    need(dve, q["hot_ready"], TOPK * (s.t + 1))
                    dve.tensor_scalar(A[:, s.p, 1], slot_hot[:, s.p], part_no[:, 0:1], None, ALU.mult).then_inc(q["A_lo_ready"], 1)
                    for k in range(TOPK):
                        dve.tensor_tensor(B[:, s.p, k * T:(k + 1) * T], along(row_bf, P), across(destrow_bf, k, s, P), ALU.is_equal).then_inc(q["B_ready"], 1)
            run_steps(dve, invert, 0)
            dve.wait_ge(q["inv_done"], STEPS)
            then(dve.tensor_copy(hi_no[:], p_inv[:, 0, :]))
            then(dve.tensor_copy(lo_no[:], p_inv[:, 1, :]))
            then(dve.tensor_scalar(row_f[:], hi_no[:], float(P), -float(P), ALU.mult, ALU.add))
            then(dve.tensor_tensor(row_f[:], row_f[:], lo_no[:], ALU.add))
            then(dve.tensor_scalar(off_f[:], hi_no[:], 0.0, float(NO_ROW), ALU.is_equal, ALU.mult))
            then(dve.tensor_tensor(off_f[:], off_f[:], row_f[:], ALU.add))
            then(dve.tensor_copy(scatter_rows[:], off_f[:]))
            then(dve.tensor_scalar(off_f[:], row_f[:], float(NT * P), -float(NT * P), ALU.is_ge, ALU.mult))
            then(dve.tensor_tensor(off_f[:], off_f[:], row_f[:], ALU.add))
            then(dve.tensor_scalar(off_f[:], off_f[:], 0.0, None, ALU.max))
            then(dve.tensor_copy(gather_rows[:], off_f[:]))

        @block.tensor
        def _(pe):
            pe.wait_ge(q["consts"], 16 * 6 + 3)

            def body(s):
                b = s.back(1)
                if s.live():
                    need(pe, q["xT_ready"], s.t)
                    need(pe, q["xn_ready"], T * (s.t + 1))
                    for j in range(T):
                        last = pe.transpose(p_xT[:, j * P:(j + 1) * P], xn[:, s.p, j, :], eye[:])
                    last.then_inc(q["xT_done"], 1)
                if b.live():
                    need(pe, q["log_ready"], b.t)
                    need(pe, q["xT_ready"], b.t + 1)
                    for j in range(T):
                        last = pe.matmul(p_log[:, j, :], xT[:, b.p, j * P:(j + 1) * P], router[:], start=True, stop=True)
                    last.then_inc(q["log_done"], 1)
            run_steps(pe, body, 1)
            pe.wait_ge(q["chain"], 14)
            chosen = both[:].rearrange("p t e -> p (t e)")
            pe.matmul(p_rank[:].rearrange("p t e -> p (t e)"), before[:], chosen, start=True, stop=True).then_inc(q["ranked"], 1)
            pe.matmul(p_total[:].rearrange("p t e -> p (t e)"), ones[:], chosen, start=True, stop=True).then_inc(q["ranked"], 1)

            def invert(s):
                if s.live():
                    need(pe, q["B_ready"], TOPK * (s.t + 1))
                    need(pe, q["A_hi_ready"], MEM * (s.t + 1))
                    need(pe, q["A_lo_ready"], s.t + 1)
                    for m in range(MEM):
                        first = isinstance(s.t, int) and s.t == 0 and m == 0
                        last = pe.matmul(p_inv[:].rearrange("p a b -> p (a b)"), B[:, s.p, m], A[:, s.p, :, m], start=first, stop=False, skip_group_check=True)
                    last.then_inc(q["inv_done"], 1)
            run_steps(pe, invert, 0)


def expert_phase(nc, gather_rows, scatter_rows, tile_expert, experts, xn_dram, y_dram, eye):
    MOD = QUAD
    GATHER, TURN, UP, TURN_G, DOWN, SCATTER = 1, 4, 5, 7, 8, 9
    with ExitStack() as ctx:
        ph = Phase(nc, ctx, "e_")
        sb, pair, sem = ph.sb, ph.pair, ph.sem
        w1, w3, w2 = experts
        rows_in = sb("rows_in", [P, MOD, 1], I32)
        rows_out = sb("rows_out", [P, MOD, 1], I32)
        xg = sb("xg", [P, MOD, P])
        xT = pair("xT", [P, 2, P])
        sl = sb("sl", [P, MOD, HP])
        g = sb("g", [P, MOD, HP])
        gT = pair("gT", [P, 2, len(CH), P])
        y = sb("y", [P, MOD, P])
        y_lo = sb("y_lo", [P, P])
        p_x = ph.psum("p_x", [P, S])
        p_h1, p_h3 = ([ph.psum(f"p_{n}{k}", [P, S]) for k in range(2)] for n in ("h1", "h3"))
        p_g = ph.psum("p_g", [P, len(CH), P])
        p_y = ph.psum("p_y", [P, S])
        names = ("p_g_clear in_ready out_ready x_done x_hi x_split h1_done h3_done sl_ready g_ready gT_done gT_hi "
                 "gT_split y_done y_lo_ready y_ready")
        q = {s: sem(s) for s in names.split()}
        gathered = [sem(f"gathered{p}") for p in range(MOD)]
        scattered = [sem(f"scattered{p}") for p in range(MOD)]
        block = ctx.enter_context(nc.Block())

        @block.gpsimd
        def _(pool):
            def body(s):
                i, o = s.back(GATHER), s.back(SCATTER)
                if i.live():
                    need(pool, q["in_ready"], i.t + 1)
                    hold(pool, q["x_done"], i.t - 3)
                    pool.indirect_dma_start(xg[:, i.p], None, xn_dram, bass.IndirectOffsetOnAxis(ap=rows_in[:, i.p], axis=0)).then_inc(gathered[i.p], 16)
                if o.live():
                    need(pool, q["out_ready"], o.t + 1)
                    hold(pool, q["y_ready"], o.t + 1)
                    pool.indirect_dma_start(y_dram, bass.IndirectOffsetOnAxis(ap=rows_out[:, o.p], axis=0), y[:, o.p], None,
                                            bounds_check=TOPK * NT * P - 1, oob_is_err=False).then_inc(scattered[o.p], 16)
            run_steps(pool, body, SCATTER, SLOTS, MOD)
            for p in range(MOD):
                pool.wait_ge(scattered[p], 16 * SLOTS // MOD)

        @block.scalar
        def _(act):
            act.preload_act_table(ACT.Silu)

            def body(s):
                a, b, c, d = s.back(TURN), s.back(UP), s.back(TURN_G), s.back(DOWN)
                if a.live():
                    need(act, q["h3_done"], a.t - 1)
                    need(act, q["x_done"], a.t + 1)
                    act.activation(xT.hi[:, a.p % 2], p_x[:, 0:P], ACT.Copy).then_inc(q["x_hi"], 1)
                if c.live():
                    need(act, q["y_done"], c.t - 1)
                    need(act, q["gT_done"], c.t + 1)
                    act.activation(gT.hi[:, c.p % 2], p_g[:], ACT.Copy).then_inc(q["gT_hi"], 1)
                if b.live():
                    need(act, q["g_ready"], b.t - 3)
                    need(act, q["h1_done"], b.t + 1)
                    act.activation(sl[:, b.p], p_h1[b.p % 2][:, 0:HP], ACT.Silu).then_inc(q["sl_ready"], 1)
                if d.live():
                    need(act, q["y_ready"], d.t)
                    need(act, q["y_done"], d.t + 1)
                    act.activation(y_lo[:], p_y[:, P:2 * P], ACT.Copy).then_inc(q["y_lo_ready"], 1)
            run_steps(act, body, DOWN, SLOTS, MOD)

        @block.vector
        def _(dve):
            dve.memset(p_g[:], 0.0).then_inc(q["p_g_clear"], 1)

            def body(s):
                a, b, c, d = s.back(TURN), s.back(UP), s.back(TURN_G), s.back(DOWN)
                if s.live():
                    need(dve, gathered[s.p], 16 * s.u)
                    dve.tensor_copy(rows_in[:, s.p], gather_rows[:, bass.ds(s.t, 1)]).then_inc(q["in_ready"], 1)
                if a.live():
                    need(dve, q["h3_done"], a.t - 1)
                    need(dve, q["x_hi"], a.t + 1)
                    dve.tensor_tensor(xT.lo[:, a.p % 2], p_x[:, 0:P], xT.hi[:, a.p % 2].bitcast(F32), ALU.subtract).then_inc(q["x_split"], 1)
                if c.live():
                    need(dve, q["y_done"], c.t - 1)
                    need(dve, q["gT_hi"], c.t + 1)
                    dve.tensor_tensor(gT.lo[:, c.p % 2], p_g[:], gT.hi[:, c.p % 2].bitcast(F32), ALU.subtract).then_inc(q["gT_split"], 1)
                if b.live():
                    need(dve, q["gT_done"], b.t - 3)
                    need(dve, q["h3_done"], b.t + 1)
                    need(dve, q["sl_ready"], b.t + 1)
                    dve.tensor_tensor(g[:, b.p], sl[:, b.p], p_h3[b.p % 2][:, 0:HP], ALU.mult).then_inc(q["g_ready"], 1)
                if d.live():
                    need(dve, scattered[d.p], 16 * d.u)
                    dve.tensor_copy(rows_out[:, d.p], scatter_rows[:, bass.ds(d.t, 1)]).then_inc(q["out_ready"], 1)
                    need(dve, q["y_lo_ready"], d.t + 1)
                    dve.tensor_tensor(y[:, d.p], p_y[:, 0:P], y_lo[:], ALU.add).then_inc(q["y_ready"], 1)
            run_steps(dve, body, DOWN, SLOTS, MOD)

        @block.tensor
        def _(pe):
            pe.wait_ge(q["p_g_clear"], 1)
            up_word, down_word = pe.alloc_register("up_word"), pe.alloc_register("down_word")

            def expert_of(word, p):
                return pe.snap((pe.snap(word) // EX ** p) % EX, min_val=0, max_val=EX - 1)

            def body(s):
                a, b, c, d = s.back(TURN), s.back(UP), s.back(TURN_G), s.back(DOWN)
                if a.live():
                    need(pe, q["x_split"], a.t)
                    need(pe, gathered[a.p], 16 * (a.u + 1))
                    pe.transpose(p_x[:, 0:P], xg[:, a.p], eye[:]).then_inc(q["x_done"], 1)
                if c.live():
                    need(pe, q["gT_split"], c.t)
                    need(pe, q["g_ready"], c.t + 1)
                    for k, (h0, r) in enumerate(CH):
                        last = pe.transpose(p_g[0:r, k, :], g[:, c.p, h0:h0 + r], eye[:])
                    last.then_inc(q["gT_done"], 1)
                if b.live():
                    need(pe, q["g_ready"], b.t - 1)
                    hold(pe, q["x_split"], b.t + 1)
                    if b.p == 0:
                        pe.reg_load(up_word, tile_expert[0:1, bass.ds(b.u, 1)])
                    e = expert_of(up_word, b.p)
                    for bank, wk, done in ((p_h1, w1, "h1_done"), (p_h3, w3, "h3_done")):
                        rhs = Pair(wk.hi[:].rearrange("p e h -> p (e h)"), wk.lo[:].rearrange("p e h -> p (e h)"))[:, bass.ts(e, HP)]
                        product(pe, bank[b.p % 2][:, 0:HP], xT[:, b.p % 2], rhs, True, True).then_inc(q[done], 1)
                if d.live():
                    need(pe, q["y_ready"], d.t)
                    hold(pe, q["gT_split"], d.t + 1)
                    if d.p == 0:
                        pe.reg_mov(down_word, up_word)
                    e = expert_of(down_word, d.p)
                    for k, (_, r) in enumerate(CH):
                        w2k = w2[0:r, k].rearrange("p e h d -> p (e h d)")
                        if k == len(CH) - 1:
                            pe.matmul(p_y[:, 0:P], gT.lo[0:r, d.p % 2, k], w2k[:, bass.ds(e * 2 * P, P)], start=False, stop=False)
                        last = pe.matmul(p_y[:, 0:2 * P], gT.hi[0:r, d.p % 2, k], w2k[:, bass.ts(e, 2 * P)], start=k == 0, stop=k == len(CH) - 1)
                        if k < len(CH) - 1:
                            pe.matmul(p_y[:, 0:P], gT.lo[0:r, d.p % 2, k], w2k[:, bass.ds(e * 2 * P, P)], start=False, stop=False)
                    last.then_inc(q["y_done"], 1)
            run_steps(pe, body, DOWN, SLOTS, MOD)


def combine_phase(nc, X, gate, y_dram, out_dram):
    MOD = 4
    with ExitStack() as ctx:
        ph = Phase(nc, ctx, "o_")
        sb, sem = ph.sb, ph.sem
        y = sb("y", [P, MOD, TOPK, T, P])
        y_in = [sem(f"y_in{p}") for p in range(MOD)]
        written = [sem(f"written{p}") for p in range(MOD)]
        scaled, added, summed = sem("scaled"), sem("added"), sem("summed")
        block = ctx.enter_context(nc.Block())

        @block.sync
        def _(sp):
            def body(s):
                if s.live():
                    hold(sp, summed, T * (s.t - MOD + 1))
                    for k in range(TOPK):
                        sp.dma_start(y[:, s.p, k], y_dram[bass.ds(k * NT * P + s.t * S, S)].rearrange("(t p) d -> p t d", p=P)).then_inc(y_in[s.p], 16)
            run_steps(sp, body, MOD - 1, mod=MOD)

        @block.scalar
        def _(act):
            def body(s):
                o = s.back(2)
                if s.live():
                    hold(act, y_in[s.p], 32 * (s.u + 1))
                    for j in range(T):
                        act.activation(y[:, s.p, 0, j], y[:, s.p, 0, j], ACT.Copy, scale=gate[:, 0, bass.ds(s.t * T + j, 1)]).then_inc(scaled, 1)
                if o.live():
                    hold(act, summed, T * (o.t + 1))
                    act.dma_start(out_dram[bass.ts(o.t, T)].rearrange("t p d -> p t d"), X[:, bass.ts(o.t, T), :]).then_inc(written[o.p], 16)
            run_steps(act, body, 3, mod=MOD)
            for p in range(MOD):
                act.wait_ge(written[p], 16 * STEPS // MOD)

        @block.gpsimd
        def _(pool):
            def body(s):
                if s.live():
                    need(pool, scaled, T * (s.t + 1))
                    pool.tensor_tensor(X[:, bass.ts(s.t, T), :], X[:, bass.ts(s.t, T), :], y[:, s.p, 0], ALU.add).then_inc(added, 1)
            run_steps(pool, body, 0, mod=MOD)

        @block.vector
        def _(dve):
            def body(s):
                if s.live():
                    need(dve, y_in[s.p], 32 * (s.u + 1))
                    need(dve, added, s.t + 1)
                    for j in range(T):
                        xt = X[:, s.t * T + j, :]
                        dve.scalar_tensor_tensor(out=xt, in0=y[:, s.p, 1, j], scalar=gate[:, 1, bass.ds(s.t * T + j, 1)], in1=xt,
                                                 op0=ALU.mult, op1=ALU.add).then_inc(summed, 1)
            run_steps(dve, body, 0, mod=MOD)


def build(nc, ins, out_dram, scratch):
    with ExitStack() as ctx:
        X = ctx.enter_context(nc.sbuf_tensor("x_tokens", [P, NT, P], F32))
        eye = ctx.enter_context(nc.sbuf_tensor("eye", [P, P], F32))
        eye_in = ctx.enter_context(nc.semaphore("eye_in"))
        x_dram = ins["x"].rearrange("b (t p) d -> (b t) p d", p=P)
        with nc.Block() as block:
            @block.sync
            def _(sp):
                sp.dma_start(eye[:], ins["eye"]).then_inc(eye_in, 16)
                sp.wait_ge(eye_in, 16)
        gnn_phase(nc, x_dram, ins["adjT"], ins, X, eye)
        with ExitStack() as table_ctx:
            XT = table_ctx.enter_context(nc.sbuf_tensor("xT_all", [P, NT * P], F32))
            table = table_ctx.enter_context(nc.sbuf_tensor("table", [P, NT, 3, HEADS], F32))
            weights = mamba_weights(nc, table_ctx, ins)
            dt_phase(nc, ins, X, XT, table, weights, scratch["cum"], eye)
            mamba_phase(nc, weights, X, XT, table, scratch["cum"], eye)
        graph_phase(nc, ins, X, ins["adjT"], eye)
        gate = ctx.enter_context(nc.sbuf_tensor("gate", [P, TOPK, NT], F32))
        gather_rows = ctx.enter_context(nc.sbuf_tensor("gather_rows", [P, SLOTS], I32))
        scatter_rows = ctx.enter_context(nc.sbuf_tensor("scatter_rows", [P, SLOTS], I32))
        tile_expert = ctx.enter_context(nc.sbuf_tensor("tile_expert", [P, SLOTS // QUAD], I32))
        xn_tiles = scratch["xn"].rearrange("(t p) d -> t p d", p=P)
        with ExitStack() as experts_ctx:
            experts = expert_weights(nc, experts_ctx)
            route_phase(nc, ins, X, gate, gather_rows, scatter_rows, tile_expert, experts, xn_tiles, eye)
            expert_phase(nc, gather_rows, scatter_rows, tile_expert, experts, scratch["xn"], scratch["y"], eye)
        combine_phase(nc, X, gate, scratch["y"], out_dram.rearrange("b (t p) d -> (b t) p d", p=P))


def kernel(x, adj, L0_gnn_w_se, L0_gnn_b_se, L0_gnn_conv1_w, L0_gnn_bn1_g, L0_gnn_bn1_b, L0_gnn_bn1_m, L0_gnn_bn1_v,
           L0_gnn_conv2_w, L0_gnn_bn2_g, L0_gnn_bn2_b, L0_gnn_bn2_m, L0_gnn_bn2_v, L0_gnn_w_msg, L0_gnn_b_msg,
           L0_gnn_w_ih, L0_gnn_b_ih, L0_gnn_w_hh, L0_gnn_b_hh, L0_ffn_W_in, L0_ffn_conv_w, L0_ffn_conv_b,
           L0_ffn_dt_bias, L0_ffn_A_log, L0_ffn_D, L0_ffn_norm_w, L0_ffn_W_out, L0_ffn_W_lin, L0_ffn_b_lin,
           L1_gnn_weight, L1_gnn_bias, L1_ffn_router_w, L1_ffn_w1, L1_ffn_w2, L1_ffn_w3):
    import numpy as np
    import concourse.bacc as bacc
    from concourse.bass_utils import run_bass_kernel_spmd

    def lay(a, *order):
        a = np.asarray(a)
        return np.ascontiguousarray(a.transpose(*order) if order else a)

    lr_const = np.zeros((64, 3), np.float32)
    for rows, col in ((slice(0, 3), (0, 0, 2)), (slice(3, 6), (0, -1, 0)), (slice(6, 9), (1, 0, -1)),
                      (slice(32, 35), (0, 0, 1)), (slice(35, 38), (1, 0, 1)), (slice(38, 41), (0, 1, 0))):
        lr_const[rows] = col
    arrays = {
        "x": lay(x), "adjT": lay(adj, 0, 2, 1), "eye": np.eye(P, dtype=np.float32), "lr_const": lr_const,
        "w_seT": lay(L0_gnn_w_se, 1, 0), "b_se": lay(L0_gnn_b_se),
        "conv1T": lay(np.asarray(L0_gnn_conv1_w)[:, :, 0], 1, 0),
        "conv2T": lay(L0_gnn_conv2_w, 1, 2, 0).reshape(P, -1),
        "gnn_vecs": np.stack([np.asarray(a).reshape(-1, P)[k] for a in (
            L0_gnn_bn1_g, L0_gnn_bn1_b, L0_gnn_bn1_m, L0_gnn_bn1_v, L0_gnn_bn2_g, L0_gnn_bn2_b, L0_gnn_bn2_m,
            L0_gnn_bn2_v, L0_gnn_b_ih, L0_gnn_b_hh) for k in range(np.asarray(a).size // P)], axis=1),
        "w_msgT": lay(L0_gnn_w_msg, 1, 0), "b_msg": lay(L0_gnn_b_msg),
        "w_ihT": lay(np.asarray(L0_gnn_w_ih).reshape(3 * P, 2, P), 2, 1, 0).reshape(P, -1),
        "w_hhT": lay(L0_gnn_w_hh, 1, 0),
        "w1T": lay(L1_ffn_w1, 2, 0, 1).reshape(P, -1), "w3T": lay(L1_ffn_w3, 2, 0, 1).reshape(P, -1),
        "w2T": lay(L1_ffn_w2, 2, 0, 1).reshape(H, -1), "routerT": lay(L1_ffn_router_w, 1, 0),
        "rev8": np.arange(EX, 0, -1, dtype=np.float32), "before": np.triu(np.ones((P, P), np.float32), 1),
        "tile_no": np.arange(1, NT + 1, dtype=np.float32), "part_no": np.arange(P, dtype=np.float32),
        "slot_iota": np.arange(SLOTS, dtype=np.float32),
        "gcn_w": lay(L1_gnn_weight), "gcn_b": lay(L1_gnn_bias),
        "W_in_zx": lay(np.asarray(L0_ffn_W_in)[:, :DI + XBC]), "W_dt": lay(np.asarray(L0_ffn_W_in)[:, DI + XBC:]),
        "dt_bias": lay(L0_ffn_dt_bias), "A_log": lay(L0_ffn_A_log), "D": lay(L0_ffn_D), "b_lin": lay(L0_ffn_b_lin),
        "W_outT": lay(L0_ffn_W_out, 1, 0), "W_lin": lay(L0_ffn_W_lin),
        "mamba_vecs": np.concatenate([np.asarray(L0_ffn_conv_w).reshape(3, P, TAPS).transpose(1, 0, 2).reshape(P, -1),
                                      np.asarray(L0_ffn_conv_b).reshape(3, P).T, np.asarray(L0_ffn_norm_w).reshape(2, P).T], axis=1),
        "mask": np.concatenate([np.triu(np.ones((P, P), np.float32)), np.ones((P, P), np.float32), np.triu(np.ones((P, P), np.float32))], axis=1),
    }
    nc = bacc.Bacc("TRN2", target_bir_lowering=False, num_devices=1)
    ins = {name: nc.dram_tensor(f"in_{name}", a.shape, F32, kind="ExternalInput").ap() for name, a in arrays.items()}
    out = nc.dram_tensor("out", (BS, N, P), F32, kind="ExternalOutput").ap()
    scratch = {"cum": nc.dram_tensor("cum_scratch", (HEADS, BS * N), F32, kind="Internal").ap(),
               "xn": nc.dram_tensor("xn_scratch", (NT * P, P), F32, kind="Internal").ap(),
               "y": nc.dram_tensor("y_scratch", (TOPK * NT * P, P), F32, kind="Internal").ap()}
    build(nc, ins, out, scratch)
    result = run_bass_kernel_spmd(nc, [{f"in_{name}": a for name, a in arrays.items()}], core_ids=[0])
    return result.results[0]["out"]
```
